# Optimizing a Trainium2 kernel written in Bass

```python
import numpy as np
import jax
import jax.numpy as jnp

def _softmax(x, axis=-1):
    return jax.nn.softmax(x, axis=axis)

def _gelu(x):
    return jax.nn.gelu(x, approximate=True)

def _silu(x):
    return jax.nn.silu(x)

def _sigmoid(x):
    return jax.nn.sigmoid(x)

def _layernorm(x, axis=-1, eps=1e-05):
    m = jnp.mean(x, axis=axis, keepdims=True)
    v = jnp.var(x, axis=axis, keepdims=True)
    return (x - m) / jnp.sqrt(v + eps)

def _scatter_add(tgt, idx, src, axis=0):
    return tgt.at[idx].add(src)

def _segment_sum(src, seg, n):
    return jax.ops.segment_sum(src, seg, n)
kernel_name = 'mk_recurrent_d4_jaxref_r8_c0a422'

def setup_inputs(seed: int=0):
    np.random.seed(seed)
    _w = jnp.asarray

    def _L0_attn_setup():
        import jax, jax.numpy as jnp
        import numpy as np
        HIDDEN = 128
        D_MEM = 32
        BATCH = 4
        SEQ = 128
        EPS = 1e-06

        def elu_plus_one(x):
            return jnp.where(x > 0, x + 1.0, jnp.exp(x))

        def _retrieve(sigma_x, memory, memory_norm):
            a_unnorm = jnp.matmul(sigma_x, memory)
            norm = jnp.clip(jnp.matmul(sigma_x, memory_norm), EPS, None)[..., None]
            out = a_unnorm / norm
            return jnp.where(memory_norm.sum() < EPS, jnp.zeros_like(out), out)

        def _reference_tuple_inner(hidden_states, w_q, w_k, w_v, w_o, gate, memory, memory_norm):
            b, s, _ = hidden_states.shape
            q = jnp.einsum('bsh,dh->bsd', hidden_states, w_q)
            k = jnp.einsum('bsh,dh->bsd', hidden_states, w_k)
            v = jnp.einsum('bsh,dh->bsd', hidden_states, w_v)
            sigma_q = elu_plus_one(q)
            sigma_k = elu_plus_one(k)
            memory_output = _retrieve(sigma_q, memory, memory_norm)
            kv = jnp.einsum('bsd,bse->bsde', sigma_k, v)
            kv_cumsum = jnp.cumsum(kv, axis=1)
            k_cumsum = jnp.cumsum(sigma_k, axis=1)
            numerator = jnp.einsum('bsd,bsde->bse', sigma_q, kv_cumsum)
            denominator = jnp.clip(jnp.einsum('bsd,bsd->bs', sigma_q, k_cumsum), EPS, None)[..., None]
            local_output = numerator / denominator
            g = jax.nn.sigmoid(gate[0])
            combined = g * memory_output + (1.0 - g) * local_output
            output = jnp.einsum('bsd,hd->bsh', combined, w_o)
            retrieved_unnorm = jnp.matmul(sigma_k, memory)
            norm = jnp.clip(jnp.matmul(sigma_k, memory_norm), EPS, None)[..., None]
            delta_v = v - retrieved_unnorm / norm
            memory_update = jnp.einsum('bsd,bse->de', sigma_k, delta_v) / (b * s)
            new_memory = jax.lax.stop_gradient(memory + memory_update)
            z_update = sigma_k.sum(axis=(0, 1)) / b
            new_memory_norm = jax.lax.stop_gradient(memory_norm + z_update)
            return (output, new_memory, new_memory_norm)
        key = jax.random.key(seed)
        ks = jax.random.split(key, 8)
        hidden_states = jax.random.normal(ks[0], (BATCH, SEQ, HIDDEN), dtype=jnp.float32)
        s = 1.0 / np.sqrt(HIDDEN)
        w_q = jax.random.normal(ks[1], (D_MEM, HIDDEN), dtype=jnp.float32) * s
        w_k = jax.random.normal(ks[2], (D_MEM, HIDDEN), dtype=jnp.float32) * s
        w_v = jax.random.normal(ks[3], (D_MEM, HIDDEN), dtype=jnp.float32) * s
        w_o = jax.random.normal(ks[4], (HIDDEN, D_MEM), dtype=jnp.float32) * (1.0 / np.sqrt(D_MEM))
        gate = jnp.zeros((1,), dtype=jnp.float32)
        memory = jax.random.normal(ks[5], (D_MEM, D_MEM), dtype=jnp.float32) * 0.1
        memory_norm = jax.random.uniform(ks[6], (D_MEM,), dtype=jnp.float32) * 10.0 + 1.0
        return {'hidden_states': hidden_states, 'w_q': w_q, 'w_k': w_k, 'w_v': w_v, 'w_o': w_o, 'gate': gate, 'memory': memory, 'memory_norm': memory_norm}
    _L0_attn_in = _L0_attn_setup()

    def _L0_ffn_setup():
        import jax, jax.numpy as jnp
        import numpy as np
        E = 8
        K = 2
        D = 128
        B, N = (4, 512)
        DC = 64
        key = jax.random.key(seed)
        ks = jax.random.split(key, 6)
        x = jax.random.normal(ks[0], (B, N, D), jnp.float32)
        cond = jax.random.normal(ks[1], (B, N, DC), jnp.float32)
        mask = jnp.ones((B, N), jnp.float32)
        W_shared = jax.random.normal(ks[2], (D, D), jnp.float32) * 0.02
        W_expert = jax.random.normal(ks[3], (D, D), jnp.float32) * 0.02
        W_gate = jax.random.normal(ks[4], (D, E - 1), jnp.float32) * 0.02
        bias = jnp.zeros((D,), jnp.float32)
        return dict(x=x, cond=cond, mask=mask, W_shared=W_shared, W_expert=W_expert, W_gate=W_gate, bias=bias)
    _L0_ffn_in = _L0_ffn_setup()

    def _L1_attn_setup():
        import jax, jax.numpy as jnp
        import numpy as np
        BATCH, SEQ, D_MODEL = (2, 512, 128)
        D_STATE, EXPAND = (64, 2)
        D_INNER = D_MODEL * EXPAND

        def _silu(v):
            return v * jax.nn.sigmoid(v)
        key = jax.random.key(seed)
        ks = jax.random.split(key, 12)
        s = 0.02
        return {'x': jax.random.normal(ks[0], (BATCH, SEQ, D_MODEL), dtype=jnp.float32), 'W_in': jax.random.normal(ks[1], (D_MODEL, 2 * D_INNER), dtype=jnp.float32) * s, 'b_in': jnp.zeros((2 * D_INNER,), dtype=jnp.float32), 'W_xp': jax.random.normal(ks[2], (D_INNER, D_STATE), dtype=jnp.float32) * s, 'b_xp': jnp.zeros((D_STATE,), dtype=jnp.float32), 'W_dt': jax.random.normal(ks[3], (D_INNER, D_MODEL), dtype=jnp.float32) * s, 'b_dt': jnp.zeros((D_MODEL,), dtype=jnp.float32), 'W_out': jax.random.normal(ks[4], (D_INNER, D_MODEL), dtype=jnp.float32) * s, 'b_out': jnp.zeros((D_MODEL,), dtype=jnp.float32), 'A_log': jax.random.normal(ks[5], (D_STATE,), dtype=jnp.float32), 'D': jax.random.normal(ks[6], (D_MODEL,), dtype=jnp.float32)}
    _L1_attn_in = _L1_attn_setup()

    def _L1_ffn_setup():
        import jax, jax.numpy as jnp
        import numpy as np
        D, H, O, E, TOPK = (128, 512, 128, 8, 2)
        B, S = (4, 128)
        key = jax.random.key(seed)
        ks = jax.random.split(key, 12)
        std = 0.02
        return {'hidden_states': jax.random.normal(ks[0], (B, S, D), dtype=jnp.float32), 'norm_weight': jnp.ones((D,), dtype=jnp.float32), 'router_w': jax.random.normal(ks[1], (E, D), dtype=jnp.float32) * std, 'sw1': jax.random.normal(ks[2], (D, H), dtype=jnp.float32) * (1.0 / np.sqrt(D)), 'sb1': jnp.zeros((H,), dtype=jnp.float32), 'sw2': jax.random.normal(ks[3], (H, O), dtype=jnp.float32) * (1.0 / np.sqrt(H)), 'sb2': jnp.zeros((O,), dtype=jnp.float32), 'ew1': jax.random.normal(ks[4], (E, D, H), dtype=jnp.float32) * (1.0 / np.sqrt(D)), 'eb1': jnp.zeros((E, H), dtype=jnp.float32), 'ew2': jax.random.normal(ks[5], (E, H, O), dtype=jnp.float32) * (1.0 / np.sqrt(H)), 'eb2': jnp.zeros((E, O), dtype=jnp.float32)}
    _L1_ffn_in = _L1_ffn_setup()

    def _L2_attn_setup():
        import jax, jax.numpy as jnp
        import numpy as np
        N, T, D = (2, 512, 128)
        H, E, L = (8, 4, 32)
        DK, DV = (64, 64)

        def _pscan(A, Xv, Y0):
            Ae = jnp.broadcast_to(A[..., None], Xv.shape)
            Xv = Xv.at[..., 0, :].add(A[..., 0, None] * Y0)

            def op(c1, c2):
                a1, x1 = c1
                a2, x2 = c2
                return (a1 * a2, a2 * x1 + x2)
            _, Y = jax.lax.associative_scan(op, (Ae, Xv), axis=3)
            return Y
        key = jax.random.key(seed)
        ks = jax.random.split(key, 8)

        def randw(k, *d):
            return jax.random.normal(k, d, dtype=jnp.float32) / np.float32(np.sqrt(d[-1]))
        return {'X': jax.random.normal(ks[0], (N, T, D), dtype=jnp.float32), 'w_G': randw(ks[1], H, E, D), 'b_G': jnp.full((H, E), -float(H) ** 0.5, dtype=jnp.float32), 'w_K': randw(ks[2], H, DK, D), 'w_V': randw(ks[3], H, DV, D), 'w_Q': randw(ks[4], H, DK, D), 'w_O': randw(ks[5], DV * H, D), 'init_K_rec': randw(ks[6], E, L, DK), 'init_V_rec': randw(ks[7], E, L, DV)}
    _L2_attn_in = _L2_attn_setup()

    def _L2_ffn_setup():
        import jax, jax.numpy as jnp
        import numpy as np
        DIM = 128

        def _reference_tuple_inner(x, W_r, W_k, W_v, mu_r, mu_k):
            B, T, C = x.shape
            x_prev = jnp.concatenate([jnp.zeros((B, 1, C), x.dtype), x[:, :-1, :]], axis=1)
            xr = mu_r * x + (1.0 - mu_r) * x_prev
            xk = mu_k * x + (1.0 - mu_k) * x_prev
            r = jax.nn.sigmoid(jnp.einsum('btc,dc->btd', xr, W_r))
            k = jnp.einsum('btc,dc->btd', xk, W_k)
            k_act = jnp.square(jax.nn.relu(k))
            out = r * jnp.einsum('btc,dc->btd', k_act, W_v)
            new_state = x[:, -1, :]
            return (out, new_state)
        key = jax.random.key(seed)
        ks = jax.random.split(key, 6)
        B, T, C = (8, 256, DIM)
        x = jax.random.normal(ks[0], (B, T, C), dtype=jnp.float32)
        s = 1.0 / np.sqrt(C)
        W_r = jax.random.uniform(ks[1], (C, C), jnp.float32, -s, s)
        W_k = jax.random.uniform(ks[2], (C, C), jnp.float32, -s, s)
        W_v = jax.random.uniform(ks[3], (C, C), jnp.float32, -s, s)
        mu_r = jax.random.uniform(ks[4], (C,), jnp.float32)
        mu_k = jax.random.uniform(ks[5], (C,), jnp.float32)
        return {'x': x, 'W_r': W_r, 'W_k': W_k, 'W_v': W_v, 'mu_r': mu_r, 'mu_k': mu_k}
    _L2_ffn_in = _L2_ffn_setup()

    def _L3_attn_setup():
        import jax, jax.numpy as jnp
        import numpy as np
        DIM_IN, DIM_OUT, DIM_INNER = (128, 128, 64)
        key = jax.random.key(seed)
        k1, k2, k3, k4 = jax.random.split(key, 4)
        x = jax.random.normal(k1, (4, 256, DIM_IN), dtype=jnp.float32)
        w_qkv = jax.random.uniform(k2, (DIM_INNER * 3, DIM_IN), dtype=jnp.float32, minval=-1.0, maxval=1.0) / np.sqrt(DIM_IN)
        w_out = jax.random.uniform(k3, (DIM_OUT, DIM_INNER), dtype=jnp.float32, minval=-1.0, maxval=1.0) / np.sqrt(DIM_INNER)
        b_out = jax.random.uniform(k4, (DIM_OUT,), dtype=jnp.float32, minval=-1.0, maxval=1.0) / np.sqrt(DIM_INNER)
        return {'x': x, 'w_qkv': w_qkv, 'w_out': w_out, 'b_out': b_out}
    _L3_attn_in = _L3_attn_setup()

    def _L3_ffn_setup():
        import jax, jax.numpy as jnp
        import numpy as np
        DIM = 128
        EXPERT_DIM = 64
        N_EXPERTS = 16
        TOPK = 2
        SHARED_HIDDEN = EXPERT_DIM * TOPK
        B, T = (4, 128)

        def _moe_forward(x, router_w, router_bias, up_proj, gate_proj, down_proj, sh_gate, sh_up, sh_down):
            Bb, Tt, D = x.shape
            flat = x.reshape(Bb * Tt, D)
            N = flat.shape[0]
            logits = flat @ router_w.T
            topk_scores, topk_idx = jax.lax.top_k(logits + router_bias, TOPK)
            topk_scores = jax.nn.softmax(topk_scores, axis=-1)
            combine = jnp.zeros((N, N_EXPERTS), flat.dtype)
            combine = combine.at[jnp.arange(N)[:, None], topk_idx].add(topk_scores)
            up_all = jnp.einsum('nd,kde->nke', flat, up_proj)
            gate_all = jnp.einsum('nd,kde->nke', flat, gate_proj)
            hidden = jax.nn.silu(gate_all) * up_all
            down_all = jnp.einsum('nke,ked->nkd', hidden, down_proj)
            out = jnp.einsum('nk,nkd->nd', combine, down_all)
            sh_hidden = jax.nn.silu(flat @ sh_gate.T) * (flat @ sh_up.T)
            out = out + sh_hidden @ sh_down.T
            return out.reshape(Bb, Tt, D)
        key = jax.random.key(seed)
        ks = jax.random.split(key, 9)
        std = 0.02
        return {'x': jax.random.normal(ks[0], (B, T, DIM), jnp.float32), 'router_w': jax.random.normal(ks[1], (N_EXPERTS, DIM), jnp.float32) * std, 'router_bias': jnp.zeros((N_EXPERTS,), jnp.float32), 'up_proj': jax.random.normal(ks[2], (N_EXPERTS, DIM, EXPERT_DIM), jnp.float32) * std, 'gate_proj': jax.random.normal(ks[3], (N_EXPERTS, DIM, EXPERT_DIM), jnp.float32) * std, 'down_proj': jax.random.normal(ks[4], (N_EXPERTS, EXPERT_DIM, DIM), jnp.float32) * std, 'sh_gate': jax.random.normal(ks[5], (SHARED_HIDDEN, DIM), jnp.float32) * std, 'sh_up': jax.random.normal(ks[6], (SHARED_HIDDEN, DIM), jnp.float32) * std, 'sh_down': jax.random.normal(ks[7], (DIM, SHARED_HIDDEN), jnp.float32) * std}
    _L3_ffn_in = _L3_ffn_setup()
    _d = {'L0_attn_hidden_states': _L0_attn_in['hidden_states'], 'L0_attn_w_q': _L0_attn_in['w_q'], 'L0_attn_w_k': _L0_attn_in['w_k'], 'L0_attn_w_v': _L0_attn_in['w_v'], 'L0_attn_w_o': _L0_attn_in['w_o'], 'L0_attn_gate': _L0_attn_in['gate'], 'L0_attn_memory': _L0_attn_in['memory'], 'L0_attn_memory_norm': _L0_attn_in['memory_norm'], 'L0_ffn_cond': _L0_ffn_in['cond'], 'L0_ffn_mask': _L0_ffn_in['mask'], 'L0_ffn_W_shared': _L0_ffn_in['W_shared'], 'L0_ffn_W_expert': _L0_ffn_in['W_expert'], 'L0_ffn_W_gate': _L0_ffn_in['W_gate'], 'L0_ffn_bias': _L0_ffn_in['bias'], 'L1_attn_W_in': _L1_attn_in['W_in'], 'L1_attn_b_in': _L1_attn_in['b_in'], 'L1_attn_W_xp': _L1_attn_in['W_xp'], 'L1_attn_b_xp': _L1_attn_in['b_xp'], 'L1_attn_W_dt': _L1_attn_in['W_dt'], 'L1_attn_b_dt': _L1_attn_in['b_dt'], 'L1_attn_W_out': _L1_attn_in['W_out'], 'L1_attn_b_out': _L1_attn_in['b_out'], 'L1_attn_A_log': _L1_attn_in['A_log'], 'L1_attn_D': _L1_attn_in['D'], 'L1_ffn_norm_weight': _L1_ffn_in['norm_weight'], 'L1_ffn_router_w': _L1_ffn_in['router_w'], 'L1_ffn_sw1': _L1_ffn_in['sw1'], 'L1_ffn_sb1': _L1_ffn_in['sb1'], 'L1_ffn_sw2': _L1_ffn_in['sw2'], 'L1_ffn_sb2': _L1_ffn_in['sb2'], 'L1_ffn_ew1': _L1_ffn_in['ew1'], 'L1_ffn_eb1': _L1_ffn_in['eb1'], 'L1_ffn_ew2': _L1_ffn_in['ew2'], 'L1_ffn_eb2': _L1_ffn_in['eb2'], 'L2_attn_w_G': _L2_attn_in['w_G'], 'L2_attn_b_G': _L2_attn_in['b_G'], 'L2_attn_w_K': _L2_attn_in['w_K'], 'L2_attn_w_V': _L2_attn_in['w_V'], 'L2_attn_w_Q': _L2_attn_in['w_Q'], 'L2_attn_w_O': _L2_attn_in['w_O'], 'L2_attn_init_K_rec': _L2_attn_in['init_K_rec'], 'L2_attn_init_V_rec': _L2_attn_in['init_V_rec'], 'L2_ffn_W_r': _L2_ffn_in['W_r'], 'L2_ffn_W_k': _L2_ffn_in['W_k'], 'L2_ffn_W_v': _L2_ffn_in['W_v'], 'L2_ffn_mu_r': _L2_ffn_in['mu_r'], 'L2_ffn_mu_k': _L2_ffn_in['mu_k'], 'L3_attn_w_qkv': _L3_attn_in['w_qkv'], 'L3_attn_w_out': _L3_attn_in['w_out'], 'L3_attn_b_out': _L3_attn_in['b_out'], 'L3_ffn_router_w': _L3_ffn_in['router_w'], 'L3_ffn_router_bias': _L3_ffn_in['router_bias'], 'L3_ffn_up_proj': _L3_ffn_in['up_proj'], 'L3_ffn_gate_proj': _L3_ffn_in['gate_proj'], 'L3_ffn_down_proj': _L3_ffn_in['down_proj'], 'L3_ffn_sh_gate': _L3_ffn_in['sh_gate'], 'L3_ffn_sh_up': _L3_ffn_in['sh_up'], 'L3_ffn_sh_down': _L3_ffn_in['sh_down']}
    _x0 = _d['L0_attn_hidden_states']
    _d['L0_attn_hidden_states'] = jax.random.normal(jax.random.fold_in(jax.random.key(seed), 1), (2, 1024, 128), dtype=_x0.dtype)
    del _x0
    return _d

def reference(L0_attn_hidden_states, L0_attn_w_q, L0_attn_w_k, L0_attn_w_v, L0_attn_w_o, L0_attn_gate, L0_attn_memory, L0_attn_memory_norm, L0_ffn_cond, L0_ffn_mask, L0_ffn_W_shared, L0_ffn_W_expert, L0_ffn_W_gate, L0_ffn_bias, L1_attn_W_in, L1_attn_b_in, L1_attn_W_xp, L1_attn_b_xp, L1_attn_W_dt, L1_attn_b_dt, L1_attn_W_out, L1_attn_b_out, L1_attn_A_log, L1_attn_D, L1_ffn_norm_weight, L1_ffn_router_w, L1_ffn_sw1, L1_ffn_sb1, L1_ffn_sw2, L1_ffn_sb2, L1_ffn_ew1, L1_ffn_eb1, L1_ffn_ew2, L1_ffn_eb2, L2_attn_w_G, L2_attn_b_G, L2_attn_w_K, L2_attn_w_V, L2_attn_w_Q, L2_attn_w_O, L2_attn_init_K_rec, L2_attn_init_V_rec, L2_ffn_W_r, L2_ffn_W_k, L2_ffn_W_v, L2_ffn_mu_r, L2_ffn_mu_k, L3_attn_w_qkv, L3_attn_w_out, L3_attn_b_out, L3_ffn_router_w, L3_ffn_router_bias, L3_ffn_up_proj, L3_ffn_gate_proj, L3_ffn_down_proj, L3_ffn_sh_gate, L3_ffn_sh_up, L3_ffn_sh_down):

    def _L0_attn_ref(hidden_states, w_q, w_k, w_v, w_o, gate, memory, memory_norm):
        import jax, jax.numpy as jnp
        import numpy as np
        HIDDEN = 128
        D_MEM = 32
        BATCH = 4
        SEQ = 128
        EPS = 1e-06

        def elu_plus_one(x):
            return jnp.where(x > 0, x + 1.0, jnp.exp(x))

        def _retrieve(sigma_x, memory, memory_norm):
            a_unnorm = jnp.matmul(sigma_x, memory)
            norm = jnp.clip(jnp.matmul(sigma_x, memory_norm), EPS, None)[..., None]
            out = a_unnorm / norm
            return jnp.where(memory_norm.sum() < EPS, jnp.zeros_like(out), out)

        def _reference_tuple_inner(hidden_states, w_q, w_k, w_v, w_o, gate, memory, memory_norm):
            b, s, _ = hidden_states.shape
            q = jnp.einsum('bsh,dh->bsd', hidden_states, w_q)
            k = jnp.einsum('bsh,dh->bsd', hidden_states, w_k)
            v = jnp.einsum('bsh,dh->bsd', hidden_states, w_v)
            sigma_q = elu_plus_one(q)
            sigma_k = elu_plus_one(k)
            memory_output = _retrieve(sigma_q, memory, memory_norm)
            kv = jnp.einsum('bsd,bse->bsde', sigma_k, v)
            kv_cumsum = jnp.cumsum(kv, axis=1)
            k_cumsum = jnp.cumsum(sigma_k, axis=1)
            numerator = jnp.einsum('bsd,bsde->bse', sigma_q, kv_cumsum)
            denominator = jnp.clip(jnp.einsum('bsd,bsd->bs', sigma_q, k_cumsum), EPS, None)[..., None]
            local_output = numerator / denominator
            g = jax.nn.sigmoid(gate[0])
            combined = g * memory_output + (1.0 - g) * local_output
            output = jnp.einsum('bsd,hd->bsh', combined, w_o)
            retrieved_unnorm = jnp.matmul(sigma_k, memory)
            norm = jnp.clip(jnp.matmul(sigma_k, memory_norm), EPS, None)[..., None]
            delta_v = v - retrieved_unnorm / norm
            memory_update = jnp.einsum('bsd,bse->de', sigma_k, delta_v) / (b * s)
            new_memory = jax.lax.stop_gradient(memory + memory_update)
            z_update = sigma_k.sum(axis=(0, 1)) / b
            new_memory_norm = jax.lax.stop_gradient(memory_norm + z_update)
            return (output, new_memory, new_memory_norm)
        return _reference_tuple_inner(hidden_states, w_q, w_k, w_v, w_o, gate, memory, memory_norm)[0]

    def _L0_ffn_ref(x, cond, mask, W_shared, W_expert, W_gate, bias):
        import jax, jax.numpy as jnp
        import numpy as np
        E = 8
        K = 2
        D = 128
        B, N = (4, 512)
        DC = 64
        b, n, d = x.shape
        T = b * n
        xf = x.reshape(T, d)
        scores = jax.nn.softmax(xf @ W_gate, axis=-1)
        expert_weights, _ = jax.lax.top_k(scores, K)
        expert_weights = expert_weights / expert_weights.sum(-1, keepdims=True)
        expert_indices = (jnp.arange(T * K) % E).reshape(T, K)
        te = expert_indices.reshape(-1)
        w = expert_weights.reshape(-1)
        capacity = K * T // E
        order = jnp.argsort(te, stable=True)
        sorted_e = te[order]
        hist = jnp.bincount(te, length=E)
        starts = jnp.concatenate([jnp.zeros((1,), hist.dtype), jnp.cumsum(hist)[:-1]])
        pos = jnp.arange(T * K) - starts[sorted_e]
        valid = pos < capacity
        dest = jnp.where(valid, sorted_e * capacity + pos, E * capacity)
        tok = order // K
        gathered = jnp.zeros((E * capacity + 1, d), x.dtype).at[dest].set(xf[tok])
        gathered = gathered[:-1]
        y = gathered @ W_expert.T
        contrib = w[order][:, None] * y[jnp.minimum(dest, E * capacity - 1)]
        moe_out = jnp.zeros((T, d), x.dtype).at[tok].add(jnp.where(valid[:, None], contrib, 0.0))
        shared = xf @ W_shared.T
        out = (shared + moe_out + bias).reshape(b, n, d)
        return out

    def _L1_attn_ref(x, W_in, b_in, W_xp, b_xp, W_dt, b_dt, W_out, b_out, A_log, D):
        import jax, jax.numpy as jnp
        import numpy as np
        BATCH, SEQ, D_MODEL = (2, 512, 128)
        D_STATE, EXPAND = (64, 2)
        D_INNER = D_MODEL * EXPAND

        def _silu(v):
            return v * jax.nn.sigmoid(v)
        xr = x @ W_in + b_in
        x_inner, res = jnp.split(xr, 2, axis=-1)
        x_inner = _silu(x_inner)
        A = -jnp.exp(A_log)
        delta = jax.nn.softplus(x_inner @ W_dt + b_dt)
        mean_delta = delta.mean(axis=-1)
        a = jnp.exp(A[None, None, :] * mean_delta[..., None])
        bx = x_inner @ W_xp + b_xp

        def step(state, inp):
            a_t, bx_t = inp
            state = a_t * state + bx_t
            return (state, state.sum(axis=-1))
        init = jnp.zeros((x.shape[0], D_STATE), dtype=x.dtype)
        _, s_sum = jax.lax.scan(step, init, (a.transpose(1, 0, 2), bx.transpose(1, 0, 2)))
        s_sum = s_sum.T
        y = s_sum[..., None] * x_inner
        y = y * _silu(res)
        out = y @ W_out + b_out + x * D
        return out

    def _L1_ffn_ref(hidden_states, norm_weight, router_w, sw1, sb1, sw2, sb2, ew1, eb1, ew2, eb2):
        import jax, jax.numpy as jnp
        import numpy as np
        D, H, O, E, TOPK = (128, 512, 128, 8, 2)
        B, S = (4, 128)
        b, s, d = hidden_states.shape
        var = jnp.mean(jnp.square(hidden_states), axis=-1, keepdims=True)
        normed = hidden_states * jax.lax.rsqrt(var + 1e-08) * norm_weight
        shared = jnp.maximum(normed @ sw1 + sb1, 0.0) @ sw2 + sb2
        flat = normed.reshape(-1, d)
        T = flat.shape[0]
        probs = jax.nn.sigmoid(flat @ router_w.T)
        scores, idx = jax.lax.top_k(probs, TOPK)
        w = scores / (jnp.sum(scores, axis=-1, keepdims=True) + 1e-06)
        comb = jnp.zeros((T, E), dtype=flat.dtype)
        comb = comb.at[jnp.arange(T)[:, None], idx].add(w)
        h = jnp.maximum(jnp.einsum('td,edh->teh', flat, ew1) + eb1[None, :, :], 0.0)
        eo = jnp.einsum('teh,eho->teo', h, ew2) + eb2[None, :, :]
        routed = jnp.einsum('teo,te->to', eo, comb)
        return shared + routed.reshape(b, s, -1)

    def _L2_attn_ref(X, w_G, b_G, w_K, w_V, w_Q, w_O, init_K_rec, init_V_rec):
        import jax, jax.numpy as jnp
        import numpy as np
        N, T, D = (2, 512, 128)
        H, E, L = (8, 4, 32)
        DK, DV = (64, 64)

        def _pscan(A, Xv, Y0):
            Ae = jnp.broadcast_to(A[..., None], Xv.shape)
            Xv = Xv.at[..., 0, :].add(A[..., 0, None] * Y0)

            def op(c1, c2):
                a1, x1 = c1
                a2, x2 = c2
                return (a1 * a2, a2 * x1 + x2)
            _, Y = jax.lax.associative_scan(op, (Ae, Xv), axis=3)
            return Y
        n, t, _ = X.shape
        t_pad = ((t - 1) // L + 1) * L
        Xp = jnp.pad(X, ((0, 0), (0, t_pad - t), (0, 0)))
        G = jax.nn.sigmoid(jnp.einsum('ntd,hed->nhet', Xp, w_G) + b_G[None, :, :, None])
        K = jnp.einsum('ntc,hdc->nhtd', Xp, w_K)
        V = jnp.einsum('ntc,hdc->nhtd', Xp, w_V)
        A = 1.0 - jnp.minimum(G.sum(axis=1), 1.0)
        gK = jnp.einsum('nhet,nhtd->netd', G, K)
        gV = jnp.einsum('nhet,nhtd->netd', G, V)
        tc = t_pad // L
        A = A.reshape(n, E, L, tc)
        gK = gK.reshape(n, E, L, tc, DK)
        gV = gV.reshape(n, E, L, tc, DV)
        iK = jnp.broadcast_to(init_K_rec[None], (n, E, L, DK))
        iV = jnp.broadcast_to(init_V_rec[None], (n, E, L, DV))
        nK = _pscan(A, gK, iK).reshape(n, E, t_pad, DK)
        nV = _pscan(A, gV, iV).reshape(n, E, t_pad, DV)
        recK = jnp.concatenate([iK, nK], axis=2)
        recV = jnp.concatenate([iV, nV], axis=2)
        idx = 1 + jnp.arange(t_pad)[:, None] + jnp.arange(L)[None, :]
        uk = recK[:, :, idx]
        uv = recV[:, :, idx]
        Q = jnp.einsum('ntc,hdc->nhtd', Xp, w_Q)
        scores = jnp.einsum('nhtd,netld->nhtel', Q, uk) / jnp.float32(np.sqrt(DK))
        probs = jax.nn.softmax(scores.reshape(n, H, t_pad, E * L), axis=-1).reshape(scores.shape)
        Y = jnp.einsum('nhtel,netld->nthd', probs, uv).reshape(n, t_pad, H * DV)
        return (Y @ w_O)[:, :t]

    def _L2_ffn_ref(x, W_r, W_k, W_v, mu_r, mu_k):
        import jax, jax.numpy as jnp
        import numpy as np
        DIM = 128

        def _reference_tuple_inner(x, W_r, W_k, W_v, mu_r, mu_k):
            B, T, C = x.shape
            x_prev = jnp.concatenate([jnp.zeros((B, 1, C), x.dtype), x[:, :-1, :]], axis=1)
            xr = mu_r * x + (1.0 - mu_r) * x_prev
            xk = mu_k * x + (1.0 - mu_k) * x_prev
            r = jax.nn.sigmoid(jnp.einsum('btc,dc->btd', xr, W_r))
            k = jnp.einsum('btc,dc->btd', xk, W_k)
            k_act = jnp.square(jax.nn.relu(k))
            out = r * jnp.einsum('btc,dc->btd', k_act, W_v)
            new_state = x[:, -1, :]
            return (out, new_state)
        return _reference_tuple_inner(x, W_r, W_k, W_v, mu_r, mu_k)[0]

    def _L3_attn_ref(x, w_qkv, w_out, b_out):
        import jax, jax.numpy as jnp
        import numpy as np
        DIM_IN, DIM_OUT, DIM_INNER = (128, 128, 64)
        scale = DIM_INNER ** (-0.5)
        qkv = jnp.einsum('bnd,ed->bne', x, w_qkv)
        q, k, v = jnp.split(qkv, 3, axis=-1)
        sim = jnp.einsum('bid,bjd->bij', q, k) * scale
        n = sim.shape[-1]
        causal = jnp.tril(jnp.ones((n, n), dtype=bool))
        sim = jnp.where(causal[None], sim, -jnp.finfo(sim.dtype).max)
        attn = jax.nn.softmax(sim, axis=-1)
        out = jnp.einsum('bij,bjd->bid', attn, v)
        return jnp.einsum('bnd,od->bno', out, w_out) + b_out

    def _L3_ffn_ref(x, router_w, router_bias, up_proj, gate_proj, down_proj, sh_gate, sh_up, sh_down):
        import jax, jax.numpy as jnp
        import numpy as np
        DIM = 128
        EXPERT_DIM = 64
        N_EXPERTS = 16
        TOPK = 2
        SHARED_HIDDEN = EXPERT_DIM * TOPK
        B, T = (4, 128)

        def _moe_forward(x, router_w, router_bias, up_proj, gate_proj, down_proj, sh_gate, sh_up, sh_down):
            Bb, Tt, D = x.shape
            flat = x.reshape(Bb * Tt, D)
            N = flat.shape[0]
            logits = flat @ router_w.T
            topk_scores, topk_idx = jax.lax.top_k(logits + router_bias, TOPK)
            topk_scores = jax.nn.softmax(topk_scores, axis=-1)
            combine = jnp.zeros((N, N_EXPERTS), flat.dtype)
            combine = combine.at[jnp.arange(N)[:, None], topk_idx].add(topk_scores)
            up_all = jnp.einsum('nd,kde->nke', flat, up_proj)
            gate_all = jnp.einsum('nd,kde->nke', flat, gate_proj)
            hidden = jax.nn.silu(gate_all) * up_all
            down_all = jnp.einsum('nke,ked->nkd', hidden, down_proj)
            out = jnp.einsum('nk,nkd->nd', combine, down_all)
            sh_hidden = jax.nn.silu(flat @ sh_gate.T) * (flat @ sh_up.T)
            out = out + sh_hidden @ sh_down.T
            return out.reshape(Bb, Tt, D)
        return _moe_forward(x, router_w, router_bias, up_proj, gate_proj, down_proj, sh_gate, sh_up, sh_down)
    x = L0_attn_hidden_states
    xn = _layernorm(x, axis=-1)
    s = _L0_attn_ref(xn, L0_attn_w_q, L0_attn_w_k, L0_attn_w_v, L0_attn_w_o, L0_attn_gate, L0_attn_memory, L0_attn_memory_norm)
    g = _silu(_L0_ffn_ref(xn, L0_ffn_cond, L0_ffn_mask, L0_ffn_W_shared, L0_ffn_W_expert, L0_ffn_W_gate, L0_ffn_bias))
    x = x + s * g
    xn = _layernorm(x, axis=-1)
    s = _L1_attn_ref(xn, L1_attn_W_in, L1_attn_b_in, L1_attn_W_xp, L1_attn_b_xp, L1_attn_W_dt, L1_attn_b_dt, L1_attn_W_out, L1_attn_b_out, L1_attn_A_log, L1_attn_D)
    g = _silu(_L1_ffn_ref(xn, L1_ffn_norm_weight, L1_ffn_router_w, L1_ffn_sw1, L1_ffn_sb1, L1_ffn_sw2, L1_ffn_sb2, L1_ffn_ew1, L1_ffn_eb1, L1_ffn_ew2, L1_ffn_eb2))
    x = x + s * g
    xn = _layernorm(x, axis=-1)
    s = _L2_attn_ref(xn, L2_attn_w_G, L2_attn_b_G, L2_attn_w_K, L2_attn_w_V, L2_attn_w_Q, L2_attn_w_O, L2_attn_init_K_rec, L2_attn_init_V_rec)
    g = _silu(_L2_ffn_ref(xn, L2_ffn_W_r, L2_ffn_W_k, L2_ffn_W_v, L2_ffn_mu_r, L2_ffn_mu_k))
    x = x + s * g
    xn = _layernorm(x, axis=-1)
    s = _L3_attn_ref(xn, L3_attn_w_qkv, L3_attn_w_out, L3_attn_b_out)
    g = _silu(_L3_ffn_ref(xn, L3_ffn_router_w, L3_ffn_router_bias, L3_ffn_up_proj, L3_ffn_gate_proj, L3_ffn_down_proj, L3_ffn_sh_gate, L3_ffn_sh_up, L3_ffn_sh_down))
    x = x + s * g
    return x

_drawn_inputs = setup_inputs


def setup_inputs(seed=0):
    import zlib

    import numpy as np

    out = dict(_drawn_inputs(seed))
    spreads = {'L0_ffn_bias': (0.0, 0.1),
     'L1_attn_b_in': (0.0, 0.1),
     'L1_attn_b_xp': (0.0, 0.1),
     'L1_attn_b_dt': (0.0, 0.1),
     'L1_attn_b_out': (0.0, 0.1),
     'L1_ffn_norm_weight': (1.0, 0.2),
     'L1_ffn_sb1': (0.0, 0.1),
     'L1_ffn_sb2': (0.0, 0.1),
     'L1_ffn_eb1': (0.0, 0.1),
     'L1_ffn_eb2': (0.0, 0.1),
     'L2_attn_b_G': (-2.8284270763397217, 0.2),
     'L3_ffn_router_bias': (0.0, 0.1)}
    factors = {}
    for name, (base, spread) in spreads.items():
        noise = np.random.default_rng([zlib.crc32(name.encode()), seed]).standard_normal(out[name].shape)
        drawn = base * np.exp(spread * noise) if base else spread * noise
        out[name] = jnp.asarray(drawn.astype(out[name].dtype))
    for name, factor in factors.items():
        out[name] = (out[name] * factor).astype(out[name].dtype)
    return out
```

```python
from contextlib import ExitStack

import numpy as np

import concourse.bass as bass
from concourse import mybir

ALU = mybir.AluOpType
ACT = mybir.ActivationFunctionType
AX = mybir.AxisListType
F32 = mybir.dt.float32
BF16 = mybir.dt.bfloat16
U32 = mybir.dt.uint32

B, T, D = 2, 1024, 128
P = 128
GT = 512
G = T // GT
CT = 128
C = GT // CT
DM = 32
EPS_MEM = 1e-6
NGATE = 7
KVG = 2 * DM + NGATE
ST = 64
E1, H1 = 8, 512
HJ = H1 // P
NH, NE, L, DK = 8, 4, 32, 64
NB = T // L
GB = GT // L
E3, H3 = 16, 64
EP3 = E3 // 2
NEG = -1e30
VT_JOBS = [[range(0, 8), range(8, 16), range(16, 17)], [range(17, 25), range(25, 33)]]
ROOM = 24200

PACK0 = [("wqk", 2 * DM), ("wkvg", KVG), ("wsh", D), ("wex", D), ("bias", 1)]
SMALL0 = [("mem", 2 * DM), ("mnorm", DM), ("gate", 1), ("wo", D)]
PACK1 = [("win", 512), ("wdt", 2 * D), ("wxp", 2 * ST), ("wout", 2 * D), ("rw", E1), ("sw1", H1), ("sw2", HJ * D),
         ("bin", 4), ("bdt", 1), ("bout", 1), ("dskip", 1), ("wn", 1), ("sb1", HJ), ("sb2", 1), ("eb1", E1 * HJ)]
SMALL1 = [("alog", 1), ("bxp", 1)]
PACK2 = [("wg", 32), ("wkv", NH * 128), ("wq", NH * DK), ("wo", 4 * D), ("init", NE * L),
         ("wr", D), ("wk", D), ("wv", D), ("mur", 1), ("muk", 1)]
PACK3 = [("wqk", 2 * DK), ("wv", DK), ("bout", 1), ("rw", E3), ("rb", E3), ("gate", E3 * H3), ("up", E3 * H3),
         ("down", EP3 * D), ("shg", D), ("shu", D), ("shd", D)]


def columns(pack):
    at, out = 0, {}
    for name, n in pack:
        out[name] = (at, at + n)
        at += n
    return out, at


class Steps:

    def __init__(self, sem, reached):
        self.sem, self.count, self.reached = sem, 0, reached

    def step(self, *milestone, by=1):
        self.count += by
        if milestone:
            self.reached[milestone] = (self.sem.name, self.count)
        return self.sem, by


def four_layers(nc, known, x_in, p0, s0, p1, s1, eb2, ew1, ew2, p2, bg, p3, wout3, out):
    reached = {}
    with ExitStack() as ctx:
        def sb(name, shape, dt=F32):
            return ctx.enter_context(nc.sbuf_tensor(name, shape, dt))

        sems = {}

        def sem(name):
            sems[name] = ctx.enter_context(nc.semaphore(name))
            return sems[name]

        def at(*milestone):
            name, value = known.get(milestone, ("loads", 16))
            return sems[name], value

        def packed(tile, pack):
            where, _ = columns(pack)
            return {name: tile[:, a:b] for name, (a, b) in where.items()}

        w0t = sb("w0", [P, columns(PACK0)[1]])
        w0s = sb("w0s", [DM, columns(SMALL0)[1]])
        w1t = sb("w1", [P, columns(PACK1)[1]])
        w1s = sb("w1s", [ST, 2])
        w_eb2 = sb("w_eb2", [E1, D])
        w_ew1 = sb("w_ew1", [P, E1, H1])
        w_ew2 = sb("w_ew2", [P, E1, HJ, D])
        w2t = sb("w2", [P, columns(PACK2)[1]])
        w_bg = sb("w_bg", [32, 1])
        w3t = sb("w3", [P, columns(PACK3)[1]])
        w_out3 = sb("w_out3", [DK, D])
        W0, S0, W1, S1 = packed(w0t, PACK0), packed(w0s, SMALL0), packed(w1t, PACK1), packed(w1s, SMALL1)
        W2, W3 = packed(w2t, PACK2), packed(w3t, PACK3)

        ident = sb("ident", [P, P])
        identb = sb("identb", [P, P], BF16)
        center = sb("center", [P, P])
        mean = sb("mean", [P, P])
        ones = sb("ones", [ST, P])
        causal = sb("causal", [P, P])
        above = sb("above", [P, P], BF16)
        iota8 = sb("iota8", [P, E3])
        flag = sb("flag", [DM, 4])
        half0 = sb("half0", [P, 1])
        half1 = sb("half1", [P, 5])
        neg_a = sb("neg_a", [ST, 1])
        neg_bg = sb("neg_bg", [32, 1])
        sel_he = sb("sel_he", [96, 32, P], BF16)
        sel_e = sb("sel_e", [96, NE, P], BF16)
        sel_q = sb("sel_q", [L, P], BF16)
        cage = sb("cage", [L, NE * 2 * L], BF16)
        sel_p = sb("sel_p", [48, EP3, P], BF16)
        neg_big = sb("neg_big", [P, 1])

        x = sb("x", [P, T])
        xn_a = sb("xn_a", [P, T + 1])
        xn_b = sb("xn_b", [P, T])
        xn = [xn_a[:, 1:T + 1], xn_b[:, :], xn_a[:, 1:T + 1], xn_b[:, :]]
        sq = sb("sq", [P, 2, GT])
        rs = sb("rs", [P, 2, GT])
        hz = sb("hz", [P, GT])
        tz = sb("tz", [P, GT])
        room = sb("arena", [P, ROOM])
        used = [0]

        def take(shape, parts=P, dt=F32):
            n = int(np.prod(shape))
            words = n if dt == F32 or dt == U32 else (n + 1) // 2
            v = room[0:parts, used[0]:used[0] + words]
            used[0] += words
            assert used[0] <= ROOM, used
            if dt != F32:
                v = v.bitcast(dt)
            names = "abcd"[:len(shape)]
            if len(shape) == 1:
                return v
            return v.rearrange(f"p ({' '.join(names)}) -> p {' '.join(names)}", **dict(zip(names, shape)))

        used[0] = 0
        xi = take([2, T])
        sr = take([2, GT])
        hx = take([2, GT])
        tx = take([2, GT])
        dab = take([GT])
        dpos = take([GT])
        decay = take([T], ST)
        bx = take([T], ST)
        states = take([T], ST)
        ssum = take([GT])
        s1out = take([GT])
        xd = take([GT])
        nm = take([T])
        hid = take([2, HJ, GT])
        acc = take([C, P])
        pr = take([2 * C, E1])
        top1 = take([2 * C, 8])
        idx1 = take([2 * C, 8], dt=U32)
        idf1 = take([2 * C, 8])
        wsm1 = take([2 * C, 4])
        oh1 = take([2, 2 * C, E1])
        cmb1 = take([2 * C, E1])
        cbt1 = take([2, GT], E1)

        ek = take([GT], ST)
        sgq = take([T], DM)
        sgk = take([T], DM)
        et = take([C, DM])
        ktok = take([2 * C, DM])
        vtok0 = sb("vtok0", [P, 2 * C, 2 * DM])
        logit = sb("logit", [P, 2 * C, 8])
        att = take([C, P])
        state = sb("state", [DM, 2 * C + 1, 2 * DM])
        rn = take([GT], DM)
        rd = take([GT], DM)
        comb0 = take([GT], DM)
        c2 = take([GT], DM)
        top = take([2 * C, 8])
        gw = take([2 * C, 6])
        ysc = take([C, P])

        used[0] = 0
        abc = take([NE, GB, L + 1])
        rec = take([NB + 1, L + 1, NE])
        vt = take([NB + 1, DK])
        qf = take([GB, NH, L], DK)
        yt = take([4, GT])
        gfm = take([3, GT], 32)
        gb = take([2, GT], 32, BF16)
        g3 = take([GT], 96, BF16)
        xs = take([3, GT])
        prob = take([3, 2, 4 * 2 * L])
        pt = take([3, GT])
        smx = take([3, 8])
        dx = take([GT])
        xr = take([GT])
        xk = take([GT])
        kr = dx
        tr = take([GT])
        of = xk

        used[0] = 0
        q3 = take([T], DK)
        k3 = take([T], DK)
        v3 = take([2 * C, DK])
        p3b = take([2, T])
        pt3 = take([2, C, P])
        sm3 = take([2 * C, 8])
        o3 = take([2, GT], DK)
        lg3 = take([2 * C, E3])
        top3 = take([2 * C, 8])
        idx3 = take([2 * C, 8], dt=U32)
        idf3 = take([2 * C, 8])
        w3s = take([2 * C, 4])
        oh3 = take([2, 2 * C, E3])
        cm3 = take([2 * C, E3])
        cb3 = take([2 * C, 48], dt=BF16)
        cr3 = take([2 * C, E3])
        ct3 = take([2, GT], 48, BF16)
        tg3 = take([2, GT])
        h3 = take([2, GT])
        hh3 = take([3, GT])

        bank = [ctx.enter_context(nc.psum_tensor(f"bank{i}", [P, GT], F32)) for i in range(8)]

        loads, stores = sem("loads"), sem("stores")
        load_x = [sem(f"load_x{g}") for g in range(G)]
        once = Steps(sem("once"), reached)
        once_v, once_a = Steps(sem("once_vector"), reached), Steps(sem("once_scalar"), reached)
        prog = {(e, l): Steps(sem(f"l{l}_{e}"), reached) for l in range(4)
                for e in ("tensor", "vector", "scalar", "gpsimd")}

        def gs(g):
            return slice(g * GT, (g + 1) * GT)

        def cs(c):
            return slice(c * CT, (c + 1) * CT)

        with nc.Block() as block:
            @block.sync
            def _(sp):
                for dst, src in ((w0t[:], p0), (w0s[:], s0), (w1t[:], p1), (w1s[:], s1), (w2t[:], p2), (w_bg[:], bg),
                                 (w_eb2[:], eb2), (w3t[:], p3), (w_out3[:], wout3),
                                 (w_ew1[:], ew1), (w_ew2[:], ew2)):
                    sp.dma_start(dst, src).then_inc(loads, 16)
                sp.wait_ge(loads, 16 * 11)

            @block.gpsimd
            def _(pool):
                def done():
                    pool.wait_ge(once.sem, once.count)
                for tile, v in ((ident, 0.0), (identb, 0.0), (ones, 1.0), (causal, 1.0), (above, 0.0), (mean, 1.0 / D),
                                (center, -1.0 / D), (sel_he, 0.0), (sel_e, 0.0), (sel_q, 0.0), (cage, 0.0),
                                (sel_p, 0.0), (xn_a, 0.0), (vtok0, 1.0), (logit, -3e38),
                                (state, 0.0), (neg_big, NEG)):
                    nc.gpsimd.memset(tile[:], v).then_inc(*once.step())
                done()

                def where(tile, op, fill, base, pattern, mult):
                    nc.gpsimd.affine_select(out=tile, in_=tile, compare_op=op, fill=fill, base=base,
                                            pattern=pattern, channel_multiplier=mult).then_inc(*once.step())
                where(ident[:], ALU.not_equal, 1.0, 0, [[-1, P]], 1)
                where(identb[:], ALU.not_equal, 1.0, 0, [[-1, P]], 1)
                where(center[:], ALU.not_equal, 1.0 - 1.0 / D, 0, [[-1, P]], 1)
                where(causal[:], ALU.is_ge, 0.0, 0, [[1, P]], -1)
                where(above[:], ALU.is_ge, NEG, 0, [[-1, P]], 1)
                nc.gpsimd.iota(iota8[:], [[1, E3]], base=0, channel_multiplier=0,
                               allow_small_or_imprecise_dtypes=True).then_inc(*once.step())
                where(sel_q[:].rearrange("p (h q) -> p h q", q=L), ALU.not_equal, 1.0, 0, [[0, 4], [-1, L]], 1)
                ks = cage[:].rearrange("p (k e) -> p k e", e=NE)
                where(ks, ALU.is_ge, NEG, -1, [[1, 2 * L], [0, NE]], -1)
                done()
                where(ks, ALU.is_ge, NEG, L, [[-1, 2 * L], [0, NE]], 1)
                for part in range(3):
                    where(sel_he[:], ALU.not_equal, 1.0, -32 * part, [[-1, 32], [0, P]], 1)
                    done()
                    where(sel_p[:].rearrange("p a (b c) -> p a b c", b=2), ALU.not_equal, 1.0, -16 * part,
                          [[-2, EP3], [-1, 2], [0, DK]], 1)
                    done()
                for h in range(3 * NH):
                    where(sel_e[:], ALU.not_equal, 1.0, -NE * h, [[-1, NE], [0, P]], 1)
                    done()

            @block.vector
            def _(dve):
                dve.wait_ge(loads, 16 * 11)
                v = once_v

                def done():
                    dve.wait_ge(v.sem, v.count)
                nc.vector.tensor_scalar(half0[:], W0["bias"], 0.5, None, ALU.mult).then_inc(*v.step())
                nc.vector.tensor_scalar(half1[:, 0:4], W1["bin"], 0.5, None, ALU.mult).then_inc(*v.step())
                nc.vector.tensor_scalar(half1[:, 4:5], W1["sb2"], 0.5, None, ALU.mult).then_inc(*v.step())
                nc.vector.tensor_scalar(neg_bg[:], w_bg[:], -1.0, None, ALU.mult).then_inc(*v.step())
                nc.vector.tensor_reduce(flag[:, 2:3], S0["mnorm"], AX.X, ALU.add).then_inc(*v.step())
                done()
                nc.vector.tensor_scalar(flag[:, 2:3], flag[:, 2:3], EPS_MEM, None, ALU.is_ge).then_inc(*v.step())
                dve.wait_ge(once_a.sem, 1)
                nc.vector.tensor_scalar(flag[:, 3:4], flag[:, 3:4], 1.0, None, ALU.add).then_inc(*v.step())
                done()
                nc.vector.reciprocal(flag[:, 3:4], flag[:, 3:4]).then_inc(*v.step())
                done()
                nc.vector.tensor_tensor(flag[:, 0:1], flag[:, 3:4], flag[:, 2:3], ALU.mult).then_inc(*v.step())
                nc.vector.tensor_scalar(flag[:, 1:2], flag[:, 3:4], -1.0, 1.0, ALU.mult, ALU.add).then_inc(*v.step())
                dve.wait_ge(once_a.sem, 2)
                nc.vector.tensor_scalar(neg_a[:], neg_a[:], -1.0, None, ALU.mult).then_inc(*v.step())

            @block.scalar
            def _(act):
                act.wait_ge(loads, 16 * 11)
                nc.scalar.activation(flag[:, 3:4], S0["gate"], ACT.Exp, scale=-1.0).then_inc(*once_a.step())
                nc.scalar.activation(neg_a[:], S1["alog"], ACT.Exp).then_inc(*once_a.step())

        with nc.Fori(0, B) as b:
            with nc.Block(no_gpsimd_drain=True) as block:

                rings = {"quick": [0, 1, 2, 3], "slow": [4, 5, 6, 7]}
                turn = {"quick": 0, "slow": 0}
                owner = {}

                @block.sync
                def _(sp):
                    xv = x_in.rearrange("b p t -> (b p) t")
                    ov = out.rearrange("b p t -> (b p) t")
                    for g in range(G):
                        sp.dma_start(x[:, gs(g)], xv[bass.ds(b * P, P), gs(g)]).then_inc(load_x[g], 16)
                        reached[("x in", g)] = (load_x[g].name, 16)
                    for g in range(G):
                        sp.wait_ge(*at("x out", g))
                        sp.dma_start(ov[bass.ds(b * P, P), gs(g)], x[:, gs(g)]).then_inc(stores, 16)
                    sp.wait_ge(stores, 16 * G)

                @block.tensor
                def _(pe):
                    now = [0]
                    growing = ["none"]

                    def step(*m):
                        if m and m == growing[0]:
                            growing[0] = "none"
                        return prog["tensor", now[0]].step(*m)

                    def fresh(ring, *job):
                        while True:
                            i = rings[ring][turn[ring] % 4]
                            turn[ring] += 1
                            if owner.get(i) != growing[0]:
                                break
                        if job[0] == "ff":
                            growing[0] = job
                        if i in owner:
                            pe.wait_ge(*at(*owner[i], "read"))
                        owner[i] = job
                        reached[job + ("bank",)] = i
                        return bank[i]

                    def mm(o, lhsT, rhs, start=True, stop=True):
                        return nc.tensor.matmul(o, lhsT, rhs, start=start, stop=stop, skip_group_check=True)

                    def norm(l, g):
                        pe.wait_ge(*(at("x in", g) if l == 0 else at("x", l, g)))
                        mm(fresh("quick", "xc", l, g)[:], center[:], x[:, gs(g)]).then_inc(*step("xc", l, g))

                    def variance(l, g, name="var"):
                        pe.wait_ge(*at("sq", name, l, g))
                        mm(fresh("quick", name, l, g)[:], mean[:], sq[:, g]).then_inc(*step(name, l, g))

                    def layer0(g):
                        norm(0, g)
                        variance(0, g)
                        xg = xn[0][:, gs(g)]
                        pe.wait_ge(*at("xn", 0, g))
                        o = fresh("quick", "qk0", g)
                        mm(o[0:2 * DM], W0["wqk"], xg).then_inc(*step("qk0", g))
                        o = fresh("quick", "kvg0", g)
                        for c in range(C):
                            i = mm(o[:, c * KVG:(c + 1) * KVG], xg[:, cs(c)], W0["wkvg"])
                        i.then_inc(*step("kvg0", g))
                        ff = fresh("slow", "ff", 0, g)
                        mm(ff[:], W0["wsh"], xg, stop=False)
                        o = fresh("quick", "y0", g)
                        for c in range(C):
                            i = mm(o[:, cs(c)], xg[:, cs(c)], W0["wex"])
                        i.then_inc(*step("y0", g))
                        o = fresh("slow", "kv0", g)
                        pe.wait_ge(*at("vtok0", g))
                        pe.wait_ge(*at("ktok0", g))
                        for c in range(C):
                            i = mm(o[0:DM, c * 64:c * 64 + 64], ktok[:, g * C + c], vtok0[:, g * C + c])
                        i.then_inc(*step("kv0", g))
                        o = fresh("quick", "a0", g)
                        pe.wait_ge(*at("sgk", g))
                        for c in range(C):
                            t = slice(g * GT + c * CT, g * GT + (c + 1) * CT)
                            i = mm(o[:, cs(c)], sgk[:, t], sgq[:, t])
                        i.then_inc(*step("a0", g))
                        o = fresh("quick", "ret0", g)
                        mm(o[0:2 * DM], S0["mem"], sgq[:, gs(g)]).then_inc(*step("ret0", g))
                        pe.wait_ge(*at("ysc", g))
                        for c in range(C):
                            i = mm(ff[:, cs(c)], ysc[:, c], ident[:], start=False, stop=c == C - 1)
                        i.then_inc(*step("ff", 0, g))
                        o = fresh("quick", "num0", g)
                        pe.wait_ge(*at("att0", g))
                        pe.wait_ge(*at("state", g))
                        for c in range(C):
                            t = slice(g * GT + c * CT, g * GT + (c + 1) * CT)
                            mm(o[0:64, cs(c)], vtok0[:, g * C + c], att[:, c], stop=False)
                            i = mm(o[0:64, cs(c)], state[:, g * C + c], sgq[:, t], start=False)
                        i.then_inc(*step("num0", g))
                        o = fresh("slow", "s", 0, g)
                        pe.wait_ge(*at("comb0", g))
                        mm(o[:], S0["wo"], comb0[:]).then_inc(*step("s", 0, g))

                    def layer1(g):
                        norm(1, g)
                        variance(1, g)
                        xg = xn[1][:, gs(g)]
                        pe.wait_ge(*at("xn", 1, g))
                        for j in range(4):
                            mm(fresh("quick", "xr", g, j)[:], W1["win"][:, cs(j)], xg).then_inc(*step("xr", g, j))
                        variance(1, g, "rms")
                        o = fresh("quick", "dt", g)
                        pe.wait_ge(*at("xi", g, 1))
                        for j in range(2):
                            i = mm(o[:], W1["wdt"][:, cs(j)], xi[:, j, gs(g)], start=j == 0, stop=j == 1)
                        i.then_inc(*step("dt", g))
                        o = fresh("quick", "bx", g)
                        for j in range(2):
                            i = mm(o[0:ST], W1["wxp"][:, j * ST:(j + 1) * ST], xi[:, j, gs(g)], start=j == 0,
                                   stop=j == 1)
                        i.then_inc(*step("bx", g))
                        o = fresh("quick", "rt1", g)
                        pe.wait_ge(*at("nm", g))
                        for c in range(C):
                            t = slice(g * GT + c * CT, g * GT + (c + 1) * CT)
                            i = mm(o[:, c * E1:(c + 1) * E1], nm[:, t], W1["rw"])
                        i.then_inc(*step("rt1", g))
                        ff = fresh("slow", "ff", 1, g)

                        def first(e):
                            for j in range(HJ):
                                w = W1["sw1"][:, cs(j)] if e == E1 else w_ew1[:, e, cs(j)]
                                mm(fresh("quick", "h1", g, e, j)[:], w, nm[:, gs(g)]).then_inc(*step("h1", g, e, j))

                        def second(e):
                            h = hid[:, e % 2]
                            if e == E1:
                                pe.wait_ge(*at("hid", g, e, 2))
                                pe.wait_ge(*at("hid", g, e, 3))
                                for j in range(HJ):
                                    i = mm(ff[:], W1["sw2"][:, cs(j)], h[:, j], start=False, stop=False)
                                i.then_inc(*step("eo", g, e))
                                return
                            o = fresh("slow", "eo", g, e)
                            pe.wait_ge(*at("hid", g, e, 2))
                            pe.wait_ge(*at("hid", g, e, 3))
                            for c in range(C):
                                for j in range(HJ):
                                    i = mm(o[:, cs(c)], h[:, j, cs(c)], w_ew2[:, e, j], start=j == 0,
                                           stop=j == HJ - 1)
                            i.then_inc(*step("eo", g, e))

                        first(0)
                        o = fresh("quick", "cbt", g)
                        pe.wait_ge(*at("cmb1", g))
                        for c in range(C):
                            i = nc.tensor.transpose(o[0:E1, cs(c)], cmb1[:, g * C + c], ident[:])
                        i.then_inc(*step("cbt", g))
                        first(1)
                        o = fresh("quick", "md", g)
                        pe.wait_ge(*at("delta", g))
                        mm(o[0:ST], mean[:, 0:ST], dab[:]).then_inc(*step("md", g))
                        second(0)
                        first(2)
                        o = fresh("quick", "ss", g)
                        pe.wait_ge(*at("states", g))
                        mm(o[:], ones[:], states[:, gs(g)]).then_inc(*step("ss", g))
                        pe.wait_ge(*at("cbt_s", g))
                        mm(ff[:], w_eb2[:], cbt1[:, g], stop=False)
                        second(1)
                        o = fresh("quick", "wo1", g)
                        pe.wait_ge(*at("z", g))
                        for j in range(2):
                            i = mm(o[:], W1["wout"][:, cs(j)], xi[:, j, gs(g)], start=j == 0, stop=j == 1)
                        i.then_inc(*step("wo1", g))
                        for e in range(3, E1 + 1):
                            first(e)
                            second(e - 1)
                        second(E1)
                        pe.wait_ge(*at("acc", g, E1 - 1))
                        for c in range(C):
                            i = mm(ff[:, cs(c)], acc[:, c], ident[:], start=False, stop=c == C - 1)
                        i.then_inc(*step("ff", 1, g))

                    def layer2_rec(g):
                        norm(2, g)
                        variance(2, g)
                        xg = xn[2][:, gs(g)]
                        pe.wait_ge(*at("xn", 2, g))
                        mm(fresh("quick", "gt", g)[0:32], W2["wg"], xg).then_inc(*step("gt", g))
                        for j in range(4):
                            mm(fresh("quick", "q2", g, j)[:], W2["wq"][:, cs(j)], xg).then_inc(*step("q2", g, j))
                        pe.wait_ge(*at("g3", g))
                        for e in range(NE):
                            mm(fresh("quick", "ga", g, e)[:], sel_e[:, e], g3[:]).then_inc(*step("ga", g, e))
                        accs = {}

                        def spread(n):
                            he = n % NH * NE + n // NH
                            mm(fresh("quick", "gb", g, n)[:], sel_he[:, he], g3[:]).then_inc(*step("gb", g, n))

                        def project(n):
                            e, h = n // NH, n % NH
                            if h == 0:
                                accs[e] = fresh("slow", "gkv", g, e)
                            pe.wait_ge(*at("xs", g, n))
                            i = mm(accs[e][:], W2["wkv"][:, h * 128:(h + 1) * 128], xs[:, n % 3], start=h == 0,
                                   stop=h == NH - 1)
                            i.then_inc(*step("gkv", g, n))
                        for n in range(NE * NH + 2):
                            if n < NE * NH:
                                spread(n)
                            if n >= 2:
                                project(n - 2)

                    def layer2_att(g):
                        for n, blocks in enumerate(VT_JOBS[g]):
                            o = fresh("quick", "vt", g, n)
                            pe.wait_ge(*at("rec", g, NE - 1))
                            for k, blk in enumerate(blocks):
                                src = rec[64:128, blk, 1:L + 1].rearrange("p c e -> p (c e)")
                                i = nc.tensor.transpose(o[:, k * DK:(k + 1) * DK], src, ident[64:128, 64:128])
                            i.then_inc(*step("vt", g, n))
                        pv_bank = {}

                        def score(l):
                            lb = g * GB + l
                            o = fresh("quick", "s2", g, l)
                            mm(o[:].rearrange("p (a b) -> p a b", a=2), sel_q[:],
                               cage[:].rearrange("p (a b) -> p a b", a=1).to_broadcast([L, 2, NE * 2 * L]), stop=False)
                            if l == 0:
                                pe.wait_ge(*at("qf", g, 3))
                            for hg in range(2):
                                i = mm(o[:, hg * 256:hg * 256 + 256],
                                       qf[:, l, 4 * hg:4 * hg + 4].rearrange("p h q -> p (h q)"),
                                       rec[0:64, lb:lb + 2, 1:L + 1].rearrange("p b c e -> p b (c e)"),
                                       start=False, stop=hg == 1)
                            i.then_inc(*step("s2", g, l))

                        def turned(l):
                            o = fresh("quick", "pt", g, l)
                            pe.wait_ge(*at("prob", g, l))
                            for blk in range(2):
                                for hg in range(2):
                                    k = (blk * 2 + hg) * P
                                    i = nc.tensor.transpose(o[:, k:k + P], prob[:, l % 3, hg, blk * P:(blk + 1) * P],
                                                            ident[:])
                            i.then_inc(*step("pt", g, l))

                        def value(l):
                            if l % 2 == 0:
                                pv_bank[0] = fresh("slow", "pv", g, l // 2)
                                if l == 0:
                                    pe.wait_ge(*at("vt_s", g, len(VT_JOBS[g]) - 1))
                            o = pv_bank[0][0:DK, (l % 2) * 256:(l % 2) * 256 + 256]
                            pe.wait_ge(*at("pt_s", g, l))
                            for blk in range(2):
                                i = mm(o, vt[:, g * GB + l + blk], pt[:, l % 3, blk * 256:(blk + 1) * 256],
                                       start=blk == 0, stop=blk == 1)
                            i.then_inc(*step("pv", g, l))
                        for l in range(GB + 4):
                            if l < GB:
                                score(l)
                            if 2 <= l < GB + 2:
                                turned(l - 2)
                            if l >= 4:
                                value(l - 4)
                        pe.wait_ge(*at("xk", g))
                        mm(fresh("quick", "r2", g)[:], W2["wr"], xr[:]).then_inc(*step("r2", g))
                        mm(fresh("quick", "k2", g)[:], W2["wk"], xk[:]).then_inc(*step("k2", g))
                        o = fresh("slow", "s", 2, g)
                        pe.wait_ge(*at("yt", g, GB // 2 - 1))
                        for j in range(4):
                            i = mm(o[:], W2["wo"][:, cs(j)], yt[:, j], start=j == 0, stop=j == 3)
                        i.then_inc(*step("s", 2, g))
                        o = fresh("quick", "v2", g)
                        pe.wait_ge(*at("kr", g))
                        mm(o[:], W2["wv"], kr[:]).then_inc(*step("v2", g))

                    def layer3(g):
                        norm(3, g)
                        variance(3, g)
                        xg = xn[3][:, gs(g)]
                        pe.wait_ge(*at("xn", 3, g))
                        mm(fresh("quick", "qk3", g)[:], W3["wqk"], xg).then_inc(*step("qk3", g))
                        o = fresh("quick", "v3", g)
                        for c in range(C):
                            i = mm(o[:, c * DK:(c + 1) * DK], xg[:, cs(c)], W3["wv"])
                        i.then_inc(*step("v3", g))
                        o = fresh("quick", "rt3", g)
                        for c in range(C):
                            i = mm(o[:, c * E3:(c + 1) * E3], xg[:, cs(c)], W3["rw"])
                        i.then_inc(*step("rt3", g))

                        def score(c):
                            n = g * C + c
                            halves = (n + 4) // 4
                            pe.wait_ge(*at("k3", g))
                            for k in range(halves):
                                keys = min(GT, (n + 1) * CT - k * GT)
                                o = fresh("quick", "s3", n, k)
                                last = k == halves - 1
                                i = mm(o[:, 0:keys], q3[:, n * CT:(n + 1) * CT], k3[:, k * GT:k * GT + keys],
                                       stop=not last)
                                if last:
                                    i = mm(o[:, keys - CT:keys], identb[:], above[:], start=False)
                                i.then_inc(*step("s3", n, k))

                        def values(c):
                            n = g * C + c
                            halves = (n + 4) // 4
                            for k in range(halves):
                                kc = min(4, n + 1 - 4 * k)
                                o = fresh("quick", "pt3", n, k)
                                if k == 0:
                                    pe.wait_ge(*at("p3", n))
                                for j in range(kc):
                                    i = nc.tensor.transpose(o[:, cs(j)], p3b[:, n % 2, k * GT + j * CT:
                                                                             k * GT + (j + 1) * CT], ident[:])
                                i.then_inc(*step("pt3", n, k))
                            for k in range(halves):
                                kc = min(4, n + 1 - 4 * k)
                                pe.wait_ge(*at("pt3_s", n, k))
                                for j in range(kc):
                                    i = mm(ob[0:DK, cs(c)], v3[:, 4 * k + j], pt3[:, k, j], start=k == 0 and j == 0,
                                           stop=4 * k + j == n)
                                i.then_inc(*step("o3", n, k))
                        ob = fresh("slow", "o3", g)
                        for c in range(C + 1):
                            if c < C:
                                score(c)
                            if c >= 1:
                                values(c - 1)
                        o = fresh("quick", "ct3", g)
                        ct_out = o[0:48].bitcast(BF16)
                        pe.wait_ge(*at("cb3", g))
                        for c in range(C):
                            i = nc.tensor.transpose(ct_out[:, cs(c)], cb3[:, g * C + c], identb[:])
                        i.then_inc(*step("ct3", g))
                        ff = fresh("slow", "ff", 3, g)

                        def first(k):
                            wg_, wu_ = ((W3["shg"], W3["shu"]) if k == EP3 else
                                        (W3["gate"][:, cs(k)], W3["up"][:, cs(k)]))
                            mm(fresh("quick", "gate3", g, k)[:], wg_, xg).then_inc(*step("gate3", g, k))
                            mm(fresh("quick", "up3", g, k)[:], wu_, xg).then_inc(*step("up3", g, k))
                            if k < EP3:
                                o = fresh("slow", "cb3", g, k)
                                if k == 0:
                                    pe.wait_ge(*at("ct3_s", g))
                                mm(o[:], sel_p[:, k], ct3[:, g]).then_inc(*step("cbb3", g, k))

                        def second(k):
                            pe.wait_ge(*at("hh3", g, k))
                            w = W3["shd"] if k == EP3 else W3["down"][:, cs(k)]
                            i = mm(ff[:], w, hh3[:, k % 3], start=k == 0, stop=k == EP3)
                            i.then_inc(*(step("ff", 3, g) if k == EP3 else step("dn3", g, k)))
                        for k in range(EP3 + 2):
                            if k <= EP3:
                                first(k)
                            if k >= 1:
                                second(k - 1)
                        o = fresh("slow", "s", 3, g)
                        pe.wait_ge(*at("o3_s", g))
                        mm(o[:], w_out3[:], o3[:, g]).then_inc(*step("s", 3, g))

                    for g in range(G):
                        layer0(g)
                    now[0] = 1
                    for g in range(G):
                        layer1(g)
                    now[0] = 2
                    for g in range(G):
                        layer2_rec(g)
                        layer2_att(g)
                    now[0] = 3
                    for g in range(G):
                        layer3(g)

                def psum(*job):
                    return bank[known.get(job + ("bank",), 0)]

                @block.scalar
                def _(act):
                    now = [0]

                    def step(*m):
                        return prog["scalar", now[0]].step(*m)

                    def after(*needs):
                        s = prog["scalar", now[0]]
                        if s.count:
                            act.wait_ge(s.sem, s.count)
                        for m in needs:
                            act.wait_ge(*at(*m))

                    def fn(o, i, f, bias=0.0, scale=1.0, **kw):
                        return nc.scalar.activation(o, i, f, bias=bias, scale=scale, **kw)

                    def rsqrt(l, g, eps, name):
                        after((name, l, g))
                        fn(rs[:, g], psum(name, l, g)[:], ACT.Ln, bias=eps).then_inc(*step(name, l, g, "read"))
                        after()
                        fn(rs[:, g], rs[:, g], ACT.Exp, scale=-0.5).then_inc(*step("rs", name, l, g))

                    def norm(l, g):
                        after(("xc", l, g), *([("xn", l - 1, g)] if l else []))
                        fn(sq[:, g], psum("xc", l, g)[:], ACT.Square).then_inc(*step("sq", "var", l, g))
                        rsqrt(l, g, 1e-5, "var")

                    def gate(l, g, src, bias, *needs):
                        after(*needs, *([("x", l + 1, 0) if l < 3 else ("x out", 0)] if g else []))
                        fn(tz[:], src, ACT.Tanh, scale=0.5, bias=bias).then_inc(*step("tz", l, g))

                    def layer0(g):
                        norm(0, g)
                        after(("qk0", g))
                        qk = psum("qk0", g)[0:2 * DM]
                        fn(ek[:], qk, ACT.Relu, scale=-1.0).then_inc(*step())
                        after()
                        fn(ek[:], ek[:], ACT.Exp, scale=-1.0).then_inc(*step("ek", g))
                        after(("kvg0", g))
                        kv = psum("kvg0", g)[:, 0:C * KVG].rearrange("p (c k) -> p c k", k=KVG)
                        fn(vtok0[:, g * C:(g + 1) * C, 0:DM], kv[:, :, DM:2 * DM], ACT.Copy).then_inc(
                            *step("vtok0", g))
                        fn(et[:], kv[:, :, 0:DM], ACT.Relu, scale=-1.0).then_inc(*step())
                        after()
                        fn(et[:], et[:], ACT.Exp, scale=-1.0).then_inc(*step("et", g))
                        after(("gdiff", g))
                        fn(gw[:, g * C:(g + 1) * C, 1], gw[:, g * C:(g + 1) * C, 0], ACT.Exp).then_inc(
                            *step("gexp", g))
                        gate(0, g, psum("ff", 0, g)[:], half0[:], ("ff", 0, g))

                    def layer1(g):
                        norm(1, g)
                        after(("xn", 1, g))
                        fn(sq[:, g], xn[1][:, gs(g)], ACT.Square).then_inc(*step("sq", "rms", 1, g))
                        for j in range(4):
                            after(("xr", g, j), *([("xi", g, j - 2)] if j >= 2 else []))
                            fn(tx[:, j % 2], psum("xr", g, j)[:], ACT.Tanh, scale=0.5,
                               bias=half1[:, j:j + 1]).then_inc(*step("tx", g, j))
                        rsqrt(1, g, 1e-8, "rms")
                        after(("rt1", g))
                        fn(pr[:, g * C:(g + 1) * C], psum("rt1", g)[:, 0:C * E1].rearrange(
                            "p (c k) -> p c k", k=E1), ACT.Exp, scale=-1.0).then_inc(*step("rt1", g, "read"))
                        after(("dt", g))
                        fn(dab[:], psum("dt", g)[:], ACT.Abs, bias=W1["bdt"]).then_inc(*step())
                        after()
                        fn(dab[:], dab[:], ACT.Exp, scale=-1.0).then_inc(*step())
                        after()
                        fn(dab[:], dab[:], ACT.Ln, bias=1.0).then_inc(*step("dab", g))
                        after(("bx", g))
                        fn(bx[:, gs(g)], psum("bx", g)[0:ST], ACT.Identity, bias=S1["bxp"]).then_inc(
                            *step("bx", g, "read"))
                        fn(xd[:], xn[1][:, gs(g)], ACT.Identity, bias=W1["bout"], scale=W1["dskip"]).then_inc(
                            *step("xd", g))

                        def relus(e):
                            for j in range(1, HJ, 2):
                                needs = [("h1", g, e, j)]
                                if e >= 2:
                                    needs.append(("eo", g, e - 2))
                                elif g == 1:
                                    needs.append(("eo", 0, E1 - 1 + (1 if e % 2 == 0 else 0)))
                                after(*needs)
                                bias = W1["sb1"][:, j:j + 1] if e == E1 else W1["eb1"][:, e * HJ + j:e * HJ + j + 1]
                                fn(hid[:, e % 2, j], psum("h1", g, e, j)[:], ACT.Relu, bias=bias).then_inc(
                                    *step("hid", g, e, j))
                                reached[("h1", g, e, j, "read")] = reached[("hid", g, e, j)]
                        relus(0)
                        after(("cbt", g))
                        fn(cbt1[:, g], psum("cbt", g)[0:E1], ACT.Copy).then_inc(*step("cbt_s", g))
                        reached[("cbt", g, "read")] = reached[("cbt_s", g)]
                        relus(1)
                        after(("md", g))
                        fn(decay[:, gs(g)], psum("md", g)[0:ST], ACT.Exp, scale=neg_a[:]).then_inc(
                            *step("decay", g))
                        reached[("md", g, "read")] = reached[("decay", g)]
                        relus(2)
                        after(("ss", g))
                        fn(ssum[:], psum("ss", g)[:], ACT.Copy).then_inc(*step("ssum", g))
                        reached[("ss", g, "read")] = reached[("ssum", g)]
                        for e in range(3, E1 + 1):
                            relus(e)
                        gate(1, g, psum("ff", 1, g)[:], half1[:, 4:5], ("ff", 1, g))

                    def layer2_rec(g):
                        norm(2, g)
                        after(("gt", g), ("x", 2, 1), *([("g3", 0)] if g else []))
                        fn(gfm[:, 0], psum("gt", g)[0:32], ACT.Exp, scale=-1.0, bias=neg_bg[:]).then_inc(
                            *step("gt", g, "read"))
                        for j in range(4):
                            after(("q2", g, j), *([("s2", 0, GB - 1)] if g else []))
                            for half in range(2):
                                fn(qf[:, :, 2 * j + half], psum("q2", g, j)[half * 64:half * 64 + 64].rearrange(
                                    "p (l q) -> p l q", q=L), ACT.Copy, scale=DK ** -0.5).then_inc(*step("qf", g, j))
                            reached[("q2", g, j, "read")] = reached[("qf", g, j)]
                        for e in range(NE):
                            after(("ga", g, e), *([("rec", 0, NE - 1)] if g else []))
                            fn(abc[:, e, :, 1:L + 1],
                               psum("ga", g, e)[:].rearrange("p (l c) -> p l c", c=L), ACT.Relu, scale=-1.0,
                               bias=1.0).then_inc(*step("abc", g, e))
                            reached[("ga", g, e, "read")] = reached[("abc", g, e)]
                        for e in range(NE):
                            after(("gkv", g, e * NH + NH - 1))
                            fn(rec[:, 1 + g * GB:1 + (g + 1) * GB, 1:L + 1, e],
                               psum("gkv", g, e)[:].rearrange("p (l c) -> p l c", c=L), ACT.Copy).then_inc(
                                *step("gkv_s", g, e))
                            reached[("gkv", g, e, "read")] = reached[("gkv_s", g, e)]

                    def layer2_att(g):
                        for n, blocks in enumerate(VT_JOBS[g]):
                            after(("vt", g, n), *([("pv", 0, GB - 1)] if g else []))
                            k = len(blocks)
                            fn(vt[:, blocks[0]:blocks[0] + k], psum("vt", g, n)[:, 0:k * DK].rearrange(
                                "p (a b) -> p a b", b=DK), ACT.Copy).then_inc(*step("vt_s", g, n))
                            reached[("vt", g, n, "read")] = reached[("vt_s", g, n)]

                        def probs(l):
                            needs = [("mx2", g, l)]
                            if l >= 3:
                                needs.append(("pt", g, l - 3))
                            elif g == 1:
                                needs.append(("pt", 0, GB - 1))
                            after(*needs)
                            for hg in range(2):
                                fn(prob[:, l % 3, hg], psum("s2", g, l)[:, hg * 256:hg * 256 + 256], ACT.Exp,
                                   bias=smx[:, l % 3, hg:hg + 1],
                                   accum_out=smx[:, l % 3, 2 + hg:3 + hg]).then_inc(*step("e2", g, l))
                            reached[("s2", g, l, "read")] = reached[("e2", g, l)]

                        def turned(l):
                            needs = [("pt", g, l)]
                            if l >= 3:
                                needs.append(("pv", g, l - 3))
                            elif g == 1:
                                needs.append(("pv", 0, GB - 1))
                            after(*needs)
                            fn(pt[:, l % 3], psum("pt", g, l)[:], ACT.Copy).then_inc(*step("pt_s", g, l))
                            reached[("pt", g, l, "read")] = reached[("pt_s", g, l)]
                        for l in range(GB + 3):
                            if l < GB:
                                probs(l)
                            if l >= 3:
                                turned(l - 3)
                        after(("r2", g))
                        fn(tr[:], psum("r2", g)[:], ACT.Tanh, scale=0.5).then_inc(*step("r2", g, "read"))
                        after(("k2", g))
                        fn(kr[:], psum("k2", g)[:], ACT.Relu).then_inc(*step("k2", g, "read"))
                        after()
                        fn(kr[:], kr[:], ACT.Square).then_inc(*step("kr", g))
                        gate(2, g, of[:], 0.0, ("of", g))

                    def layer3(g):
                        norm(3, g)
                        after(("qk3", g), ("x", 3, 1))
                        fn(q3[:, gs(g)], psum("qk3", g)[0:DK], ACT.Copy, scale=DK ** -0.5).then_inc(*step())
                        fn(k3[:, gs(g)], psum("qk3", g)[DK:P], ACT.Copy).then_inc(*step("k3", g))
                        reached[("qk3", g, "read")] = reached[("k3", g)]
                        after(("v3", g))
                        fn(v3[:, g * C:(g + 1) * C], psum("v3", g)[:, 0:C * DK].rearrange(
                            "p (c k) -> p c k", k=DK), ACT.Copy).then_inc(*step("v3_s", g))
                        reached[("v3", g, "read")] = reached[("v3_s", g)]
                        after(("gdiff3", g))
                        fn(w3s[:, g * C:(g + 1) * C, 1], w3s[:, g * C:(g + 1) * C, 0], ACT.Exp).then_inc(
                            *step("gexp3", g))

                        def probs(c):
                            n = g * C + c
                            halves = (n + 4) // 4
                            needs = [("mx3", n)]
                            if n >= 2:
                                needs.append(("pt3", n - 2, (n + 2) // 4 - 1))
                            after(*needs)
                            for k in range(halves):
                                keys = min(GT, (n + 1) * CT - k * GT)
                                fn(p3b[:, n % 2, k * GT:k * GT + keys], psum("s3", n, k)[:, 0:keys], ACT.Exp,
                                   bias=sm3[:, n, 0:1], accum_out=sm3[:, n, 1 + k:2 + k]).then_inc(
                                    *step("e3", n, k))
                                reached[("s3", n, k, "read")] = reached[("e3", n, k)]

                        def turned(c):
                            n = g * C + c
                            halves = (n + 4) // 4
                            for k in range(halves):
                                kc = min(4, n + 1 - 4 * k)
                                after(("pt3", n, k), *([("o3", n - 1, (n + 3) // 4 - 1)] if n else []))
                                fn(pt3[:, k, 0:kc], psum("pt3", n, k)[:, 0:kc * CT].rearrange(
                                    "p (a b) -> p a b", b=CT), ACT.Copy).then_inc(*step("pt3_s", n, k))
                                reached[("pt3", n, k, "read")] = reached[("pt3_s", n, k)]
                        for c in range(C + 1):
                            if c < C:
                                probs(c)
                            if c >= 1:
                                turned(c - 1)
                        after(("o3", g * C + C - 1, (g * C + C + 3) // 4 - 1))
                        fn(o3[:, g], psum("o3", g)[0:DK], ACT.Copy).then_inc(*step("o3_s", g))
                        reached[("o3", g, "read")] = reached[("o3_s", g)]
                        after(("ct3", g))
                        fn(ct3[:, g], psum("ct3", g)[0:48].bitcast(BF16)[:, 0:GT], ACT.Copy).then_inc(
                            *step("ct3_s", g))
                        reached[("ct3", g, "read")] = reached[("ct3_s", g)]
                        for k in range(EP3 + 1):
                            needs = [("gate3", g, k)]
                            if k >= 2:
                                needs.append(("hg3", g, k - 2))
                            elif g:
                                needs.append(("hg3", 0, EP3))
                            after(*needs)
                            fn(tg3[:, k % 2], psum("gate3", g, k)[:], ACT.Tanh, scale=0.5).then_inc(
                                *step("tg3", g, k))
                        gate(3, g, psum("ff", 3, g)[:], 0.0, ("ff", 3, g))

                    for g in range(G):
                        layer0(g)
                    now[0] = 1
                    for g in range(G):
                        layer1(g)
                    now[0] = 2
                    for g in range(G):
                        layer2_rec(g)
                        layer2_att(g)
                    now[0] = 3
                    for g in range(G):
                        layer3(g)

                @block.vector
                def _(dve):
                    now = [0]
                    v = nc.vector

                    def step(*m):
                        return prog["vector", now[0]].step(*m)

                    def after(*needs):
                        s = prog["vector", now[0]]
                        if s.count:
                            dve.wait_ge(s.sem, s.count)
                        for m in needs:
                            dve.wait_ge(*at(*m))

                    def norm(l, g):
                        after(("rs", "var", l, g), *([("x", l, g)] if l else []))
                        v.tensor_tensor(xn[l][:, gs(g)], psum("xc", l, g)[:], rs[:, g], ALU.mult).then_inc(
                            *step("xn", l, g))
                        reached[("xc", l, g, "read")] = reached[("xn", l, g)]

                    def merge(l, g, gate_src, gate_bias, s_src, s_bias, free_gate, free_s, *needs):
                        after(("tz", l, g), *needs)
                        v.tensor_scalar(hz[:], gate_src, gate_bias, 0.5, ALU.add, ALU.mult).then_inc(*step())
                        after()
                        v.scalar_tensor_tensor(hz[:], tz[:], 1.0, hz[:], ALU.add, ALU.mult).then_inc(
                            *step(*(("ff", l, g, "read") if free_gate else ())))
                        after(("s", l, g))
                        v.scalar_tensor_tensor(hz[:], s_src, s_bias, hz[:], ALU.add, ALU.mult).then_inc(
                            *step(*(("s", l, g, "read") if free_s else ())))
                        after()
                        v.tensor_tensor(x[:, gs(g)], x[:, gs(g)], hz[:], ALU.add).then_inc(
                            *step(*(("x", l + 1, g) if l < 3 else ("x out", g))))

                    def layer0(g):
                        norm(0, g)
                        cc = slice(g * C, (g + 1) * C)
                        qk = psum("qk0", g)
                        kv = psum("kvg0", g)[:, 0:C * KVG].rearrange("p (c k) -> p c k", k=KVG)
                        after(("ek", g))
                        v.scalar_tensor_tensor(sgq[:, gs(g)], qk[0:DM], 0.0, ek[0:DM], ALU.max,
                                               ALU.add).then_inc(*step())
                        v.scalar_tensor_tensor(sgk[:, gs(g)], qk[DM:2 * DM], 0.0, ek[DM:2 * DM], ALU.max,
                                               ALU.add).then_inc(*step("sgk", g))
                        reached[("qk0", g, "read")] = reached[("sgk", g)]
                        after(("kvg0", g), ("et", g))
                        v.tensor_copy(logit[:, cc, 0:NGATE], kv[:, :, 2 * DM:KVG]).then_inc(*step())
                        v.scalar_tensor_tensor(ktok[:, cc], kv[:, :, 0:DM], 0.0, et[:], ALU.max,
                                               ALU.add).then_inc(*step("ktok0", g))
                        reached[("kvg0", g, "read")] = reached[("ktok0", g)]
                        after()
                        for c in range(g * C, (g + 1) * C):
                            v.max(top[:, c], logit[:, c]).then_inc(*step())
                        after()
                        v.tensor_tensor(gw[:, cc, 0], top[:, cc, 1], top[:, cc, 0], ALU.subtract).then_inc(
                            *step("gdiff", g))
                        after(("gexp", g))
                        v.tensor_scalar(gw[:, cc, 2], gw[:, cc, 1], 1.0, None, ALU.add).then_inc(*step())
                        after()
                        v.reciprocal(gw[:, cc, 3], gw[:, cc, 2]).then_inc(*step())
                        after()
                        v.tensor_tensor(gw[:, cc, 4], gw[:, cc, 1], gw[:, cc, 3], ALU.mult).then_inc(*step())
                        after()
                        v.tensor_tensor(gw[:, cc, 5], gw[:, cc, 4], gw[:, cc, 3], ALU.add).then_inc(*step())
                        after(("y0", g))
                        v.tensor_tensor(ysc[:], psum("y0", g)[:].rearrange("p (c k) -> p c k", k=P),
                                        gw[:, cc, 5:6].to_broadcast([P, C, P]), ALU.mult).then_inc(*step("ysc", g))
                        reached[("y0", g, "read")] = reached[("ysc", g)]
                        for c in range(C):
                            n = g * C + c
                            after(("kv0", g))
                            v.tensor_tensor(state[:, n + 1], state[:, n], psum("kv0", g)[0:DM, c * 64:c * 64 + 64],
                                            ALU.add).then_inc(*step("state", g))
                        reached[("kv0", g, "read")] = reached[("state", g)]
                        after(("a0", g))
                        v.tensor_tensor(att[:], psum("a0", g)[:].rearrange("p (c k) -> p c k", k=P),
                                        causal[:].rearrange("p (a k) -> p a k", a=1).to_broadcast([P, C, P]),
                                        ALU.mult).then_inc(*step("att0", g))
                        reached[("a0", g, "read")] = reached[("att0", g)]
                        after(("ret0", g))
                        r = psum("ret0", g)
                        v.tensor_scalar(rn[:], r[DM:2 * DM], EPS_MEM, None, ALU.max).then_inc(*step())
                        after()
                        v.reciprocal(rn[:], rn[:]).then_inc(*step())
                        after()
                        v.scalar_tensor_tensor(comb0[:], r[0:DM], flag[:, 0:1], rn[:], ALU.mult,
                                               ALU.mult).then_inc(*step("ret0", g, "read"))
                        after(("num0", g))
                        r = psum("num0", g)
                        v.tensor_scalar(rd[:], r[DM:2 * DM], EPS_MEM, None, ALU.max).then_inc(*step())
                        after()
                        v.reciprocal(rd[:], rd[:]).then_inc(*step())
                        after()
                        v.scalar_tensor_tensor(c2[:], r[0:DM], flag[:, 1:2], rd[:], ALU.mult,
                                               ALU.mult).then_inc(*step("num0", g, "read"))
                        after()
                        v.tensor_tensor(comb0[:], comb0[:], c2[:], ALU.add).then_inc(*step("comb0", g))
                        merge(0, g, psum("ff", 0, g)[:], W0["bias"], psum("s", 0, g)[:], 0.0, True, True, ("ff", 0, g))

                    def top2(g, scores, tops, idx, idf, n):
                        after()
                        for c in range(g * C, (g + 1) * C):
                            v.max(tops[:, c], scores[:, c]).then_inc(*step())
                        after()
                        for c in range(g * C, (g + 1) * C):
                            v.max_index(idx[:, c], tops[:, c], scores[:, c]).then_inc(*step())
                        after()
                        cc = slice(g * C, (g + 1) * C)
                        v.tensor_copy(idf[:, cc], idx[:, cc]).then_inc(*step())

                    def combination(g, idf, w1, w2, oh, cm, n, *name):
                        cc = slice(g * C, (g + 1) * C)
                        io = iota8[:, 0:n].rearrange("p (a k) -> p a k", a=1).to_broadcast([P, C, n])
                        after()
                        for k in range(2):
                            v.tensor_tensor(oh[:, k, cc], io, idf[:, cc, k:k + 1].to_broadcast([P, C, n]),
                                            ALU.is_equal).then_inc(*step())
                        after()
                        for k, w in ((0, w1), (1, w2)):
                            v.tensor_tensor(oh[:, k, cc], oh[:, k, cc], w.to_broadcast([P, C, n]),
                                            ALU.mult).then_inc(*step())
                        after()
                        v.tensor_tensor(cm[:, cc], oh[:, 0, cc], oh[:, 1, cc], ALU.add).then_inc(*step(*name))

                    def layer1(g):
                        norm(1, g)
                        for j in range(4):
                            after(("tx", g, j), *([("zp", 0)] if g and j >= 2 else []))
                            v.tensor_scalar(hx[:, j % 2], psum("xr", g, j)[:], W1["bin"][:, j:j + 1], 0.5, ALU.add,
                                            ALU.mult).then_inc(*step())
                            after()
                            dst = xi[:, j, gs(g)] if j < 2 else sr[:, j - 2]
                            v.scalar_tensor_tensor(dst, tx[:, j % 2], 1.0, hx[:, j % 2], ALU.add, ALU.mult).then_inc(
                                *step("xi", g, j))
                            reached[("xr", g, j, "read")] = reached[("xi", g, j)]
                        after(("rs", "rms", 1, g))
                        v.scalar_tensor_tensor(nm[:, gs(g)], xn[1][:, gs(g)], W1["wn"], rs[:, g], ALU.mult,
                                               ALU.mult).then_inc(*step("nm", g))
                        cc = slice(g * C, (g + 1) * C)
                        after(("rt1", g, "read"))
                        v.tensor_scalar(pr[:, cc], pr[:, cc], 1.0, None, ALU.add).then_inc(*step())
                        after()
                        v.reciprocal(pr[:, cc], pr[:, cc]).then_inc(*step())
                        top2(g, pr, top1, idx1, idf1, E1)
                        v.scalar_tensor_tensor(wsm1[:, cc, 0], top1[:, cc, 0], 1e-6, top1[:, cc, 1], ALU.add,
                                               ALU.add).then_inc(*step())
                        after()
                        v.reciprocal(wsm1[:, cc, 1], wsm1[:, cc, 0]).then_inc(*step())
                        after()
                        for k in range(2):
                            v.tensor_tensor(wsm1[:, cc, 2 + k], top1[:, cc, k], wsm1[:, cc, 1], ALU.mult).then_inc(
                                *step())
                        combination(g, idf1, wsm1[:, cc, 2:3], wsm1[:, cc, 3:4], oh1, cmb1, E1, "cmb1", g)
                        after(("dab", g))
                        v.tensor_scalar(dpos[:], psum("dt", g)[:], W1["bdt"], 0.0, ALU.add, ALU.max).then_inc(
                            *step())
                        after()
                        v.tensor_tensor(dab[:], dab[:], dpos[:], ALU.add).then_inc(*step("delta", g))
                        reached[("dt", g, "read")] = reached[("delta", g)]

                        def relus(e):
                            for j in range(0, HJ, 2):
                                needs = [("h1", g, e, j)]
                                if e >= 2:
                                    needs.append(("eo", g, e - 2))
                                elif g == 1:
                                    needs.append(("eo", 0, E1 - 1 + (1 if e % 2 == 0 else 0)))
                                after(*needs)
                                bias = W1["sb1"][:, j:j + 1] if e == E1 else W1["eb1"][:, e * HJ + j:e * HJ + j + 1]
                                v.tensor_scalar(hid[:, e % 2, j], psum("h1", g, e, j)[:], bias, 0.0, ALU.add,
                                                ALU.max).then_inc(*step("hid", g, e, j))
                                reached[("h1", g, e, j, "read")] = reached[("hid", g, e, j)]

                        def weigh(e):
                            after(("eo", g, e))
                            for c in range(C):
                                w = cmb1[:, g * C + c, e:e + 1]
                                src = psum("eo", g, e)[:, cs(c)]
                                if e == 0:
                                    i = v.tensor_scalar(acc[:, c], src, w, None, ALU.mult)
                                else:
                                    i = v.scalar_tensor_tensor(acc[:, c], src, w, acc[:, c], ALU.mult, ALU.add)
                                i.then_inc(*step("acc", g, e))
                            reached[("eo", g, e, "read")] = reached[("acc", g, e)]
                        relus(0)
                        relus(1)
                        after(("decay", g), ("bx", g, "read"))
                        v.tensor_tensor_scan(states[:, gs(g)], decay[:, gs(g)], bx[:, gs(g)],
                                             states[:, g * GT - 1:g * GT] if g else 0.0, ALU.mult,
                                             ALU.add).then_inc(*step("states", g))
                        weigh(0)
                        relus(2)
                        weigh(1)
                        after(("wo1", g), ("ssum", g))
                        v.tensor_tensor(s1out[:], psum("wo1", g)[:], ssum[:], ALU.mult).then_inc(
                            *step("wo1", g, "read"))
                        after(("xd", g))
                        v.tensor_tensor(s1out[:], s1out[:], xd[:], ALU.add).then_inc(*step("s", 1, g))
                        relus(3)
                        for e in range(4, E1 + 1):
                            weigh(e - 2)
                            relus(e)
                        weigh(E1 - 1)
                        merge(1, g, psum("ff", 1, g)[:], W1["sb2"], s1out[:], 0.0, True, False, ("ff", 1, g))

                    def chains():
                        after(("s", 1, 1))
                        init = W2["init"].rearrange("p (l e) -> p l e", e=NE)
                        v.tensor_copy(rec[:, 0, 1:L + 1], init).then_inc(*step())
                        v.tensor_copy(rec[:, 1:NB + 1, 0], init).then_inc(*step())
                        v.memset(rec[:, 0, 0], 0.0).then_inc(*step())
                        v.memset(abc[:, :, :, 0:1], 0.0).then_inc(*step("chains"))

                    def layer2_rec(g):
                        norm(2, g)
                        if g == 0:
                            chains()
                        after(("gt", g, "read"))
                        q = gfm[:]
                        v.tensor_scalar(q[:, 0], q[:, 0], 1.0, None, ALU.add).then_inc(*step())
                        after()
                        v.reciprocal(q[:, 1], q[:, 0]).then_inc(*step())
                        after()
                        v.tensor_copy(gb[:, 0], q[:, 1]).then_inc(*step())
                        if g:
                            dve.wait_ge(*at("gkv", 0, NE * NH - 1))
                        v.tensor_copy(g3[0:32], q[:, 1]).then_inc(*step())
                        after()
                        v.tensor_tensor(q[:, 2], q[:, 1], gb[:, 0], ALU.subtract).then_inc(*step())
                        after()
                        v.tensor_copy(gb[:, 1], q[:, 2]).then_inc(*step())
                        v.tensor_copy(g3[32:64], q[:, 2]).then_inc(*step())
                        after()
                        v.tensor_tensor(g3[64:96], q[:, 2], gb[:, 1], ALU.subtract).then_inc(*step("g3", g))
                        for n in range(NE * NH):
                            needs = [("gb", g, n)]
                            if n >= 3:
                                needs.append(("gkv", g, n - 3))
                            elif g:
                                needs.append(("gkv", 0, NE * NH - 1))
                            after(*needs)
                            v.tensor_tensor(xs[:, n % 3], psum("gb", g, n)[:], xn[2][:, gs(g)], ALU.mult).then_inc(
                                *step("xs", g, n))
                            reached[("gb", g, n, "read")] = reached[("xs", g, n)]
                            if n % NH == NH - 1 and n // NH >= 1:
                                scan(g, n // NH - 1)
                        scan(g, NE - 1)

                    def scan(g, e):
                        after(("gkv_s", g, e), ("abc", g, e))
                        r = rec[:, 1 + g * GB:1 + (g + 1) * GB].rearrange("p l c e -> p (l c) e")[:, :, e]
                        a = abc[:, e].rearrange("p l c -> p (l c)")
                        v.tensor_tensor_scan(r, a, r, 0.0, ALU.mult, ALU.add).then_inc(*step("rec", g, e))

                    def layer2_att(g):
                        def maxima(l):
                            needs = [("s2", g, l)]
                            after(*needs)
                            v.tensor_reduce(smx[:, l % 3, 0:2], psum("s2", g, l)[:].rearrange(
                                "p (a b) -> p a b", a=2), AX.X, ALU.max, negate=True).then_inc(*step("mx2", g, l))

                        def sums(l):
                            after(("e2", g, l))
                            v.reciprocal(smx[:, l % 3, 4:6], smx[:, l % 3, 2:4]).then_inc(*step("rc2", g, l))
                            after()
                            v.tensor_tensor(prob[:, l % 3], prob[:, l % 3],
                                            smx[:, l % 3, 4:6].rearrange("p (a b) -> p a b", b=1).to_broadcast(
                                                [P, 2, 4 * 2 * L]), ALU.mult).then_inc(*step("prob", g, l))

                        def out_rows(l2):
                            after(("pv", g, 2 * l2 + 1))
                            src = psum("pv", g, l2)[0:DK].rearrange("p (l h a q) -> p l h a q", l=2, h=4, a=2)
                            for half in range(2):
                                for l in range(2):
                                    t0 = (2 * l2 + l) * L
                                    v.tensor_copy(yt[half * 64:half * 64 + 64, :, t0:t0 + L],
                                                  src[:, l, :, half]).then_inc(*step("yt", g, l2))
                            reached[("pv", g, l2, "read")] = reached[("yt", g, l2)]
                        for l in range(GB + 6):
                            if l < GB:
                                maxima(l)
                            if 1 <= l < GB + 1:
                                sums(l - 1)
                            if l >= 6 and l % 2 == 1:
                                out_rows((l - 6) // 2)
                        out_rows(GB // 2 - 1)
                        after(*([("x", 3, 0)] if g else []))
                        now_, before = xn[2][:, gs(g)], xn_a[:, g * GT:(g + 1) * GT]
                        v.tensor_tensor(dx[:], now_, before, ALU.subtract).then_inc(*step())
                        after()
                        v.scalar_tensor_tensor(xr[:], dx[:], W2["mur"], before, ALU.mult, ALU.add).then_inc(
                            *step())
                        v.scalar_tensor_tensor(xk[:], dx[:], W2["muk"], before, ALU.mult, ALU.add).then_inc(
                            *step("xk", g))
                        after(("r2", g, "read"))
                        v.tensor_scalar(tr[:], tr[:], 1.0, 0.5, ALU.add, ALU.mult).then_inc(*step())
                        after(("v2", g))
                        v.tensor_tensor(of[:], psum("v2", g)[:], tr[:], ALU.mult).then_inc(*step("of", g))
                        reached[("v2", g, "read")] = reached[("of", g)]
                        merge(2, g, of[:], 0.0, psum("s", 2, g)[:], 0.0, False, True)

                    def layer3(g):
                        norm(3, g)
                        cc = slice(g * C, (g + 1) * C)
                        after(("rt3", g), ("x", 3, 1))
                        v.tensor_tensor(lg3[:, cc], psum("rt3", g)[:, 0:C * E3].rearrange("p (c k) -> p c k", k=E3),
                                        W3["rb"].rearrange("p (a k) -> p a k", a=1).to_broadcast([P, C, E3]),
                                        ALU.add).then_inc(*step("rt3", g, "read"))
                        top2(g, lg3, top3, idx3, idf3, E3)
                        v.tensor_tensor(w3s[:, cc, 0], top3[:, cc, 1], top3[:, cc, 0], ALU.subtract).then_inc(
                            *step("gdiff3", g))
                        after(("gexp3", g))
                        v.tensor_scalar(w3s[:, cc, 0], w3s[:, cc, 1], 1.0, None, ALU.add).then_inc(*step())
                        after()
                        v.reciprocal(w3s[:, cc, 2], w3s[:, cc, 0]).then_inc(*step())
                        after()
                        v.tensor_tensor(w3s[:, cc, 3], w3s[:, cc, 1], w3s[:, cc, 2], ALU.mult).then_inc(*step())
                        combination(g, idf3, w3s[:, cc, 2:3], w3s[:, cc, 3:4], oh3, cm3, E3)
                        after()
                        v.tensor_copy(cb3[:, cc, 0:16], cm3[:, cc]).then_inc(*step())
                        after()
                        v.tensor_tensor(cr3[:, cc], cm3[:, cc], cb3[:, cc, 0:16], ALU.subtract).then_inc(*step())
                        after()
                        v.tensor_copy(cb3[:, cc, 16:32], cr3[:, cc]).then_inc(*step())
                        after()
                        v.tensor_tensor(cb3[:, cc, 32:48], cr3[:, cc], cb3[:, cc, 16:32], ALU.subtract).then_inc(
                            *step("cb3", g))

                        def maxima(c):
                            n = g * C + c
                            halves = (n + 4) // 4
                            for k in range(halves):
                                keys = min(GT, (n + 1) * CT - k * GT)
                                after(("s3", n, k))
                                i = v.tensor_reduce(sm3[:, n, 3 + k:4 + k], psum("s3", n, k)[:, 0:keys], AX.X,
                                                    ALU.max, negate=True)
                                i.then_inc(*step())
                            after()
                            if halves == 1:
                                v.tensor_copy(sm3[:, n, 0:1], sm3[:, n, 3:4]).then_inc(*step("mx3", n))
                            else:
                                v.tensor_tensor(sm3[:, n, 0:1], sm3[:, n, 3:4], sm3[:, n, 4:5], ALU.min).then_inc(
                                    *step("mx3", n))

                        def sums(c):
                            n = g * C + c
                            halves = (n + 4) // 4
                            after(("e3", n, halves - 1))
                            s = sm3[:, n, 1:2]
                            if halves == 2:
                                v.tensor_tensor(s, s, sm3[:, n, 2:3], ALU.add).then_inc(*step())
                                after()
                            v.reciprocal(sm3[:, n, 5:6], s).then_inc(*step())
                            after()
                            keys = (n + 1) * CT
                            v.tensor_scalar(p3b[:, n % 2, 0:keys], p3b[:, n % 2, 0:keys], sm3[:, n, 5:6], None,
                                            ALU.mult).then_inc(*step("p3", n))
                        for c in range(C):
                            maxima(c)
                            sums(c)
                        for k in range(EP3 + 1):
                            after(("tg3", g, k))
                            v.scalar_tensor_tensor(h3[:, k % 2], tg3[:, k % 2], 1.0, psum("gate3", g, k)[:], ALU.add,
                                                   ALU.mult).then_inc(*step("hg3", g, k))
                            reached[("gate3", g, k, "read")] = reached[("hg3", g, k)]
                            needs = [("up3", g, k)]
                            if k >= 3:
                                needs.append(("dn3", g, k - 3))
                            elif g:
                                needs.append(("ff", 3, 0))
                            after(*needs)
                            o = hh3[:, k % 3]
                            v.scalar_tensor_tensor(o, h3[:, k % 2], 0.5, psum("up3", g, k)[:], ALU.mult,
                                                   ALU.mult).then_inc(*step(*(("hh3", g, k) if k == EP3 else
                                                                              ("up3", g, k, "read"))))
                            if k == EP3:
                                reached[("up3", g, k, "read")] = reached[("hh3", g, k)]
                            else:
                                after(("cbb3", g, k))
                                v.tensor_tensor(o, o, psum("cb3", g, k)[:], ALU.mult).then_inc(*step("hh3", g, k))
                                reached[("cb3", g, k, "read")] = reached[("hh3", g, k)]
                        merge(3, g, psum("ff", 3, g)[:], 0.0, psum("s", 3, g)[:], W3["bout"], True, True,
                              ("ff", 3, g))

                    for g in range(G):
                        layer0(g)
                    now[0] = 1
                    for g in range(G):
                        layer1(g)
                    now[0] = 2
                    for g in range(G):
                        layer2_rec(g)
                        layer2_att(g)
                    now[0] = 3
                    for g in range(G):
                        layer3(g)

                @block.gpsimd
                def _(pool):
                    for g in range(G):
                        pool.wait_ge(*at("xi", g, 3))
                        pool.wait_ge(*at("bx", g))
                        nc.gpsimd.tensor_tensor(xi[:, 0, gs(g)], xi[:, 0, gs(g)], sr[:, 0], ALU.mult).then_inc(
                            *prog["gpsimd", 1].step())
                        nc.gpsimd.tensor_tensor(xi[:, 1, gs(g)], xi[:, 1, gs(g)], sr[:, 1], ALU.mult).then_inc(
                            *prog["gpsimd", 1].step("z", g))
                        reached[("zp", g)] = reached[("z", g)]

            nc.all_engine_barrier()
            for name, s in sems.items():
                if not name.startswith("once") and name != "loads":
                    nc.sync.sem_clear(s)
            nc.all_engine_barrier()
    return reached


def kernel(**inputs):
    import concourse.bacc as bacc
    from concourse.bass_utils import run_bass_kernel_spmd as run

    a = {k: np.asarray(v) for k, v in inputs.items()}

    def rows(w, p=P):
        return w.reshape(-1, p, w.shape[-1]).transpose(1, 0, 2).reshape(p, -1)

    def col(v, p=P):
        return v.reshape(-1, p).T

    def pack(pieces, spec):
        for piece, (name, n) in zip(pieces, spec):
            assert piece.shape[1] == n, (name, piece.shape, n)
        return np.concatenate(pieces, axis=1)

    p0 = pack([np.concatenate([a["L0_attn_w_q"], a["L0_attn_w_k"]]).T,
               np.concatenate([a["L0_attn_w_k"], a["L0_attn_w_v"], a["L0_ffn_W_gate"].T]).T,
               a["L0_ffn_W_shared"].T, a["L0_ffn_W_expert"].T, col(a["L0_ffn_bias"])], PACK0)
    mn = a["L0_attn_memory_norm"]
    s0 = pack([np.concatenate([a["L0_attn_memory"], np.repeat(mn[:, None], DM, 1)], 1), np.repeat(mn[None], DM, 0),
               np.repeat(a["L0_attn_gate"][None], DM, 0), a["L0_attn_w_o"].T], SMALL0)
    p1 = pack([a["L1_attn_W_in"], rows(a["L1_attn_W_dt"]), rows(a["L1_attn_W_xp"]), rows(a["L1_attn_W_out"]),
               a["L1_ffn_router_w"].T, a["L1_ffn_sw1"], rows(a["L1_ffn_sw2"]), col(a["L1_attn_b_in"]),
               col(a["L1_attn_b_dt"]), col(a["L1_attn_b_out"]), col(a["L1_attn_D"]), col(a["L1_ffn_norm_weight"]),
               col(a["L1_ffn_sb1"]), col(a["L1_ffn_sb2"]), col(a["L1_ffn_eb1"])], PACK1)
    s1 = pack([col(a["L1_attn_A_log"], ST), col(a["L1_attn_b_xp"], ST)], SMALL1)
    eb2 = a["L1_ffn_eb2"]
    ew1 = a["L1_ffn_ew1"].transpose(1, 0, 2)
    ew2 = a["L1_ffn_ew2"].reshape(E1, HJ, P, D).transpose(2, 0, 1, 3)
    wkv = np.concatenate([a["L2_attn_w_K"], a["L2_attn_w_V"]], 1).transpose(2, 0, 1).reshape(D, -1)
    init = np.concatenate([a["L2_attn_init_K_rec"], a["L2_attn_init_V_rec"]], 2).transpose(2, 1, 0).reshape(P, -1)
    p2 = pack([a["L2_attn_w_G"].reshape(NH * NE, D).T, wkv, a["L2_attn_w_Q"].reshape(NH * DK, D).T,
               rows(a["L2_attn_w_O"]), init, a["L2_ffn_W_r"].T, a["L2_ffn_W_k"].T, a["L2_ffn_W_v"].T,
               col(a["L2_ffn_mu_r"]), col(a["L2_ffn_mu_k"])], PACK2)
    bg = a["L2_attn_b_G"].reshape(NH * NE, 1)
    qkv = a["L3_attn_w_qkv"]
    p3 = pack([qkv[:2 * DK].T, qkv[2 * DK:].T, col(a["L3_attn_b_out"]), a["L3_ffn_router_w"].T,
               np.repeat(a["L3_ffn_router_bias"][None], P, 0),
               a["L3_ffn_gate_proj"].transpose(1, 0, 2).reshape(D, -1),
               a["L3_ffn_up_proj"].transpose(1, 0, 2).reshape(D, -1),
               rows(a["L3_ffn_down_proj"].reshape(E3 * H3, D)),
               a["L3_ffn_sh_gate"].T, a["L3_ffn_sh_up"].T, a["L3_ffn_sh_down"].T], PACK3)
    wout3 = a["L3_attn_w_out"].T
    x = a["L0_attn_hidden_states"].transpose(0, 2, 1)
    given = dict(x=x, p0=p0, s0=s0, p1=p1, s1=s1, eb2=eb2, ew1=ew1, ew2=ew2, p2=p2, bg=bg, p3=p3, wout3=wout3)
    given = {f"in_{k}": np.ascontiguousarray(v) for k, v in given.items()}

    def build(known):
        nc = bacc.Bacc("TRN2", target_bir_lowering=False, num_devices=1)
        args = [nc.dram_tensor(k, v.shape, F32, kind="ExternalInput").ap() for k, v in given.items()]
        args.append(nc.dram_tensor("out_x", (B, P, T), F32, kind="ExternalOutput").ap())
        return nc, four_layers(nc, known, *args)

    _, known = build({})
    nc, _ = build(known)
    r = run(nc, [given], core_ids=[0])
    return np.ascontiguousarray(r.results[0]["out_x"].transpose(0, 2, 1))
```

```python
from contextlib import ExitStack
from itertools import zip_longest

import numpy as np

import concourse.bass as bass
from concourse import mybir

ALU = mybir.AluOpType
ACT = mybir.ActivationFunctionType
AX = mybir.AxisListType
F32 = mybir.dt.float32
BF16 = mybir.dt.bfloat16
U32 = mybir.dt.uint32

B, T, D = 2, 1024, 128
P = 128
GT = 512
G = T // GT
CT = 128
C = GT // CT
DM = 32
EPS_MEM = 1e-6
NGATE = 7
KVG = 2 * DM + NGATE
ST = 64
E1, H1 = 8, 512
HJ = H1 // P
NH, NE, L, DK = 8, 4, 32, 64
NB = T // L
GB = GT // L
E3, H3 = 16, 64
EP3 = E3 // 2
NEG = -1e30
VT_JOBS = [[range(0, 8), range(8, 16), range(16, 17)], [range(17, 25), range(25, 33)]]
HID_UNDER = 4096
ROOM = 24200

PACK0 = [("wqk", 2 * DM), ("wkvg", KVG), ("wsh", D), ("wex", D), ("bias", 1)]
SMALL0 = [("mem", 2 * DM), ("mnorm", DM), ("gate", 1), ("wo", D)]
PACK1 = [("win", 512), ("wdt", 2 * D), ("wxp", 2 * ST), ("wout", 2 * D), ("rw", E1), ("sw1", H1), ("sw2", HJ * D)]
BIAS1 = [("bin", 4), ("bdt", 1), ("bout", 1), ("dskip", 1), ("wn", 1), ("sb1", HJ), ("sb2", 1), ("eb1", E1 * HJ)]
SMALL1 = [("alog", 1), ("bxp", 1)]
PACK2 = [("wg", 32), ("wkv", NH * 128), ("wq", NH * DK), ("wo", 4 * D), ("init", NE * L),
         ("wr", D), ("wk", D), ("wv", D), ("mur", 1), ("muk", 1)]
PACK3 = [("wqk", 2 * DK), ("wv", DK), ("bout", 1), ("rw", E3), ("rb", E3), ("gate", E3 * H3), ("up", E3 * H3),
         ("down", EP3 * D), ("shg", D), ("shu", D), ("shd", D)]


CONST = [("ident", P), ("center", P), ("mean", P), ("causal", P), ("ones", P), ("iota", E3)]
CONSTB = [("ident", P), ("above", P), ("sel_q", P), ("cage", NE * 2 * L), ("sel_p", EP3 * P), ("sel_e", NE),
          ("sel_he", NH * NE)]


def constants():
    k = np.arange(P)
    eye = np.eye(P, dtype=np.float32)
    c = dict(ident=eye, center=eye - np.float32(1 / D), mean=np.full((P, P), 1 / D, np.float32),
             causal=(k[:, None] <= k[None]).astype(np.float32), ones=np.ones((P, P), np.float32),
             iota=np.repeat(np.arange(E3, dtype=np.float32)[None], P, 0))
    q, key = np.arange(L), np.arange(2 * L)
    cage = np.zeros((P, 2 * L), np.float32)
    cage[:L] = np.where((key[None] > q[:, None]) & (key[None] <= q[:, None] + L), 0, NEG)
    col = np.arange(P)
    b = dict(ident=eye, above=np.where(k[None] > k[:, None], np.float32(NEG), np.float32(0)),
             sel_q=(k[:, None] == col[None] % L).astype(np.float32),
             cage=np.repeat(cage, NE, 1),
             sel_p=(k[:, None, None] % 16 == 2 * np.arange(EP3)[None, :, None] + col[None, None] // H3).reshape(P, -1),
             sel_e=k[:, None] % NE == np.arange(NE)[None],
             sel_he=k[:, None] % 32 == np.arange(32)[None])
    return (np.concatenate([c[n].astype(np.float32) for n, _ in CONST], 1),
            np.concatenate([b[n].astype(mybir.dt.np(BF16)) for n, _ in CONSTB], 1))


def columns(pack):
    at, out = 0, {}
    for name, n in pack:
        out[name] = (at, at + n)
        at += n
    return out, at


class Steps:

    def __init__(self, sem, reached):
        self.sem, self.count, self.reached = sem, 0, reached

    def step(self, *milestone, by=1):
        self.count += by
        if milestone:
            self.reached[milestone] = (self.sem.name, self.count)
        return self.sem, by


def four_layers(nc, known, x_in, cf, cb, p0, s0, p1, b1, s1, eb2, ew1, ew2, p2, bg, p3, wout3, out):
    reached = {}
    with ExitStack() as ctx:
        def sb(name, shape, dt=F32):
            return ctx.enter_context(nc.sbuf_tensor(name, shape, dt))

        sems = {}

        def sem(name):
            sems[name] = ctx.enter_context(nc.semaphore(name))
            return sems[name]

        def at(*milestone):
            name, value = known.get(milestone, ("next_x", 16))
            return sems[name], value

        def packed(tile, pack):
            where, _ = columns(pack)
            return {name: tile[:, a:b] for name, (a, b) in where.items()}

        w0t = sb("w0", [P, columns(PACK0)[1]])
        w0s = sb("w0s", [DM, columns(SMALL0)[1]])
        w1t = sb("w1", [P, columns(PACK1)[1]])
        w1b = sb("w1b", [P, columns(BIAS1)[1]])
        w1s = sb("w1s", [ST, 2])
        w_eb2 = sb("w_eb2", [E1, D])
        w_ew1 = sb("w_ew1", [P, E1, H1])
        w_ew2 = sb("w_ew2", [P, E1, HJ, D])
        w2t = sb("w2", [P, columns(PACK2)[1]])
        w_bg = sb("w_bg", [32, 1])
        w3t = sb("w3", [P, columns(PACK3)[1]])
        w_out3 = sb("w_out3", [DK, D])
        W0, S0, S1 = packed(w0t, PACK0), packed(w0s, SMALL0), packed(w1s, SMALL1)
        W1 = packed(w1t, PACK1) | packed(w1b, BIAS1)
        W2, W3 = packed(w2t, PACK2), packed(w3t, PACK3)

        const = sb("const", [P, columns(CONST)[1]])
        constb = sb("constb", [P, columns(CONSTB)[1]], BF16)
        K, KB = packed(const, CONST), packed(constb, CONSTB)
        ident = K["ident"]
        center = K["center"]
        mean = K["mean"]
        ones = K["ones"][0:ST]
        causal = K["causal"]
        iota8 = K["iota"]
        identb = KB["ident"]
        above = KB["above"]
        sel_q = KB["sel_q"][0:L]
        cage = KB["cage"][0:L]
        sel_p = KB["sel_p"][0:48].rearrange("p (a b) -> p a b", b=P)
        sel_e = KB["sel_e"][0:96]
        sel_he = KB["sel_he"][0:96]
        flag = sb("flag", [DM, 4])
        half0 = sb("half0", [P, 1])
        half1 = sb("half1", [P, 5])
        neg_a = sb("neg_a", [ST, 1])
        neg_bg = sb("neg_bg", [32, 1])

        x0 = sb("x0", [P, T])
        x = sb("x", [P, T])
        xn_a = sb("xn_a", [P, T + 1])
        xn_b = sb("xn_b", [P, T])
        xn = [xn_a[:, 1:T + 1], xn_b[:, :], xn_a[:, 1:T + 1], xn_b[:, :]]
        sq = sb("sq", [P, 2, GT])
        rs = sb("rs", [P, 2, GT])
        hz = sb("hz", [P, GT])
        tz = sb("tz", [P, GT])
        room = sb("arena", [P, ROOM])
        used, ends = [0], []

        def take(shape, parts=P, dt=F32):
            n = int(np.prod(shape))
            words = n if dt == F32 or dt == U32 else (n + 1) // 2
            v = room[0:parts, used[0]:used[0] + words]
            used[0] += words
            ends.append(used[0])
            if dt != F32:
                v = v.bitcast(dt)
            names = "abcd"[:len(shape)]
            if len(shape) == 1:
                return v
            return v.rearrange(f"p ({' '.join(names)}) -> p {' '.join(names)}", **dict(zip(names, shape)))

        used[0] = 0
        xi = take([2, T])
        sr = take([2, GT])
        hx = take([2, GT])
        tx = take([2, GT])
        dab = take([GT])
        dpos = take([GT])
        decay = take([T], ST)
        bx = take([T], ST)
        states = take([T], ST)
        ssum = take([GT])
        s1out = take([GT])
        xd = take([GT])
        nm = take([T])
        acc = take([C, P])
        pr = take([2 * C, E1])
        top1 = take([2 * C, 8])
        idx1 = take([2 * C, 8], dt=U32)
        idf1 = take([2 * C, 8])
        wsm1 = take([2 * C, 4])
        oh1 = take([2, 2 * C, E1])
        cmb1 = take([2 * C, E1])
        cbt1 = take([2, GT], E1)
        hid = take([2, HJ, GT])

        used[0] -= HID_UNDER
        ek = take([2, GT], ST)
        sgq = take([T], DM)
        sgk = take([T], DM)
        et = take([2, C, DM])
        ktok = take([2 * C, DM])
        vtok0 = sb("vtok0", [P, 2 * C, 2 * DM])
        logit = sb("logit", [P, 2 * C, 8])
        att = take([2, C, P])
        state = sb("state", [DM, 2 * C + 1, 2 * DM])
        rn = take([2, GT], DM)
        rd = take([2, GT], DM)
        comb0 = take([2, GT], DM)
        c2 = take([2, GT], DM)
        top = take([2 * C, 8])
        gw = take([2 * C, 6])
        ysc = take([2, C, P])

        used[0] = 0
        abc = take([NE, GB, L + 1])
        rec = take([NB + 1, L + 1, NE])
        vt = take([NB + 1, DK])
        qf = take([GB, NH, L], DK)
        yt = take([4, GT])
        gfm = take([3, GT], 32)
        gb = take([2, GT], 32, BF16)
        g3 = take([GT], 96, BF16)
        xs = take([3, GT])
        prob = take([3, 2, 4 * 2 * L])
        pt = take([3, GT])
        smx = take([3, 8])
        dx = take([GT])
        xr = take([GT])
        xk = take([GT])
        kr = dx
        tr = take([GT])
        of = xk

        used[0] = 0
        q3 = take([T], DK)
        k3 = take([T], DK)
        v3 = take([2 * C, DK])
        p3b = take([2, T])
        pt3 = take([2, C, P])
        sm3 = take([2 * C, 8])
        o3 = take([2, GT], DK)
        lg3 = take([2 * C, E3])
        top3 = take([2 * C, 8])
        idx3 = take([2 * C, 8], dt=U32)
        idf3 = take([2 * C, 8])
        w3s = take([2 * C, 4])
        oh3 = take([2, 2 * C, E3])
        cm3 = take([2 * C, E3])
        cb3 = take([2 * C, 48], dt=BF16)
        cr3 = take([2 * C, E3])
        ct3 = take([2, GT], 48, BF16)
        tg3 = take([2, GT])
        h3 = take([2, GT])
        hh3 = take([3, GT])

        assert max(ends) <= ROOM, ends
        bank = [ctx.enter_context(nc.psum_tensor(f"bank{i}", [P, GT], F32)) for i in range(8)]

        ready = {n: sem(f"loaded_{n}") for n in ("first", "one", "experts", "two", "three")}
        next_x, stores = sem("next_x"), sem("stores")
        once = Steps(sem("once"), reached)
        once_v, once_a = Steps(sem("once_vector"), reached), Steps(sem("once_scalar"), reached)
        prog = {(e, l): Steps(sem(f"l{l}_{e}"), reached) for l in range(4)
                for e in ("tensor", "vector", "scalar", "gpsimd")}

        def gs(g):
            return slice(g * GT, (g + 1) * GT)

        def cs(c):
            return slice(c * CT, (c + 1) * CT)

        with nc.Block() as block:
            @block.sync
            def _(sp):
                xv = x_in.rearrange("b p t -> (b p) t")
                for name, pieces in (
                        ("first", ((const[:], cf), (x0[:], xv[0:P]), (w0t[:], p0), (w0s[:], s0), (w1b[:], b1),
                                   (w1s[:], s1), (w_bg[:], bg))),
                        ("one", ((w1t[:], p1), (w_eb2[:], eb2))),
                        ("experts", ((w_ew1[:], ew1), (w_ew2[:], ew2))),
                        ("three", ((w3t[:], p3), (w_out3[:], wout3)))):
                    for dst, src in pieces:
                        sp.dma_start(dst, src).then_inc(ready[name], 16)
                sp.wait_ge(ready["first"], 16 * 7)

            @block.gpsimd
            def _(pool):
                pool.dma_start(constb[:], cb).then_inc(ready["two"], 16)
                pool.dma_start(w2t[:], p2).then_inc(ready["two"], 16)
                for tile, v in ((xn_a, 0.0), (vtok0, 1.0), (logit, -3e38), (state, 0.0)):
                    nc.gpsimd.memset(tile[:], v).then_inc(*once.step())
                pool.wait_ge(once.sem, once.count)

            @block.vector
            def _(dve):
                dve.wait_ge(ready["first"], 16 * 7)
                v = once_v

                def done():
                    dve.wait_ge(v.sem, v.count)
                nc.vector.tensor_scalar(half0[:], W0["bias"], 0.5, None, ALU.mult).then_inc(*v.step())
                nc.vector.tensor_scalar(half1[:, 0:4], W1["bin"], 0.5, None, ALU.mult).then_inc(*v.step())
                nc.vector.tensor_scalar(half1[:, 4:5], W1["sb2"], 0.5, None, ALU.mult).then_inc(*v.step())
                nc.vector.tensor_scalar(neg_bg[:], w_bg[:], -1.0, None, ALU.mult).then_inc(*v.step())
                nc.vector.tensor_reduce(flag[:, 2:3], S0["mnorm"], AX.X, ALU.add).then_inc(*v.step())
                done()
                nc.vector.tensor_scalar(flag[:, 2:3], flag[:, 2:3], EPS_MEM, None, ALU.is_ge).then_inc(*v.step())
                dve.wait_ge(once_a.sem, 1)
                nc.vector.tensor_scalar(flag[:, 3:4], flag[:, 3:4], 1.0, None, ALU.add).then_inc(*v.step())
                done()
                nc.vector.reciprocal(flag[:, 3:4], flag[:, 3:4]).then_inc(*v.step())
                done()
                nc.vector.tensor_tensor(flag[:, 0:1], flag[:, 3:4], flag[:, 2:3], ALU.mult).then_inc(*v.step())
                nc.vector.tensor_scalar(flag[:, 1:2], flag[:, 3:4], -1.0, 1.0, ALU.mult, ALU.add).then_inc(*v.step())
                dve.wait_ge(once_a.sem, 2)
                nc.vector.tensor_scalar(neg_a[:], neg_a[:], -1.0, None, ALU.mult).then_inc(*v.step())

            @block.scalar
            def _(act):
                act.wait_ge(ready["first"], 16 * 7)
                nc.scalar.activation(flag[:, 3:4], S0["gate"], ACT.Exp, scale=-1.0).then_inc(*once_a.step())
                nc.scalar.activation(neg_a[:], S1["alog"], ACT.Exp).then_inc(*once_a.step())

        with nc.Fori(0, B) as b:
            with nc.Block(no_gpsimd_drain=True) as block:

                rings = {"quick": [0, 1, 2, 3], "slow": [4, 5, 6, 7]}
                turn = {"quick": 0, "slow": 0}
                owner = {}

                @block.sync
                def _(sp):
                    xv = x_in.rearrange("b p t -> (b p) t")
                    ov = out.rearrange("b p t -> (b p) t")
                    sp.wait_ge(*at("x", 1, G - 1))
                    sp.dma_start(x0[:], xv[bass.ds((B - 1 - b) * P, P)]).then_inc(next_x, 16)
                    for g in range(G):
                        sp.wait_ge(*at("x out", g))
                        sp.dma_start(ov[bass.ds(b * P, P), gs(g)], x[:, gs(g)]).then_inc(stores, 16)
                    sp.wait_ge(stores, 16 * G)
                    sp.wait_ge(next_x, 16)

                @block.tensor
                def _(pe):
                    now = [0]
                    growing = set()

                    def step(*m):
                        growing.discard(m)
                        return prog["tensor", now[0]].step(*m)

                    def fresh(ring, *job):
                        while True:
                            i = rings[ring][turn[ring] % 4]
                            turn[ring] += 1
                            if owner.get(i) not in growing:
                                break
                        if job[0] == "ff":
                            growing.add(job)
                        if i in owner:
                            pe.wait_ge(*at(*owner[i], "read"))
                        owner[i] = job
                        reached[job + ("bank",)] = i
                        return bank[i]

                    def mm(o, lhsT, rhs, start=True, stop=True):
                        return nc.tensor.matmul(o, lhsT, rhs, start=start, stop=stop, skip_group_check=True)

                    def norm(l, g):
                        if l:
                            pe.wait_ge(*at("x", l, g))
                        src = x if l else x0
                        mm(fresh("quick", "xc", l, g)[:], center[:], src[:, gs(g)]).then_inc(*step("xc", l, g))

                    def variance(l, g, name="var"):
                        pe.wait_ge(*at("sq", name, l, g))
                        mm(fresh("quick", name, l, g)[:], mean[:], sq[:, g]).then_inc(*step(name, l, g))

                    def head(l, g):
                        norm(l, g)
                        variance(l, g)

                    def layer0(g):
                        xg = xn[0][:, gs(g)]
                        pe.wait_ge(*at("xn", 0, g))
                        o = fresh("quick", "qk0", g)
                        mm(o[0:2 * DM], W0["wqk"], xg).then_inc(*step("qk0", g))
                        o = fresh("quick", "kvg0", g)
                        for c in range(C):
                            i = mm(o[:, c * KVG:(c + 1) * KVG], xg[:, cs(c)], W0["wkvg"])
                        i.then_inc(*step("kvg0", g))
                        ff = fresh("slow", "ff", 0, g)
                        mm(ff[:], W0["wsh"], xg, stop=False)
                        o = fresh("quick", "y0", g)
                        for c in range(C):
                            i = mm(o[:, cs(c)], xg[:, cs(c)], W0["wex"])
                        i.then_inc(*step("y0", g))
                        yield
                        o = fresh("slow", "kv0", g)
                        pe.wait_ge(*at("vtok0", g))
                        pe.wait_ge(*at("ktok0", g))
                        for c in range(C):
                            i = mm(o[0:DM, c * 64:c * 64 + 64], ktok[:, g * C + c], vtok0[:, g * C + c])
                        i.then_inc(*step("kv0", g))
                        yield
                        o = fresh("quick", "a0", g)
                        pe.wait_ge(*at("sgk", g))
                        for c in range(C):
                            t = slice(g * GT + c * CT, g * GT + (c + 1) * CT)
                            i = mm(o[:, cs(c)], sgk[:, t], sgq[:, t])
                        i.then_inc(*step("a0", g))
                        o = fresh("quick", "ret0", g)
                        mm(o[0:2 * DM], S0["mem"], sgq[:, gs(g)]).then_inc(*step("ret0", g))
                        yield
                        pe.wait_ge(*at("ysc", g))
                        for c in range(C):
                            i = mm(ff[:, cs(c)], ysc[:, g, c], ident[:], start=False, stop=c == C - 1)
                        i.then_inc(*step("ff", 0, g))
                        yield
                        o = fresh("quick", "num0", g)
                        pe.wait_ge(*at("att0", g))
                        pe.wait_ge(*at("state", g))
                        for c in range(C):
                            t = slice(g * GT + c * CT, g * GT + (c + 1) * CT)
                            mm(o[0:64, cs(c)], vtok0[:, g * C + c], att[:, g, c], stop=False)
                            i = mm(o[0:64, cs(c)], state[:, g * C + c], sgq[:, t], start=False)
                        i.then_inc(*step("num0", g))
                        yield
                        o = fresh("slow", "s", 0, g)
                        pe.wait_ge(*at("comb0", g))
                        mm(o[:], S0["wo"], comb0[:, g]).then_inc(*step("s", 0, g))

                    def layer1(g):
                        xg = xn[1][:, gs(g)]
                        pe.wait_ge(*at("xn", 1, g))
                        for j in range(4):
                            mm(fresh("quick", "xr", g, j)[:], W1["win"][:, cs(j)], xg).then_inc(*step("xr", g, j))
                        variance(1, g, "rms")
                        o = fresh("quick", "dt", g)
                        pe.wait_ge(*at("xi", g, 1))
                        for j in range(2):
                            i = mm(o[:], W1["wdt"][:, cs(j)], xi[:, j, gs(g)], start=j == 0, stop=j == 1)
                        i.then_inc(*step("dt", g))
                        o = fresh("quick", "bx", g)
                        for j in range(2):
                            i = mm(o[0:ST], W1["wxp"][:, j * ST:(j + 1) * ST], xi[:, j, gs(g)], start=j == 0,
                                   stop=j == 1)
                        i.then_inc(*step("bx", g))
                        o = fresh("quick", "rt1", g)
                        pe.wait_ge(*at("nm", g))
                        for c in range(C):
                            t = slice(g * GT + c * CT, g * GT + (c + 1) * CT)
                            i = mm(o[:, c * E1:(c + 1) * E1], nm[:, t], W1["rw"])
                        i.then_inc(*step("rt1", g))
                        ff = fresh("slow", "ff", 1, g)
                        if g == 0:
                            pe.wait_ge(ready["experts"], 32)

                        def first(e):
                            for j in range(HJ):
                                w = W1["sw1"][:, cs(j)] if e == E1 else w_ew1[:, e, cs(j)]
                                mm(fresh("quick", "h1", g, e, j)[:], w, nm[:, gs(g)]).then_inc(*step("h1", g, e, j))

                        def second(e):
                            h = hid[:, e % 2]
                            if e == E1:
                                pe.wait_ge(*at("hid", g, e, 2))
                                pe.wait_ge(*at("hid", g, e, 3))
                                for j in range(HJ):
                                    i = mm(ff[:], W1["sw2"][:, cs(j)], h[:, j], start=False, stop=False)
                                i.then_inc(*step("eo", g, e))
                                return
                            o = fresh("slow", "eo", g, e)
                            pe.wait_ge(*at("hid", g, e, 2))
                            pe.wait_ge(*at("hid", g, e, 3))
                            for c in range(C):
                                for j in range(HJ):
                                    i = mm(o[:, cs(c)], h[:, j, cs(c)], w_ew2[:, e, j], start=j == 0,
                                           stop=j == HJ - 1)
                            i.then_inc(*step("eo", g, e))

                        first(0)
                        o = fresh("quick", "cbt", g)
                        pe.wait_ge(*at("cmb1", g))
                        for c in range(C):
                            i = nc.tensor.transpose(o[0:E1, cs(c)], cmb1[:, g * C + c], ident[:])
                        i.then_inc(*step("cbt", g))
                        first(1)
                        head(*((1, 1) if g == 0 else (2, 0)))
                        o = fresh("quick", "md", g)
                        pe.wait_ge(*at("delta", g))
                        mm(o[0:ST], mean[:, 0:ST], dab[:]).then_inc(*step("md", g))
                        second(0)
                        first(2)
                        o = fresh("quick", "ss", g)
                        pe.wait_ge(*at("states", g))
                        mm(o[:], ones[:], states[:, gs(g)]).then_inc(*step("ss", g))
                        pe.wait_ge(*at("cbt_s", g))
                        mm(ff[:], w_eb2[:], cbt1[:, g], stop=False)
                        second(1)
                        o = fresh("quick", "wo1", g)
                        pe.wait_ge(*at("z", g))
                        for j in range(2):
                            i = mm(o[:], W1["wout"][:, cs(j)], xi[:, j, gs(g)], start=j == 0, stop=j == 1)
                        i.then_inc(*step("wo1", g))
                        for e in range(3, E1 + 1):
                            first(e)
                            second(e - 1)
                        second(E1)
                        pe.wait_ge(*at("acc", g, E1 - 1))
                        for c in range(C):
                            i = mm(ff[:, cs(c)], acc[:, c], ident[:], start=False, stop=c == C - 1)
                        i.then_inc(*step("ff", 1, g))

                    def layer2_rec(g):
                        xg = xn[2][:, gs(g)]
                        pe.wait_ge(*at("xn", 2, g))
                        mm(fresh("quick", "gt", g)[0:32], W2["wg"], xg).then_inc(*step("gt", g))
                        for j in range(4):
                            mm(fresh("quick", "q2", g, j)[:], W2["wq"][:, cs(j)], xg).then_inc(*step("q2", g, j))
                        pe.wait_ge(*at("g3", g))
                        for e in range(NE):
                            mm(fresh("quick", "ga", g, e)[:], sel_e[:, e:e + 1].to_broadcast([96, P]), g3[:]).then_inc(*step("ga", g, e))
                        accs = {}

                        def spread(n):
                            he = n % NH * NE + n // NH
                            mm(fresh("quick", "gb", g, n)[:], sel_he[:, he:he + 1].to_broadcast([96, P]), g3[:]).then_inc(
                                *step("gb", g, n))

                        def project(n):
                            e, h = n // NH, n % NH
                            if h == 0:
                                accs[e] = fresh("slow", "gkv", g, e)
                            pe.wait_ge(*at("xs", g, n))
                            i = mm(accs[e][:], W2["wkv"][:, h * 128:(h + 1) * 128], xs[:, n % 3], start=h == 0,
                                   stop=h == NH - 1)
                            i.then_inc(*step("gkv", g, n))
                        for n in range(NE * NH + 2):
                            if n == NE * NH // 2:
                                head(*((2, 1) if g == 0 else (3, 0)))
                            if n < NE * NH:
                                spread(n)
                            if n >= 2:
                                project(n - 2)

                    def layer2_att(g):
                        for n, blocks in enumerate(VT_JOBS[g]):
                            o = fresh("quick", "vt", g, n)
                            pe.wait_ge(*at("rec", g, NE - 1))
                            for k, blk in enumerate(blocks):
                                src = rec[64:128, blk, 1:L + 1].rearrange("p c e -> p (c e)")
                                i = nc.tensor.transpose(o[:, k * DK:(k + 1) * DK], src, ident[64:128, 64:128])
                            i.then_inc(*step("vt", g, n))
                        pv_bank = {}

                        def score(l):
                            lb = g * GB + l
                            o = fresh("quick", "s2", g, l)
                            mm(o[:].rearrange("p (a b) -> p a b", a=2), sel_q[:],
                               cage[:].rearrange("p (a b) -> p a b", a=1).to_broadcast([L, 2, NE * 2 * L]), stop=False)
                            if l == 0:
                                pe.wait_ge(*at("qf", g, 3))
                            for hg in range(2):
                                i = mm(o[:, hg * 256:hg * 256 + 256],
                                       qf[:, l, 4 * hg:4 * hg + 4].rearrange("p h q -> p (h q)"),
                                       rec[0:64, lb:lb + 2, 1:L + 1].rearrange("p b c e -> p b (c e)"),
                                       start=False, stop=hg == 1)
                            i.then_inc(*step("s2", g, l))

                        def turned(l):
                            o = fresh("quick", "pt", g, l)
                            pe.wait_ge(*at("prob", g, l))
                            for blk in range(2):
                                for hg in range(2):
                                    k = (blk * 2 + hg) * P
                                    i = nc.tensor.transpose(o[:, k:k + P], prob[:, l % 3, hg, blk * P:(blk + 1) * P],
                                                            ident[:])
                            i.then_inc(*step("pt", g, l))

                        def value(l):
                            if l % 2 == 0:
                                pv_bank[0] = fresh("slow", "pv", g, l // 2)
                                if l == 0:
                                    pe.wait_ge(*at("vt_s", g, len(VT_JOBS[g]) - 1))
                            o = pv_bank[0][0:DK, (l % 2) * 256:(l % 2) * 256 + 256]
                            pe.wait_ge(*at("pt_s", g, l))
                            for blk in range(2):
                                i = mm(o, vt[:, g * GB + l + blk], pt[:, l % 3, blk * 256:(blk + 1) * 256],
                                       start=blk == 0, stop=blk == 1)
                            i.then_inc(*step("pv", g, l))
                        for l in range(GB + 4):
                            if l < GB:
                                score(l)
                            if 2 <= l < GB + 2:
                                turned(l - 2)
                            if l >= 4:
                                value(l - 4)
                        pe.wait_ge(*at("xk", g))
                        mm(fresh("quick", "r2", g)[:], W2["wr"], xr[:]).then_inc(*step("r2", g))
                        mm(fresh("quick", "k2", g)[:], W2["wk"], xk[:]).then_inc(*step("k2", g))
                        o = fresh("slow", "s", 2, g)
                        pe.wait_ge(*at("yt", g, GB // 2 - 1))
                        for j in range(4):
                            i = mm(o[:], W2["wo"][:, cs(j)], yt[:, j], start=j == 0, stop=j == 3)
                        i.then_inc(*step("s", 2, g))
                        o = fresh("quick", "v2", g)
                        pe.wait_ge(*at("kr", g))
                        mm(o[:], W2["wv"], kr[:]).then_inc(*step("v2", g))

                    def layer3(g):
                        xg = xn[3][:, gs(g)]
                        pe.wait_ge(*at("xn", 3, g))
                        mm(fresh("quick", "qk3", g)[:], W3["wqk"], xg).then_inc(*step("qk3", g))
                        o = fresh("quick", "v3", g)
                        for c in range(C):
                            i = mm(o[:, c * DK:(c + 1) * DK], xg[:, cs(c)], W3["wv"])
                        i.then_inc(*step("v3", g))
                        o = fresh("quick", "rt3", g)
                        for c in range(C):
                            i = mm(o[:, c * E3:(c + 1) * E3], xg[:, cs(c)], W3["rw"])
                        i.then_inc(*step("rt3", g))

                        def score(c):
                            n = g * C + c
                            halves = (n + 4) // 4
                            pe.wait_ge(*at("k3", g))
                            for k in range(halves):
                                keys = min(GT, (n + 1) * CT - k * GT)
                                o = fresh("quick", "s3", n, k)
                                last = k == halves - 1
                                i = mm(o[:, 0:keys], q3[:, n * CT:(n + 1) * CT], k3[:, k * GT:k * GT + keys],
                                       stop=not last)
                                if last:
                                    i = mm(o[:, keys - CT:keys], identb[:], above[:], start=False)
                                i.then_inc(*step("s3", n, k))

                        def values(c):
                            n = g * C + c
                            halves = (n + 4) // 4
                            for k in range(halves):
                                kc = min(4, n + 1 - 4 * k)
                                o = fresh("quick", "pt3", n, k)
                                if k == 0:
                                    pe.wait_ge(*at("p3", n))
                                for j in range(kc):
                                    i = nc.tensor.transpose(o[:, cs(j)], p3b[:, n % 2, k * GT + j * CT:
                                                                             k * GT + (j + 1) * CT], ident[:])
                                i.then_inc(*step("pt3", n, k))
                            for k in range(halves):
                                kc = min(4, n + 1 - 4 * k)
                                pe.wait_ge(*at("pt3_s", n, k))
                                for j in range(kc):
                                    i = mm(ob[0:DK, cs(c)], v3[:, 4 * k + j], pt3[:, k, j], start=k == 0 and j == 0,
                                           stop=4 * k + j == n)
                                i.then_inc(*step("o3", n, k))
                        if g == 0:
                            head(3, 1)
                        ob = fresh("slow", "o3", g)
                        for c in range(C + 1):
                            if c < C:
                                score(c)
                            if c >= 1:
                                values(c - 1)
                        o = fresh("quick", "ct3", g)
                        ct_out = o[0:48].bitcast(BF16)
                        pe.wait_ge(*at("cb3", g))
                        for c in range(C):
                            i = nc.tensor.transpose(ct_out[:, cs(c)], cb3[:, g * C + c], identb[:])
                        i.then_inc(*step("ct3", g))
                        ff = fresh("slow", "ff", 3, g)

                        def first(k):
                            wg_, wu_ = ((W3["shg"], W3["shu"]) if k == EP3 else
                                        (W3["gate"][:, cs(k)], W3["up"][:, cs(k)]))
                            mm(fresh("quick", "gate3", g, k)[:], wg_, xg).then_inc(*step("gate3", g, k))
                            mm(fresh("quick", "up3", g, k)[:], wu_, xg).then_inc(*step("up3", g, k))
                            if k < EP3:
                                o = fresh("slow", "cb3", g, k)
                                if k == 0:
                                    pe.wait_ge(*at("ct3_s", g))
                                mm(o[:], sel_p[:, k], ct3[:, g]).then_inc(*step("cbb3", g, k))

                        def second(k):
                            pe.wait_ge(*at("hh3", g, k))
                            w = W3["shd"] if k == EP3 else W3["down"][:, cs(k)]
                            i = mm(ff[:], w, hh3[:, k % 3], start=k == 0, stop=k == EP3)
                            i.then_inc(*(step("ff", 3, g) if k == EP3 else step("dn3", g, k)))
                        for k in range(EP3 + 2):
                            if k <= EP3:
                                first(k)
                            if k >= 1:
                                second(k - 1)
                        o = fresh("slow", "s", 3, g)
                        pe.wait_ge(*at("o3_s", g))
                        mm(o[:], w_out3[:], o3[:, g]).then_inc(*step("s", 3, g))

                    for g in range(G):
                        head(0, g)
                    for _ in zip_longest(*[layer0(g) for g in range(G)]):
                        pass
                    head(1, 0)
                    now[0] = 1
                    pe.wait_ge(ready["one"], 32)
                    for g in range(G):
                        layer1(g)
                    now[0] = 2
                    pe.wait_ge(ready["two"], 32)
                    for g in range(G):
                        layer2_rec(g)
                        layer2_att(g)
                    now[0] = 3
                    pe.wait_ge(ready["three"], 32)
                    for g in range(G):
                        layer3(g)

                def psum(*job):
                    return bank[known.get(job + ("bank",), 0)]

                @block.scalar
                def _(act):
                    now = [0]

                    def step(*m):
                        return prog["scalar", now[0]].step(*m)

                    def after(*needs):
                        s = prog["scalar", now[0]]
                        if s.count:
                            act.wait_ge(s.sem, s.count)
                        for m in needs:
                            act.wait_ge(*at(*m))

                    def fn(o, i, f, bias=0.0, scale=1.0, **kw):
                        return nc.scalar.activation(o, i, f, bias=bias, scale=scale, **kw)

                    def rsqrt(l, g, eps, name):
                        after((name, l, g))
                        fn(rs[:, g], psum(name, l, g)[:], ACT.Ln, bias=eps).then_inc(*step(name, l, g, "read"))
                        after()
                        fn(rs[:, g], rs[:, g], ACT.Exp, scale=-0.5).then_inc(*step("rs", name, l, g))

                    def norm(l, g):
                        after(("xc", l, g), *([("xn", l - 1, g)] if l else []))
                        fn(sq[:, g], psum("xc", l, g)[:], ACT.Square).then_inc(*step("sq", "var", l, g))
                        rsqrt(l, g, 1e-5, "var")

                    def gate(l, g, src, bias, *needs):
                        after(*needs, *([("x", l + 1, 0) if l < 3 else ("x out", 0)] if g else []))
                        fn(tz[:], src, ACT.Tanh, scale=0.5, bias=bias).then_inc(*step("tz", l, g))

                    def layer0(g):
                        after(("qk0", g))
                        qk = psum("qk0", g)[0:2 * DM]
                        fn(ek[:, g], qk, ACT.Relu, scale=-1.0).then_inc(*step())
                        after()
                        fn(ek[:, g], ek[:, g], ACT.Exp, scale=-1.0).then_inc(*step("ek", g))
                        yield
                        after(("kvg0", g))
                        kv = psum("kvg0", g)[:, 0:C * KVG].rearrange("p (c k) -> p c k", k=KVG)
                        fn(vtok0[:, g * C:(g + 1) * C, 0:DM], kv[:, :, DM:2 * DM], ACT.Copy).then_inc(
                            *step("vtok0", g))
                        fn(et[:, g], kv[:, :, 0:DM], ACT.Relu, scale=-1.0).then_inc(*step())
                        after()
                        fn(et[:, g], et[:, g], ACT.Exp, scale=-1.0).then_inc(*step("et", g))
                        yield
                        after(("gdiff", g))
                        fn(gw[:, g * C:(g + 1) * C, 1], gw[:, g * C:(g + 1) * C, 0], ACT.Exp).then_inc(
                            *step("gexp", g))
                        yield
                        gate(0, g, psum("ff", 0, g)[:], half0[:], ("ff", 0, g))

                    def layer1(g):
                        after(("xn", 1, g))
                        fn(sq[:, g], xn[1][:, gs(g)], ACT.Square).then_inc(*step("sq", "rms", 1, g))
                        for j in range(4):
                            after(("xr", g, j), *([("xi", g, j - 2)] if j >= 2 else []))
                            fn(tx[:, j % 2], psum("xr", g, j)[:], ACT.Tanh, scale=0.5,
                               bias=half1[:, j:j + 1]).then_inc(*step("tx", g, j))
                        rsqrt(1, g, 1e-8, "rms")
                        after(("rt1", g))
                        fn(pr[:, g * C:(g + 1) * C], psum("rt1", g)[:, 0:C * E1].rearrange(
                            "p (c k) -> p c k", k=E1), ACT.Exp, scale=-1.0).then_inc(*step("rt1", g, "read"))
                        after(("dt", g))
                        fn(dab[:], psum("dt", g)[:], ACT.Abs, bias=W1["bdt"]).then_inc(*step())
                        after()
                        fn(dab[:], dab[:], ACT.Exp, scale=-1.0).then_inc(*step())
                        after()
                        fn(dab[:], dab[:], ACT.Ln, bias=1.0).then_inc(*step("dab", g))
                        after(("bx", g))
                        fn(bx[:, gs(g)], psum("bx", g)[0:ST], ACT.Identity, bias=S1["bxp"]).then_inc(
                            *step("bx", g, "read"))
                        fn(xd[:], xn[1][:, gs(g)], ACT.Identity, bias=W1["bout"], scale=W1["dskip"]).then_inc(
                            *step("xd", g))

                        def relus(e):
                            for j in range(1, HJ, 2):
                                needs = [("h1", g, e, j)]
                                if e >= 2:
                                    needs.append(("eo", g, e - 2))
                                elif g == 1:
                                    needs.append(("eo", 0, E1 - 1 + (1 if e % 2 == 0 else 0)))
                                after(*needs)
                                bias = W1["sb1"][:, j:j + 1] if e == E1 else W1["eb1"][:, e * HJ + j:e * HJ + j + 1]
                                fn(hid[:, e % 2, j], psum("h1", g, e, j)[:], ACT.Relu, bias=bias).then_inc(
                                    *step("hid", g, e, j))
                                reached[("h1", g, e, j, "read")] = reached[("hid", g, e, j)]
                        relus(0)
                        after(("cbt", g))
                        fn(cbt1[:, g], psum("cbt", g)[0:E1], ACT.Copy).then_inc(*step("cbt_s", g))
                        reached[("cbt", g, "read")] = reached[("cbt_s", g)]
                        relus(1)
                        norm(*((1, 1) if g == 0 else (2, 0)))
                        after(("md", g))
                        fn(decay[:, gs(g)], psum("md", g)[0:ST], ACT.Exp, scale=neg_a[:]).then_inc(
                            *step("decay", g))
                        reached[("md", g, "read")] = reached[("decay", g)]
                        relus(2)
                        after(("ss", g))
                        fn(ssum[:], psum("ss", g)[:], ACT.Copy).then_inc(*step("ssum", g))
                        reached[("ss", g, "read")] = reached[("ssum", g)]
                        for e in range(3, E1 + 1):
                            relus(e)
                        gate(1, g, psum("ff", 1, g)[:], half1[:, 4:5], ("ff", 1, g))

                    def layer2_rec(g):
                        after(("gt", g), ("x", 2, 1), *([("g3", 0)] if g else []))
                        fn(gfm[:, 0], psum("gt", g)[0:32], ACT.Exp, scale=-1.0, bias=neg_bg[:]).then_inc(
                            *step("gt", g, "read"))
                        for j in range(4):
                            after(("q2", g, j), *([("s2", 0, GB - 1)] if g else []))
                            for half in range(2):
                                fn(qf[:, :, 2 * j + half], psum("q2", g, j)[half * 64:half * 64 + 64].rearrange(
                                    "p (l q) -> p l q", q=L), ACT.Copy, scale=DK ** -0.5).then_inc(*step("qf", g, j))
                            reached[("q2", g, j, "read")] = reached[("qf", g, j)]
                        for e in range(NE):
                            after(("ga", g, e), *([("rec", 0, NE - 1)] if g else []))
                            fn(abc[:, e, :, 1:L + 1],
                               psum("ga", g, e)[:].rearrange("p (l c) -> p l c", c=L), ACT.Relu, scale=-1.0,
                               bias=1.0).then_inc(*step("abc", g, e))
                            reached[("ga", g, e, "read")] = reached[("abc", g, e)]
                        for e in range(NE):
                            if e == 1:
                                norm(*((2, 1) if g == 0 else (3, 0)))
                            after(("gkv", g, e * NH + NH - 1))
                            fn(rec[:, 1 + g * GB:1 + (g + 1) * GB, 1:L + 1, e],
                               psum("gkv", g, e)[:].rearrange("p (l c) -> p l c", c=L), ACT.Copy).then_inc(
                                *step("gkv_s", g, e))
                            reached[("gkv", g, e, "read")] = reached[("gkv_s", g, e)]

                    def layer2_att(g):
                        for n, blocks in enumerate(VT_JOBS[g]):
                            after(("vt", g, n), *([("pv", 0, GB - 1)] if g else []))
                            k = len(blocks)
                            fn(vt[:, blocks[0]:blocks[0] + k], psum("vt", g, n)[:, 0:k * DK].rearrange(
                                "p (a b) -> p a b", b=DK), ACT.Copy).then_inc(*step("vt_s", g, n))
                            reached[("vt", g, n, "read")] = reached[("vt_s", g, n)]

                        def probs(l):
                            needs = [("mx2", g, l)]
                            if l >= 3:
                                needs.append(("pt", g, l - 3))
                            elif g == 1:
                                needs.append(("pt", 0, GB - 1))
                            after(*needs)
                            for hg in range(2):
                                fn(prob[:, l % 3, hg], psum("s2", g, l)[:, hg * 256:hg * 256 + 256], ACT.Exp,
                                   bias=smx[:, l % 3, hg:hg + 1],
                                   accum_out=smx[:, l % 3, 2 + hg:3 + hg]).then_inc(*step("e2", g, l))
                            reached[("s2", g, l, "read")] = reached[("e2", g, l)]

                        def turned(l):
                            needs = [("pt", g, l)]
                            if l >= 3:
                                needs.append(("pv", g, l - 3))
                            elif g == 1:
                                needs.append(("pv", 0, GB - 1))
                            after(*needs)
                            fn(pt[:, l % 3], psum("pt", g, l)[:], ACT.Copy).then_inc(*step("pt_s", g, l))
                            reached[("pt", g, l, "read")] = reached[("pt_s", g, l)]
                        for l in range(GB + 3):
                            if l < GB:
                                probs(l)
                            if l >= 3:
                                turned(l - 3)
                        after(("r2", g))
                        fn(tr[:], psum("r2", g)[:], ACT.Tanh, scale=0.5).then_inc(*step("r2", g, "read"))
                        after(("k2", g))
                        fn(kr[:], psum("k2", g)[:], ACT.Relu).then_inc(*step("k2", g, "read"))
                        after()
                        fn(kr[:], kr[:], ACT.Square).then_inc(*step("kr", g))
                        gate(2, g, of[:], 0.0, ("of", g))

                    def layer3(g):
                        after(("qk3", g), ("x", 3, 1))
                        fn(q3[:, gs(g)], psum("qk3", g)[0:DK], ACT.Copy, scale=DK ** -0.5).then_inc(*step())
                        fn(k3[:, gs(g)], psum("qk3", g)[DK:P], ACT.Copy).then_inc(*step("k3", g))
                        reached[("qk3", g, "read")] = reached[("k3", g)]
                        after(("v3", g))
                        fn(v3[:, g * C:(g + 1) * C], psum("v3", g)[:, 0:C * DK].rearrange(
                            "p (c k) -> p c k", k=DK), ACT.Copy).then_inc(*step("v3_s", g))
                        reached[("v3", g, "read")] = reached[("v3_s", g)]
                        after(("gdiff3", g))
                        fn(w3s[:, g * C:(g + 1) * C, 1], w3s[:, g * C:(g + 1) * C, 0], ACT.Exp).then_inc(
                            *step("gexp3", g))

                        def probs(c):
                            n = g * C + c
                            halves = (n + 4) // 4
                            needs = [("mx3", n)]
                            if n >= 2:
                                needs.append(("pt3", n - 2, (n + 2) // 4 - 1))
                            after(*needs)
                            for k in range(halves):
                                keys = min(GT, (n + 1) * CT - k * GT)
                                fn(p3b[:, n % 2, k * GT:k * GT + keys], psum("s3", n, k)[:, 0:keys], ACT.Exp,
                                   bias=sm3[:, n, 0:1], accum_out=sm3[:, n, 1 + k:2 + k]).then_inc(
                                    *step("e3", n, k))
                                reached[("s3", n, k, "read")] = reached[("e3", n, k)]

                        def turned(c):
                            n = g * C + c
                            halves = (n + 4) // 4
                            for k in range(halves):
                                kc = min(4, n + 1 - 4 * k)
                                after(("pt3", n, k), *([("o3", n - 1, (n + 3) // 4 - 1)] if n else []))
                                fn(pt3[:, k, 0:kc], psum("pt3", n, k)[:, 0:kc * CT].rearrange(
                                    "p (a b) -> p a b", b=CT), ACT.Copy).then_inc(*step("pt3_s", n, k))
                                reached[("pt3", n, k, "read")] = reached[("pt3_s", n, k)]
                        if g == 0:
                            norm(3, 1)
                        for c in range(C + 1):
                            if c < C:
                                probs(c)
                            if c >= 1:
                                turned(c - 1)
                        after(("o3", g * C + C - 1, (g * C + C + 3) // 4 - 1))
                        fn(o3[:, g], psum("o3", g)[0:DK], ACT.Copy).then_inc(*step("o3_s", g))
                        reached[("o3", g, "read")] = reached[("o3_s", g)]
                        after(("ct3", g))
                        fn(ct3[:, g], psum("ct3", g)[0:48].bitcast(BF16)[:, 0:GT], ACT.Copy).then_inc(
                            *step("ct3_s", g))
                        reached[("ct3", g, "read")] = reached[("ct3_s", g)]
                        for k in range(EP3 + 1):
                            needs = [("gate3", g, k)]
                            if k >= 2:
                                needs.append(("hg3", g, k - 2))
                            elif g:
                                needs.append(("hg3", 0, EP3))
                            after(*needs)
                            fn(tg3[:, k % 2], psum("gate3", g, k)[:], ACT.Tanh, scale=0.5).then_inc(
                                *step("tg3", g, k))
                        gate(3, g, psum("ff", 3, g)[:], 0.0, ("ff", 3, g))

                    for g in range(G):
                        norm(0, g)
                    for _ in zip_longest(*[layer0(g) for g in range(G)]):
                        pass
                    norm(1, 0)
                    now[0] = 1
                    for g in range(G):
                        layer1(g)
                    now[0] = 2
                    for g in range(G):
                        layer2_rec(g)
                        layer2_att(g)
                    now[0] = 3
                    for g in range(G):
                        layer3(g)

                @block.vector
                def _(dve):
                    now = [0]
                    v = nc.vector

                    def step(*m):
                        return prog["vector", now[0]].step(*m)

                    def after(*needs):
                        s = prog["vector", now[0]]
                        if s.count:
                            dve.wait_ge(s.sem, s.count)
                        for m in needs:
                            dve.wait_ge(*at(*m))

                    def norm(l, g):
                        after(("rs", "var", l, g), *([("x", l, g)] if l else []))
                        v.tensor_tensor(xn[l][:, gs(g)], psum("xc", l, g)[:], rs[:, g], ALU.mult).then_inc(
                            *step("xn", l, g))
                        reached[("xc", l, g, "read")] = reached[("xn", l, g)]

                    def merge(l, g, gate_src, gate_bias, s_src, s_bias, free_gate, free_s, *needs):
                        after(("tz", l, g), *needs)
                        v.tensor_scalar(hz[:], gate_src, gate_bias, 0.5, ALU.add, ALU.mult).then_inc(*step())
                        after()
                        v.scalar_tensor_tensor(hz[:], tz[:], 1.0, hz[:], ALU.add, ALU.mult).then_inc(
                            *step(*(("ff", l, g, "read") if free_gate else ())))
                        after(("s", l, g))
                        v.scalar_tensor_tensor(hz[:], s_src, s_bias, hz[:], ALU.add, ALU.mult).then_inc(
                            *step(*(("s", l, g, "read") if free_s else ())))
                        after()
                        v.tensor_tensor(x[:, gs(g)], (x if l else x0)[:, gs(g)], hz[:], ALU.add).then_inc(
                            *step(*(("x", l + 1, g) if l < 3 else ("x out", g))))

                    def layer0(g):
                        cc = slice(g * C, (g + 1) * C)
                        qk = psum("qk0", g)
                        kv = psum("kvg0", g)[:, 0:C * KVG].rearrange("p (c k) -> p c k", k=KVG)
                        after(("ek", g))
                        v.scalar_tensor_tensor(sgq[:, gs(g)], qk[0:DM], 0.0, ek[0:DM, g], ALU.max,
                                               ALU.add).then_inc(*step())
                        v.scalar_tensor_tensor(sgk[:, gs(g)], qk[DM:2 * DM], 0.0, ek[DM:2 * DM, g], ALU.max,
                                               ALU.add).then_inc(*step("sgk", g))
                        reached[("qk0", g, "read")] = reached[("sgk", g)]
                        yield
                        after(("kvg0", g), ("et", g))
                        v.tensor_copy(logit[:, cc, 0:NGATE], kv[:, :, 2 * DM:KVG]).then_inc(*step())
                        v.scalar_tensor_tensor(ktok[:, cc], kv[:, :, 0:DM], 0.0, et[:, g], ALU.max,
                                               ALU.add).then_inc(*step("ktok0", g))
                        reached[("kvg0", g, "read")] = reached[("ktok0", g)]
                        after()
                        for c in range(g * C, (g + 1) * C):
                            v.max(top[:, c], logit[:, c]).then_inc(*step())
                        after()
                        v.tensor_tensor(gw[:, cc, 0], top[:, cc, 1], top[:, cc, 0], ALU.subtract).then_inc(
                            *step("gdiff", g))
                        yield
                        after(("gexp", g))
                        v.tensor_scalar(gw[:, cc, 2], gw[:, cc, 1], 1.0, None, ALU.add).then_inc(*step())
                        after()
                        v.reciprocal(gw[:, cc, 3], gw[:, cc, 2]).then_inc(*step())
                        after()
                        v.tensor_tensor(gw[:, cc, 4], gw[:, cc, 1], gw[:, cc, 3], ALU.mult).then_inc(*step())
                        after()
                        v.tensor_tensor(gw[:, cc, 5], gw[:, cc, 4], gw[:, cc, 3], ALU.add).then_inc(*step())
                        after(("y0", g))
                        v.tensor_tensor(ysc[:, g], psum("y0", g)[:].rearrange("p (c k) -> p c k", k=P),
                                        gw[:, cc, 5:6].to_broadcast([P, C, P]), ALU.mult).then_inc(*step("ysc", g))
                        reached[("y0", g, "read")] = reached[("ysc", g)]
                        yield
                        for c in range(C):
                            n = g * C + c
                            after(("kv0", g))
                            v.tensor_tensor(state[:, n + 1], state[:, n], psum("kv0", g)[0:DM, c * 64:c * 64 + 64],
                                            ALU.add).then_inc(*step("state", g))
                        reached[("kv0", g, "read")] = reached[("state", g)]
                        after(("a0", g))
                        v.tensor_tensor(att[:, g], psum("a0", g)[:].rearrange("p (c k) -> p c k", k=P),
                                        causal[:].rearrange("p (a k) -> p a k", a=1).to_broadcast([P, C, P]),
                                        ALU.mult).then_inc(*step("att0", g))
                        reached[("a0", g, "read")] = reached[("att0", g)]
                        yield
                        after(("ret0", g))
                        r = psum("ret0", g)
                        v.tensor_scalar(rn[:, g], r[DM:2 * DM], EPS_MEM, None, ALU.max).then_inc(*step())
                        after()
                        v.reciprocal(rn[:, g], rn[:, g]).then_inc(*step())
                        after()
                        v.scalar_tensor_tensor(comb0[:, g], r[0:DM], flag[:, 0:1], rn[:, g], ALU.mult,
                                               ALU.mult).then_inc(*step("ret0", g, "read"))
                        yield
                        after(("num0", g))
                        r = psum("num0", g)
                        v.tensor_scalar(rd[:, g], r[DM:2 * DM], EPS_MEM, None, ALU.max).then_inc(*step())
                        after()
                        v.reciprocal(rd[:, g], rd[:, g]).then_inc(*step())
                        after()
                        v.scalar_tensor_tensor(c2[:, g], r[0:DM], flag[:, 1:2], rd[:, g], ALU.mult,
                                               ALU.mult).then_inc(*step("num0", g, "read"))
                        after()
                        v.tensor_tensor(comb0[:, g], comb0[:, g], c2[:, g], ALU.add).then_inc(*step("comb0", g))
                        yield
                        merge(0, g, psum("ff", 0, g)[:], W0["bias"], psum("s", 0, g)[:], 0.0, True, True, ("ff", 0, g))

                    def top2(g, scores, tops, idx, idf, n):
                        after()
                        for c in range(g * C, (g + 1) * C):
                            v.max(tops[:, c], scores[:, c]).then_inc(*step())
                        after()
                        for c in range(g * C, (g + 1) * C):
                            v.max_index(idx[:, c], tops[:, c], scores[:, c]).then_inc(*step())
                        after()
                        cc = slice(g * C, (g + 1) * C)
                        v.tensor_copy(idf[:, cc], idx[:, cc]).then_inc(*step())

                    def combination(g, idf, w1, w2, oh, cm, n, *name):
                        cc = slice(g * C, (g + 1) * C)
                        io = iota8[:, 0:n].rearrange("p (a k) -> p a k", a=1).to_broadcast([P, C, n])
                        after()
                        for k in range(2):
                            v.tensor_tensor(oh[:, k, cc], io, idf[:, cc, k:k + 1].to_broadcast([P, C, n]),
                                            ALU.is_equal).then_inc(*step())
                        after()
                        for k, w in ((0, w1), (1, w2)):
                            v.tensor_tensor(oh[:, k, cc], oh[:, k, cc], w.to_broadcast([P, C, n]),
                                            ALU.mult).then_inc(*step())
                        after()
                        v.tensor_tensor(cm[:, cc], oh[:, 0, cc], oh[:, 1, cc], ALU.add).then_inc(*step(*name))

                    def layer1(g):
                        for j in range(4):
                            after(("tx", g, j), *([("zp", 0)] if g and j >= 2 else []))
                            v.tensor_scalar(hx[:, j % 2], psum("xr", g, j)[:], W1["bin"][:, j:j + 1], 0.5, ALU.add,
                                            ALU.mult).then_inc(*step())
                            after()
                            dst = xi[:, j, gs(g)] if j < 2 else sr[:, j - 2]
                            v.scalar_tensor_tensor(dst, tx[:, j % 2], 1.0, hx[:, j % 2], ALU.add, ALU.mult).then_inc(
                                *step("xi", g, j))
                            reached[("xr", g, j, "read")] = reached[("xi", g, j)]
                        after(("rs", "rms", 1, g))
                        v.scalar_tensor_tensor(nm[:, gs(g)], xn[1][:, gs(g)], W1["wn"], rs[:, g], ALU.mult,
                                               ALU.mult).then_inc(*step("nm", g))
                        cc = slice(g * C, (g + 1) * C)
                        after(("rt1", g, "read"))
                        v.tensor_scalar(pr[:, cc], pr[:, cc], 1.0, None, ALU.add).then_inc(*step())
                        after()
                        v.reciprocal(pr[:, cc], pr[:, cc]).then_inc(*step())
                        top2(g, pr, top1, idx1, idf1, E1)
                        v.scalar_tensor_tensor(wsm1[:, cc, 0], top1[:, cc, 0], 1e-6, top1[:, cc, 1], ALU.add,
                                               ALU.add).then_inc(*step())
                        after()
                        v.reciprocal(wsm1[:, cc, 1], wsm1[:, cc, 0]).then_inc(*step())
                        after()
                        for k in range(2):
                            v.tensor_tensor(wsm1[:, cc, 2 + k], top1[:, cc, k], wsm1[:, cc, 1], ALU.mult).then_inc(
                                *step())
                        combination(g, idf1, wsm1[:, cc, 2:3], wsm1[:, cc, 3:4], oh1, cmb1, E1, "cmb1", g)
                        after(("dab", g))
                        v.tensor_scalar(dpos[:], psum("dt", g)[:], W1["bdt"], 0.0, ALU.add, ALU.max).then_inc(
                            *step())
                        after()
                        v.tensor_tensor(dab[:], dab[:], dpos[:], ALU.add).then_inc(*step("delta", g))
                        reached[("dt", g, "read")] = reached[("delta", g)]

                        def relus(e):
                            for j in range(0, HJ, 2):
                                needs = [("h1", g, e, j)]
                                if e >= 2:
                                    needs.append(("eo", g, e - 2))
                                elif g == 1:
                                    needs.append(("eo", 0, E1 - 1 + (1 if e % 2 == 0 else 0)))
                                after(*needs)
                                bias = W1["sb1"][:, j:j + 1] if e == E1 else W1["eb1"][:, e * HJ + j:e * HJ + j + 1]
                                v.tensor_scalar(hid[:, e % 2, j], psum("h1", g, e, j)[:], bias, 0.0, ALU.add,
                                                ALU.max).then_inc(*step("hid", g, e, j))
                                reached[("h1", g, e, j, "read")] = reached[("hid", g, e, j)]

                        def weigh(e):
                            after(("eo", g, e))
                            for c in range(C):
                                w = cmb1[:, g * C + c, e:e + 1]
                                src = psum("eo", g, e)[:, cs(c)]
                                if e == 0:
                                    i = v.tensor_scalar(acc[:, c], src, w, None, ALU.mult)
                                else:
                                    i = v.scalar_tensor_tensor(acc[:, c], src, w, acc[:, c], ALU.mult, ALU.add)
                                i.then_inc(*step("acc", g, e))
                            reached[("eo", g, e, "read")] = reached[("acc", g, e)]
                        relus(0)
                        relus(1)
                        norm(*((1, 1) if g == 0 else (2, 0)))
                        after(("decay", g), ("bx", g, "read"))
                        v.tensor_tensor_scan(states[:, gs(g)], decay[:, gs(g)], bx[:, gs(g)],
                                             states[:, g * GT - 1:g * GT] if g else 0.0, ALU.mult,
                                             ALU.add).then_inc(*step("states", g))
                        weigh(0)
                        relus(2)
                        weigh(1)
                        after(("wo1", g), ("ssum", g))
                        v.tensor_tensor(s1out[:], psum("wo1", g)[:], ssum[:], ALU.mult).then_inc(
                            *step("wo1", g, "read"))
                        after(("xd", g))
                        v.tensor_tensor(s1out[:], s1out[:], xd[:], ALU.add).then_inc(*step("s", 1, g))
                        relus(3)
                        for e in range(4, E1 + 1):
                            weigh(e - 2)
                            relus(e)
                        weigh(E1 - 1)
                        merge(1, g, psum("ff", 1, g)[:], W1["sb2"], s1out[:], 0.0, True, False, ("ff", 1, g))

                    def chains():
                        after(("s", 1, 1))
                        init = W2["init"].rearrange("p (l e) -> p l e", e=NE)
                        v.tensor_copy(rec[:, 0, 1:L + 1], init).then_inc(*step())
                        v.tensor_copy(rec[:, 1:NB + 1, 0], init).then_inc(*step())
                        v.memset(rec[:, 0, 0], 0.0).then_inc(*step())
                        v.memset(abc[:, :, :, 0:1], 0.0).then_inc(*step("chains"))

                    def layer2_rec(g):
                        if g == 0:
                            dve.wait_ge(ready["two"], 32)
                            chains()
                        after(("gt", g, "read"))
                        q = gfm[:]
                        v.tensor_scalar(q[:, 0], q[:, 0], 1.0, None, ALU.add).then_inc(*step())
                        after()
                        v.reciprocal(q[:, 1], q[:, 0]).then_inc(*step())
                        after()
                        v.tensor_copy(gb[:, 0], q[:, 1]).then_inc(*step())
                        if g:
                            dve.wait_ge(*at("gkv", 0, NE * NH - 1))
                        v.tensor_copy(g3[0:32], q[:, 1]).then_inc(*step())
                        after()
                        v.tensor_tensor(q[:, 2], q[:, 1], gb[:, 0], ALU.subtract).then_inc(*step())
                        after()
                        v.tensor_copy(gb[:, 1], q[:, 2]).then_inc(*step())
                        v.tensor_copy(g3[32:64], q[:, 2]).then_inc(*step())
                        after()
                        v.tensor_tensor(g3[64:96], q[:, 2], gb[:, 1], ALU.subtract).then_inc(*step("g3", g))
                        for n in range(NE * NH):
                            if n == NE * NH // 2:
                                norm(*((2, 1) if g == 0 else (3, 0)))
                            needs = [("gb", g, n)]
                            if n >= 3:
                                needs.append(("gkv", g, n - 3))
                            elif g:
                                needs.append(("gkv", 0, NE * NH - 1))
                            after(*needs)
                            v.tensor_tensor(xs[:, n % 3], psum("gb", g, n)[:], xn[2][:, gs(g)], ALU.mult).then_inc(
                                *step("xs", g, n))
                            reached[("gb", g, n, "read")] = reached[("xs", g, n)]
                            if n % NH == NH - 1 and n // NH >= 1:
                                scan(g, n // NH - 1)
                        scan(g, NE - 1)

                    def scan(g, e):
                        after(("gkv_s", g, e), ("abc", g, e))
                        r = rec[:, 1 + g * GB:1 + (g + 1) * GB].rearrange("p l c e -> p (l c) e")[:, :, e]
                        a = abc[:, e].rearrange("p l c -> p (l c)")
                        v.tensor_tensor_scan(r, a, r, 0.0, ALU.mult, ALU.add).then_inc(*step("rec", g, e))

                    def layer2_att(g):
                        def maxima(l):
                            needs = [("s2", g, l)]
                            after(*needs)
                            v.tensor_reduce(smx[:, l % 3, 0:2], psum("s2", g, l)[:].rearrange(
                                "p (a b) -> p a b", a=2), AX.X, ALU.max, negate=True).then_inc(*step("mx2", g, l))

                        def sums(l):
                            after(("e2", g, l))
                            v.reciprocal(smx[:, l % 3, 4:6], smx[:, l % 3, 2:4]).then_inc(*step("rc2", g, l))
                            after()
                            v.tensor_tensor(prob[:, l % 3], prob[:, l % 3],
                                            smx[:, l % 3, 4:6].rearrange("p (a b) -> p a b", b=1).to_broadcast(
                                                [P, 2, 4 * 2 * L]), ALU.mult).then_inc(*step("prob", g, l))

                        def out_rows(l2):
                            after(("pv", g, 2 * l2 + 1))
                            src = psum("pv", g, l2)[0:DK].rearrange("p (l h a q) -> p l h a q", l=2, h=4, a=2)
                            for half in range(2):
                                for l in range(2):
                                    t0 = (2 * l2 + l) * L
                                    v.tensor_copy(yt[half * 64:half * 64 + 64, :, t0:t0 + L],
                                                  src[:, l, :, half]).then_inc(*step("yt", g, l2))
                            reached[("pv", g, l2, "read")] = reached[("yt", g, l2)]
                        for l in range(GB + 6):
                            if l < GB:
                                maxima(l)
                            if 1 <= l < GB + 1:
                                sums(l - 1)
                            if l >= 6 and l % 2 == 1:
                                out_rows((l - 6) // 2)
                        out_rows(GB // 2 - 1)
                        after(*([("x", 3, 0)] if g else []))
                        now_, before = xn[2][:, gs(g)], xn_a[:, g * GT:(g + 1) * GT]
                        v.tensor_tensor(dx[:], now_, before, ALU.subtract).then_inc(*step())
                        after()
                        v.scalar_tensor_tensor(xr[:], dx[:], W2["mur"], before, ALU.mult, ALU.add).then_inc(
                            *step())
                        v.scalar_tensor_tensor(xk[:], dx[:], W2["muk"], before, ALU.mult, ALU.add).then_inc(
                            *step("xk", g))
                        after(("r2", g, "read"))
                        v.tensor_scalar(tr[:], tr[:], 1.0, 0.5, ALU.add, ALU.mult).then_inc(*step())
                        after(("v2", g))
                        v.tensor_tensor(of[:], psum("v2", g)[:], tr[:], ALU.mult).then_inc(*step("of", g))
                        reached[("v2", g, "read")] = reached[("of", g)]
                        merge(2, g, of[:], 0.0, psum("s", 2, g)[:], 0.0, False, True)

                    def layer3(g):
                        cc = slice(g * C, (g + 1) * C)
                        after(("rt3", g), ("x", 3, 1))
                        v.tensor_tensor(lg3[:, cc], psum("rt3", g)[:, 0:C * E3].rearrange("p (c k) -> p c k", k=E3),
                                        W3["rb"].rearrange("p (a k) -> p a k", a=1).to_broadcast([P, C, E3]),
                                        ALU.add).then_inc(*step("rt3", g, "read"))
                        top2(g, lg3, top3, idx3, idf3, E3)
                        v.tensor_tensor(w3s[:, cc, 0], top3[:, cc, 1], top3[:, cc, 0], ALU.subtract).then_inc(
                            *step("gdiff3", g))
                        after(("gexp3", g))
                        v.tensor_scalar(w3s[:, cc, 0], w3s[:, cc, 1], 1.0, None, ALU.add).then_inc(*step())
                        after()
                        v.reciprocal(w3s[:, cc, 2], w3s[:, cc, 0]).then_inc(*step())
                        after()
                        v.tensor_tensor(w3s[:, cc, 3], w3s[:, cc, 1], w3s[:, cc, 2], ALU.mult).then_inc(*step())
                        combination(g, idf3, w3s[:, cc, 2:3], w3s[:, cc, 3:4], oh3, cm3, E3)
                        after()
                        v.tensor_copy(cb3[:, cc, 0:16], cm3[:, cc]).then_inc(*step())
                        after()
                        v.tensor_tensor(cr3[:, cc], cm3[:, cc], cb3[:, cc, 0:16], ALU.subtract).then_inc(*step())
                        after()
                        v.tensor_copy(cb3[:, cc, 16:32], cr3[:, cc]).then_inc(*step())
                        after()
                        v.tensor_tensor(cb3[:, cc, 32:48], cr3[:, cc], cb3[:, cc, 16:32], ALU.subtract).then_inc(
                            *step("cb3", g))

                        def maxima(c):
                            n = g * C + c
                            halves = (n + 4) // 4
                            for k in range(halves):
                                keys = min(GT, (n + 1) * CT - k * GT)
                                after(("s3", n, k))
                                i = v.tensor_reduce(sm3[:, n, 3 + k:4 + k], psum("s3", n, k)[:, 0:keys], AX.X,
                                                    ALU.max, negate=True)
                                i.then_inc(*step())
                            after()
                            if halves == 1:
                                v.tensor_copy(sm3[:, n, 0:1], sm3[:, n, 3:4]).then_inc(*step("mx3", n))
                            else:
                                v.tensor_tensor(sm3[:, n, 0:1], sm3[:, n, 3:4], sm3[:, n, 4:5], ALU.min).then_inc(
                                    *step("mx3", n))

                        def sums(c):
                            n = g * C + c
                            halves = (n + 4) // 4
                            after(("e3", n, halves - 1))
                            s = sm3[:, n, 1:2]
                            if halves == 2:
                                v.tensor_tensor(s, s, sm3[:, n, 2:3], ALU.add).then_inc(*step())
                                after()
                            v.reciprocal(sm3[:, n, 5:6], s).then_inc(*step())
                            after()
                            keys = (n + 1) * CT
                            v.tensor_scalar(p3b[:, n % 2, 0:keys], p3b[:, n % 2, 0:keys], sm3[:, n, 5:6], None,
                                            ALU.mult).then_inc(*step("p3", n))
                        if g == 0:
                            norm(3, 1)
                        for c in range(C):
                            maxima(c)
                            sums(c)
                        for k in range(EP3 + 1):
                            after(("tg3", g, k))
                            v.scalar_tensor_tensor(h3[:, k % 2], tg3[:, k % 2], 1.0, psum("gate3", g, k)[:], ALU.add,
                                                   ALU.mult).then_inc(*step("hg3", g, k))
                            reached[("gate3", g, k, "read")] = reached[("hg3", g, k)]
                            needs = [("up3", g, k)]
                            if k >= 3:
                                needs.append(("dn3", g, k - 3))
                            elif g:
                                needs.append(("ff", 3, 0))
                            after(*needs)
                            o = hh3[:, k % 3]
                            v.scalar_tensor_tensor(o, h3[:, k % 2], 0.5, psum("up3", g, k)[:], ALU.mult,
                                                   ALU.mult).then_inc(*step(*(("hh3", g, k) if k == EP3 else
                                                                              ("up3", g, k, "read"))))
                            if k == EP3:
                                reached[("up3", g, k, "read")] = reached[("hh3", g, k)]
                            else:
                                after(("cbb3", g, k))
                                v.tensor_tensor(o, o, psum("cb3", g, k)[:], ALU.mult).then_inc(*step("hh3", g, k))
                                reached[("cb3", g, k, "read")] = reached[("hh3", g, k)]
                        merge(3, g, psum("ff", 3, g)[:], 0.0, psum("s", 3, g)[:], W3["bout"], True, True,
                              ("ff", 3, g))

                    for g in range(G):
                        norm(0, g)
                    for _ in zip_longest(*[layer0(g) for g in range(G)]):
                        pass
                    norm(1, 0)
                    now[0] = 1
                    for g in range(G):
                        layer1(g)
                    now[0] = 2
                    dve.wait_ge(ready["two"], 32)
                    for g in range(G):
                        layer2_rec(g)
                        layer2_att(g)
                    now[0] = 3
                    dve.wait_ge(ready["three"], 32)
                    for g in range(G):
                        layer3(g)

                @block.gpsimd
                def _(pool):
                    for g in range(G):
                        pool.wait_ge(*at("xi", g, 3))
                        pool.wait_ge(*at("bx", g))
                        nc.gpsimd.tensor_tensor(xi[:, 0, gs(g)], xi[:, 0, gs(g)], sr[:, 0], ALU.mult).then_inc(
                            *prog["gpsimd", 1].step())
                        nc.gpsimd.tensor_tensor(xi[:, 1, gs(g)], xi[:, 1, gs(g)], sr[:, 1], ALU.mult).then_inc(
                            *prog["gpsimd", 1].step("z", g))
                        reached[("zp", g)] = reached[("z", g)]

            nc.all_engine_barrier()
            for name, s in sems.items():
                if not name.startswith(("once", "loaded")):
                    nc.sync.sem_clear(s)
            nc.all_engine_barrier()
    return reached


def kernel(**inputs):
    import concourse.bacc as bacc
    from concourse.bass_utils import run_bass_kernel_spmd as run

    a = {k: np.asarray(v) for k, v in inputs.items()}

    def rows(w, p=P):
        return w.reshape(-1, p, w.shape[-1]).transpose(1, 0, 2).reshape(p, -1)

    def col(v, p=P):
        return v.reshape(-1, p).T

    def pack(pieces, spec):
        for piece, (name, n) in zip(pieces, spec):
            assert piece.shape[1] == n, (name, piece.shape, n)
        return np.concatenate(pieces, axis=1)

    p0 = pack([np.concatenate([a["L0_attn_w_q"], a["L0_attn_w_k"]]).T,
               np.concatenate([a["L0_attn_w_k"], a["L0_attn_w_v"], a["L0_ffn_W_gate"].T]).T,
               a["L0_ffn_W_shared"].T, a["L0_ffn_W_expert"].T, col(a["L0_ffn_bias"])], PACK0)
    mn = a["L0_attn_memory_norm"]
    s0 = pack([np.concatenate([a["L0_attn_memory"], np.repeat(mn[:, None], DM, 1)], 1), np.repeat(mn[None], DM, 0),
               np.repeat(a["L0_attn_gate"][None], DM, 0), a["L0_attn_w_o"].T], SMALL0)
    p1 = pack([a["L1_attn_W_in"], rows(a["L1_attn_W_dt"]), rows(a["L1_attn_W_xp"]), rows(a["L1_attn_W_out"]),
               a["L1_ffn_router_w"].T, a["L1_ffn_sw1"], rows(a["L1_ffn_sw2"])], PACK1)
    b1 = pack([col(a["L1_attn_b_in"]),
               col(a["L1_attn_b_dt"]), col(a["L1_attn_b_out"]), col(a["L1_attn_D"]), col(a["L1_ffn_norm_weight"]),
               col(a["L1_ffn_sb1"]), col(a["L1_ffn_sb2"]), col(a["L1_ffn_eb1"])], BIAS1)
    s1 = pack([col(a["L1_attn_A_log"], ST), col(a["L1_attn_b_xp"], ST)], SMALL1)
    eb2 = a["L1_ffn_eb2"]
    ew1 = a["L1_ffn_ew1"].transpose(1, 0, 2)
    ew2 = a["L1_ffn_ew2"].reshape(E1, HJ, P, D).transpose(2, 0, 1, 3)
    wkv = np.concatenate([a["L2_attn_w_K"], a["L2_attn_w_V"]], 1).transpose(2, 0, 1).reshape(D, -1)
    init = np.concatenate([a["L2_attn_init_K_rec"], a["L2_attn_init_V_rec"]], 2).transpose(2, 1, 0).reshape(P, -1)
    p2 = pack([a["L2_attn_w_G"].reshape(NH * NE, D).T, wkv, a["L2_attn_w_Q"].reshape(NH * DK, D).T,
               rows(a["L2_attn_w_O"]), init, a["L2_ffn_W_r"].T, a["L2_ffn_W_k"].T, a["L2_ffn_W_v"].T,
               col(a["L2_ffn_mu_r"]), col(a["L2_ffn_mu_k"])], PACK2)
    bg = a["L2_attn_b_G"].reshape(NH * NE, 1)
    qkv = a["L3_attn_w_qkv"]
    p3 = pack([qkv[:2 * DK].T, qkv[2 * DK:].T, col(a["L3_attn_b_out"]), a["L3_ffn_router_w"].T,
               np.repeat(a["L3_ffn_router_bias"][None], P, 0),
               a["L3_ffn_gate_proj"].transpose(1, 0, 2).reshape(D, -1),
               a["L3_ffn_up_proj"].transpose(1, 0, 2).reshape(D, -1),
               rows(a["L3_ffn_down_proj"].reshape(E3 * H3, D)),
               a["L3_ffn_sh_gate"].T, a["L3_ffn_sh_up"].T, a["L3_ffn_sh_down"].T], PACK3)
    wout3 = a["L3_attn_w_out"].T
    x = a["L0_attn_hidden_states"].transpose(0, 2, 1)
    cf, cb = constants()
    given = dict(x=x, cf=cf, cb=cb, p0=p0, s0=s0, p1=p1, b1=b1, s1=s1, eb2=eb2, ew1=ew1, ew2=ew2, p2=p2, bg=bg, p3=p3, wout3=wout3)
    given = {f"in_{k}": np.ascontiguousarray(v) for k, v in given.items()}

    def build(known):
        nc = bacc.Bacc("TRN2", target_bir_lowering=False, num_devices=1)
        args = [nc.dram_tensor(k, v.shape, mybir.dt.from_np(v.dtype), kind="ExternalInput").ap() for k, v in given.items()]
        args.append(nc.dram_tensor("out_x", (B, P, T), F32, kind="ExternalOutput").ap())
        return nc, four_layers(nc, known, *args)

    _, known = build({})
    nc, _ = build(known)
    r = run(nc, [given], core_ids=[0])
    return np.ascontiguousarray(r.results[0]["out_x"].transpose(0, 2, 1))
```

```python
from contextlib import ExitStack

import numpy as np

import concourse.bass as bass
from concourse import mybir

ALU = mybir.AluOpType
ACT = mybir.ActivationFunctionType
AX = mybir.AxisListType
F32 = mybir.dt.float32
BF16 = mybir.dt.bfloat16
U32 = mybir.dt.uint32

B, T, D = 2, 1024, 128
P = 128
GT = 512
G = T // GT
CT = 128
C = GT // CT
DM = 32
EPS_MEM = 1e-6
EPS = 1e-5
EPS_RMS = 1e-8
NGATE = 7
KVG = 2 * DM + NGATE
ST = 64
E1, H1 = 8, 512
HJ = H1 // P
NH, NE, L, DK = 8, 4, 32, 64
NB = T // L
GB = GT // L
E3, H3 = 16, 64
EP3 = E3 // 2
NEG = -1e30
VT_JOBS = [[range(0, 8), range(8, 16), range(16, 17)], [range(17, 25), range(25, 33)]]
ROUTE3_STEPS = [{6: 1, 7: 1, 9: 2, 10: 3}, {0: 3, 1: 4}]
NORM0, VAR0 = {0: 0, 3: 1}, {5: 0, 6: 1}
HID_UNDER = 4096
ROOM = 24200

PACK0 = [("wqk", 2 * DM), ("wkvg", KVG), ("wsh", D), ("wex", D), ("bias", 1), ("mnorm", DM),
         ("gate", 1)]
SMALL0 = [("mem", DM + 1), ("wo", D)]
PACK1 = [("win", 512), ("wdt", 2 * D), ("wxp", 2 * ST), ("wout", 2 * D), ("rw", E1), ("sw1", H1), ("sw2", HJ * D)]
BIAS1 = [("bin", 4), ("bdt", 1), ("bout", 1), ("dskip", 1), ("wn", 1), ("sb1", HJ), ("sb2", 1), ("eb1", E1 * HJ)]
SMALL1 = [("alog", 1), ("bxp", 1)]
PACK2 = [("wg", 32), ("wkv", NH * 128), ("wq", NH * DK), ("wo", 4 * D), ("init", NE * L),
         ("wr", D), ("wk", D), ("wv", D), ("mur", 1), ("muk", 1)]
PACK3 = [("wqk", 2 * DK), ("wv", DK), ("bout", 1), ("rw", E3), ("rb", E3), ("gate", E3 * H3), ("up", E3 * H3),
         ("down", EP3 * D), ("shg", D), ("shu", D), ("shd", D)]


CONST = [("ident", P), ("center", P), ("mean", P), ("causal", P), ("ones", P), ("iota", E3)]
CONSTB = [("ident", P), ("above", P), ("sel_q", P), ("cage", NE * 2 * L), ("sel_p", EP3 * P), ("sel_e", NE),
          ("sel_he", NH * NE)]


def constants():
    k = np.arange(P)
    eye = np.eye(P, dtype=np.float32)
    c = dict(ident=eye, center=eye - np.float32(1 / D), mean=np.full((P, P), 1 / D, np.float32),
             causal=(k[:, None] <= k[None]).astype(np.float32), ones=np.ones((P, P), np.float32),
             iota=np.repeat(np.arange(E3, dtype=np.float32)[None], P, 0))
    q, key = np.arange(L), np.arange(2 * L)
    cage = np.zeros((P, 2 * L), np.float32)
    cage[:L] = np.where((key[None] > q[:, None]) & (key[None] <= q[:, None] + L), 0, NEG)
    col = np.arange(P)
    b = dict(ident=eye, above=np.where(k[None] > k[:, None], np.float32(NEG), np.float32(0)),
             sel_q=(k[:, None] == col[None] % L).astype(np.float32),
             cage=np.repeat(cage, NE, 1),
             sel_p=(k[:, None, None] % 16 == 2 * np.arange(EP3)[None, :, None] + col[None, None] // H3).reshape(P, -1),
             sel_e=k[:, None] % NE == np.arange(NE)[None],
             sel_he=k[:, None] % 32 == np.arange(32)[None])
    return (np.concatenate([c[n].astype(np.float32) for n, _ in CONST], 1),
            np.concatenate([b[n].astype(mybir.dt.np(BF16)) for n, _ in CONSTB], 1))


def columns(pack):
    at, out = 0, {}
    for name, n in pack:
        out[name] = (at, at + n)
        at += n
    return out, at


class Steps:

    def __init__(self, sem, reached):
        self.sem, self.count, self.reached = sem, 0, reached

    def step(self, *milestone, by=1):
        self.count += by
        if milestone:
            self.reached[milestone] = (self.sem.name, self.count)
        return self.sem, by


def four_layers(nc, known, x_in, cf, cb, p0, s0, p1, b1, s1, eb2, ew1, ew2, p2, bg, p3, wout3, out):
    reached = {}
    with ExitStack() as ctx:
        def sb(name, shape, dt=F32):
            return ctx.enter_context(nc.sbuf_tensor(name, shape, dt))

        sems = {}

        def sem(name):
            sems[name] = ctx.enter_context(nc.semaphore(name))
            return sems[name]

        def at(*milestone):
            name, value = known.get(milestone, ("next_x", 16))
            return sems[name], value

        def packed(tile, pack):
            where, _ = columns(pack)
            return {name: tile[:, a:b] for name, (a, b) in where.items()}

        w0t = sb("w0", [P, columns(PACK0)[1]])
        w0s = sb("w0s", [DM, columns(SMALL0)[1]])
        w1t = sb("w1", [P, columns(PACK1)[1]])
        w1b = sb("w1b", [P, columns(BIAS1)[1]])
        w1s = sb("w1s", [ST, 2])
        w_eb2 = sb("w_eb2", [E1, D])
        w_ew1 = sb("w_ew1", [P, E1, H1])
        w_ew2 = sb("w_ew2", [P, E1, HJ, D])
        w2t = sb("w2", [P, columns(PACK2)[1]])
        w_bg = sb("w_bg", [32, 1])
        w3t = sb("w3", [P, columns(PACK3)[1]])
        w_out3 = sb("w_out3", [DK, D])
        W0, S0, S1 = packed(w0t, PACK0), packed(w0s, SMALL0), packed(w1s, SMALL1)
        W1 = packed(w1t, PACK1) | packed(w1b, BIAS1)
        W2, W3 = packed(w2t, PACK2), packed(w3t, PACK3)

        const = sb("const", [P, columns(CONST)[1]])
        constb = sb("constb", [P, columns(CONSTB)[1]], BF16)
        K, KB = packed(const, CONST), packed(constb, CONSTB)
        ident = K["ident"]
        center = K["center"]
        mean = K["mean"]
        ones = K["ones"][0:ST]
        causal = K["causal"]
        iota8 = K["iota"]
        identb = KB["ident"]
        above = KB["above"]
        sel_q = KB["sel_q"][0:L]
        cage = KB["cage"][0:L]
        sel_p = KB["sel_p"][0:48].rearrange("p (a b) -> p a b", b=P)
        sel_e = KB["sel_e"][0:96]
        sel_he = KB["sel_he"][0:96]
        flag = sb("flag", [P, 4])
        half0 = sb("half0", [P, 1])
        half1 = sb("half1", [P, 5])
        neg_a = sb("neg_a", [ST, 1])
        neg_bg = sb("neg_bg", [32, 1])
        called = sb("called", [P, 1])

        x0 = sb("x0", [P, T])
        x = sb("x", [P, T])
        xn_a = sb("xn_a", [P, T + 1])
        xn_b = sb("xn_b", [P, T])
        xn = [xn_a[:, 1:T + 1], xn_b[:, :], xn_a[:, 1:T + 1], xn_b[:, :]]
        sq = sb("sq", [P, 2, GT])
        rs = sb("rs", [P, 2, GT])
        hz = sb("hz", [P, GT])
        tz = sb("tz", [P, GT])
        room = sb("arena", [P, ROOM])
        used, ends = [0], []

        def take(shape, parts=P, dt=F32):
            n = int(np.prod(shape))
            words = n if dt == F32 or dt == U32 else (n + 1) // 2
            v = room[0:parts, used[0]:used[0] + words]
            used[0] += words
            ends.append(used[0])
            if dt != F32:
                v = v.bitcast(dt)
            names = "abcd"[:len(shape)]
            if len(shape) == 1:
                return v
            return v.rearrange(f"p ({' '.join(names)}) -> p {' '.join(names)}", **dict(zip(names, shape)))

        used[0] = 0
        xi = take([2, T])
        sr = take([2, GT])
        hx = take([2, GT])
        tx = take([2, GT])
        dab = take([GT])
        dpos = take([GT])
        decay = take([T], ST)
        bx = take([T], ST)
        states = take([T], ST)
        ssum = take([GT])
        s1out = take([GT])
        rs2 = s1out
        xd = take([GT])
        nm = take([T])
        acc = take([C, P])
        pr = take([2 * C, E1])
        top1 = take([2 * C, 8])
        idx1 = take([2 * C, 8], dt=U32)
        idf1 = take([2 * C, 8])
        wsm1 = take([2 * C, 4])
        oh1 = take([2, 2 * C, E1])
        cmb1 = take([2 * C, E1])
        cbt1 = take([2, GT], E1)
        hid = take([2, HJ, GT])
        L1_END = used[0]

        used[0] -= HID_UNDER
        ek = take([2, GT], ST)
        sgq = take([T], DM)
        sgk = take([T], DM)
        et = take([2, C, DM])
        ktok = take([2 * C, DM])
        vtok0 = sb("vtok0", [P, 2 * C, 2 * DM])
        logit = sb("logit", [P, 2 * C, 8])
        att = take([2, C, P])
        state = sb("state", [DM, 2 * C + 1, 2, DM + 1])
        den = take([2, C, 2])
        parts = take([2, C, 2, DM])
        ctok = take([2, C, DM])
        comb0 = take([2, GT], DM)
        tz0 = take([2, GT])
        gz0 = take([2, GT])
        top = take([2 * C, 8])
        gw = take([2 * C, 6])
        ysc = take([2, C, P])

        used[0] = 0
        abc = take([NE, GB, L + 1])
        spare_a = used[0]
        rec = take([NB + 1, L + 1, NE])
        vt = take([NB + 1, DK])
        spare_b = used[0]
        qf = take([GB, NH, L], DK)
        prob = take([4, 2, 4 * 2 * L])
        pt = take([3, GT])
        smx = take([4, 6])
        spare_c = used[0]
        dx = take([GT])
        xr = take([GT])
        kr = dx
        tr = take([GT])
        assert used[0] <= L1_END
        used[0] = L1_END
        gfm = take([2, GT], 32)
        gb = take([2, GT], 32, BF16)
        g3 = take([GT], 96, BF16)
        xs = take([3, GT])
        spare_d = used[0]
        yt = take([4, GT])
        xk = take([GT])
        of = xk

        used[0] = 0
        lg3 = take([2 * C, E3])
        top3 = take([2 * C, 8])
        idx3 = take([2 * C, 8], dt=U32)
        idf3 = take([2 * C, 8])
        w3s = take([2 * C, 4])
        oh3 = take([2, 2 * C, E3])
        cm3 = take([2 * C, E3])
        cb3 = take([2 * C, 48], dt=BF16)
        cr3 = take([2 * C, E3])
        ct3 = take([2, GT], 48, BF16)
        assert used[0] <= spare_a
        used[0] = L1_END
        q3 = take([T], DK)
        k3 = take([T], DK)
        v3 = take([2 * C, DK])
        assert used[0] <= spare_d
        used[0] = spare_b
        tg3 = take([2, GT])
        h3 = take([2, GT])
        hh3 = take([3, GT])
        sm3 = take([2 * C, 8])
        s3h = take([GT])
        used[0] = spare_a
        p3b = take([2, T])
        pt3 = take([2, C, P])
        ot3 = take([2, C, DK])
        o3 = take([2, GT], DK)
        assert used[0] <= spare_b, (used[0], spare_b)

        assert max(ends) <= ROOM, ends
        bank = [ctx.enter_context(nc.psum_tensor(f"bank{i}", [P, GT], F32)) for i in range(8)]

        ready = {n: sem(f"loaded_{n}") for n in ("input", "first", "one", "experts", "two", "three")}
        next_x, stores = sem("next_x"), sem("stores")
        once = Steps(sem("once"), reached)
        once_p = Steps(sem("once_tensor"), reached)
        once_v, once_a = Steps(sem("once_vector"), reached), Steps(sem("once_scalar"), reached)
        prog = {(e, l): Steps(sem(f"l{l}_{e}"), reached) for l in range(4)
                for e in ("tensor", "vector", "scalar", "gpsimd")}

        def gs(g):
            return slice(g * GT, (g + 1) * GT)

        def cs(c):
            return slice(c * CT, (c + 1) * CT)

        with nc.Block() as block:
            @block.sync
            def _(sp):
                xv = x_in.rearrange("b p t -> (b p) t")
                for name, pieces in (
                        ("input", ((const[:], cf), (x0[:], xv[0:P]))),
                        ("first", ((w0t[:], p0), (w0s[:], s0), (w1b[:], b1), (w1s[:], s1), (w_bg[:], bg))),
                        ("one", ((w1t[:], p1), (w_eb2[:], eb2))),
                        ("experts", ((w_ew1[:], ew1), (w_ew2[:], ew2))),
                        ("three", ((w3t[:], p3), (w_out3[:], wout3)))):
                    for dst, src in pieces:
                        sp.dma_start(dst, src).then_inc(ready[name], 16)
                sp.wait_ge(ready["first"], 16 * 5)

            @block.tensor
            def _(pe):
                pe.wait_ge(ready["input"], 16 * 2)
                for g in range(G):
                    nc.tensor.matmul(bank[g][:], center[:], x0[:, gs(g)], start=True, stop=True).then_inc(
                        *once_p.step("first xc", g))
                for g in range(G):
                    pe.wait_ge(*at("first sq", g))
                    nc.tensor.matmul(bank[G + g][:], mean[:], sq[:, g], start=True, stop=True).then_inc(
                        *once_p.step("first var", g))

            @block.gpsimd
            def _(pool):
                pool.dma_start(constb[:], cb).then_inc(ready["two"], 16)
                pool.dma_start(w2t[:], p2).then_inc(ready["two"], 16)
                for tile, v in ((xn_a, 0.0), (vtok0, 1.0), (logit, -3e38), (state, 0.0)):
                    nc.gpsimd.memset(tile[:], v).then_inc(*once.step())
                pool.wait_ge(once.sem, once.count)

            @block.vector
            def _(dve):
                v = once_v
                dve.wait_ge(once.sem, 4)
                for g in range(G):
                    dve.wait_ge(*at("first rs", g))
                    nc.vector.tensor_tensor(xn[0][:, gs(g)], bank[g][:], rs[:, g], ALU.mult).then_inc(*v.step())
                dve.wait_ge(ready["first"], 16 * 5)

                def done():
                    dve.wait_ge(v.sem, v.count)
                nc.vector.tensor_copy(state[:, :, 1], S0["mem"].rearrange("p (a d) -> p a d", a=1).to_broadcast(
                    [DM, 2 * C + 1, DM + 1])).then_inc(*v.step())
                nc.vector.tensor_scalar(half0[:], W0["bias"], 0.5, None, ALU.mult).then_inc(*v.step())
                nc.vector.tensor_scalar(half1[:, 0:4], W1["bin"], 0.5, None, ALU.mult).then_inc(*v.step())
                nc.vector.tensor_scalar(half1[:, 4:5], W1["sb2"], 0.5, None, ALU.mult).then_inc(*v.step())
                nc.vector.tensor_scalar(neg_bg[:], w_bg[:], -1.0, None, ALU.mult).then_inc(*v.step())
                nc.vector.tensor_reduce(flag[:, 2:3], W0["mnorm"], AX.X, ALU.add).then_inc(*v.step())
                done()
                nc.vector.tensor_scalar(flag[:, 2:3], flag[:, 2:3], EPS_MEM, None, ALU.is_ge).then_inc(*v.step())
                dve.wait_ge(*at("gate exp"))
                nc.vector.tensor_scalar(flag[:, 3:4], flag[:, 3:4], 1.0, None, ALU.add).then_inc(*v.step())
                done()
                nc.vector.reciprocal(flag[:, 3:4], flag[:, 3:4]).then_inc(*v.step())
                done()
                nc.vector.tensor_tensor(flag[:, 1:2], flag[:, 3:4], flag[:, 2:3], ALU.mult).then_inc(*v.step())
                nc.vector.tensor_scalar(flag[:, 0:1], flag[:, 3:4], -1.0, 1.0, ALU.mult, ALU.add).then_inc(*v.step())
                dve.wait_ge(*at("a exp"))
                nc.vector.tensor_scalar(neg_a[:], neg_a[:], -1.0, None, ALU.mult).then_inc(*v.step())

            @block.scalar
            def _(act):
                for g in range(G):
                    act.wait_ge(*at("first xc", g))
                    nc.scalar.activation(sq[:, g], bank[g][:], ACT.Square).then_inc(*once_a.step("first sq", g))
                for g in range(G):
                    act.wait_ge(*at("first var", g))
                    nc.scalar.activation(rs[:, g], bank[G + g][:], ACT.Ln, bias=EPS).then_inc(*once_a.step())
                for g in range(G):
                    act.wait_ge(once_a.sem, once_a.count)
                    nc.scalar.activation(rs[:, g], rs[:, g], ACT.Exp, scale=-0.5).then_inc(*once_a.step("first rs", g))
                act.wait_ge(ready["first"], 16 * 5)
                nc.scalar.activation(flag[:, 3:4], W0["gate"], ACT.Exp, scale=-1.0).then_inc(*once_a.step("gate exp"))
                nc.scalar.activation(neg_a[:], S1["alog"], ACT.Exp).then_inc(*once_a.step("a exp"))

        with nc.Fori(0, B) as b:
            with nc.Block(no_gpsimd_drain=True) as block:

                rings = {"quick": [0, 1, 2, 3], "slow": [4, 5, 6, 7]}
                turn = {"quick": 0, "slow": 0}
                owner = {}

                def side_by_side(layer):
                    left = {g: layer(g) for g in range(G)}
                    while left:
                        for g in list(left):
                            if next(left[g], "end") == "end":
                                del left[g]

                @block.sync
                def _(sp):
                    xv = x_in.rearrange("b p t -> (b p) t")
                    ov = out.rearrange("b p t -> (b p) t")
                    sp.wait_ge(*at("x", 1, G - 1))
                    sp.dma_start(x0[:], xv[bass.ds((B - 1 - b) * P, P)]).then_inc(next_x, 16)
                    for g in range(G):
                        sp.wait_ge(*at("x out", g))
                        sp.dma_start(ov[bass.ds(b * P, P), gs(g)], x[:, gs(g)]).then_inc(stores, 16)
                    sp.wait_ge(stores, 16 * G)
                    sp.wait_ge(next_x, 16)

                @block.tensor
                def _(pe):
                    now = [0]
                    growing = set()

                    def step(*m):
                        growing.discard(m)
                        return prog["tensor", now[0]].step(*m)

                    def fresh(ring, *job):
                        while True:
                            i = rings[ring][turn[ring] % 4]
                            turn[ring] += 1
                            if owner.get(i) not in growing:
                                break
                        if job[0] in ("ff", "s", "o3"):
                            growing.add(job)
                        if i in owner:
                            pe.wait_ge(*at(*owner[i], "read"))
                        owner[i] = job
                        reached[job + ("bank",)] = i
                        return bank[i]

                    def mm(o, lhsT, rhs, start=True, stop=True):
                        return nc.tensor.matmul(o, lhsT, rhs, start=start, stop=stop, skip_group_check=True)

                    def norm(l, g):
                        pe.wait_ge(*at("x", l, g) if l else (next_x, 16))
                        src = x if l else x0
                        mm(fresh("slow", "xc", l, g)[:], center[:], src[:, gs(g)]).then_inc(*step("xc", l, g))

                    def variance(l, g):
                        pe.wait_ge(*at("sq", l, g))
                        mm(fresh("quick", "var", l, g)[:], mean[:], sq[:, g]).then_inc(*step("var", l, g))

                    def head(l, g):
                        norm(l, g)
                        variance(l, g)

                    def layer0(g):
                        xg = xn[0][:, gs(g)]
                        o = fresh("quick", "qk0", g)
                        mm(o[0:2 * DM], W0["wqk"], xg).then_inc(*step("qk0", g))
                        o = fresh("quick", "kvg0", g)
                        for c in range(C):
                            i = mm(o[:, c * KVG:(c + 1) * KVG], xg[:, cs(c)], W0["wkvg"])
                        i.then_inc(*step("kvg0", g))
                        ff = fresh("slow", "ff", 0, g)
                        mm(ff[:], W0["wsh"], xg, stop=False)
                        o = fresh("quick", "y0", g)
                        for c in range(C):
                            i = mm(o[:, cs(c)], xg[:, cs(c)], W0["wex"])
                        i.then_inc(*step("y0", g))
                        yield
                        o = fresh("slow", "kv0", g)
                        pe.wait_ge(*at("vtok0", g))
                        pe.wait_ge(*at("ktok0", g))
                        for c in range(C):
                            i = mm(o[0:DM, c * 64:c * 64 + 64], ktok[:, g * C + c], vtok0[:, g * C + c])
                        i.then_inc(*step("kv0", g))
                        yield
                        o = fresh("quick", "a0", g)
                        pe.wait_ge(*at("sgk", g))
                        for c in range(C):
                            t = slice(g * GT + c * CT, g * GT + (c + 1) * CT)
                            i = mm(o[:, cs(c)], sgk[:, t], sgq[:, t])
                        i.then_inc(*step("a0", g))
                        yield
                        pe.wait_ge(*at("ysc", g))
                        for c in range(C):
                            i = mm(ff[:, cs(c)], ysc[:, g, c], ident[:], start=False, stop=c == C - 1)
                        i.then_inc(*step("ff", 0, g))
                        yield
                        o = fresh("quick", "num0", g)
                        pe.wait_ge(*at("att0", g))
                        pe.wait_ge(*at("state", g))
                        for c in range(C):
                            t = slice(g * GT + c * CT, g * GT + (c + 1) * CT)
                            local = 2 * c * (DM + 1)
                            mm(o[:, local:local + 2 * (DM + 1)], sgq[:, t],
                               state[:, g * C + c].rearrange("p k d -> p (k d)"), stop=False)
                            i = mm(o[:, local:local + DM + 1], att[:, g, c], vtok0[:, g * C + c, 0:DM + 1], start=False)
                        i.then_inc(*step("num0", g))
                        yield
                        o = fresh("quick", "ct0", g)
                        pe.wait_ge(*at("ctok", g))
                        for c in range(C):
                            i = nc.tensor.transpose(o[0:DM, cs(c)], ctok[:, g, c], ident[:])
                        i.then_inc(*step("ct0", g))
                        yield
                        o = fresh("slow", "s", 0, g)
                        pe.wait_ge(*at("comb0", g))
                        mm(o[:], S0["wo"], comb0[:, g]).then_inc(*step("s", 0, g))

                    def layer1(g):
                        xg = xn[1][:, gs(g)]
                        o = fresh("quick", "rt1", g)
                        pe.wait_ge(*at("nm", g))
                        for c in range(C):
                            t = slice(g * GT + c * CT, g * GT + (c + 1) * CT)
                            i = mm(o[:, c * E1:(c + 1) * E1], nm[:, t], W1["rw"])
                        i.then_inc(*step("rt1", g))
                        pe.wait_ge(*at("xn", 1, g))
                        for j in range(4):
                            mm(fresh("quick", "xr", g, j)[:], W1["win"][:, cs(j)], xg).then_inc(*step("xr", g, j))
                        if g == 0:
                            pe.wait_ge(ready["experts"], 32)

                        def first(e):
                            for j in range(HJ):
                                w = W1["sw1"][:, cs(j)] if e == E1 else w_ew1[:, e, cs(j)]
                                mm(fresh("quick", "h1", g, e, j)[:], w, nm[:, gs(g)]).then_inc(*step("h1", g, e, j))

                        def second(e):
                            h = hid[:, e % 2]
                            if e == E1:
                                pe.wait_ge(*at("hid", g, e, 2))
                                pe.wait_ge(*at("hid", g, e, 3))
                                for j in range(HJ):
                                    i = mm(ff[:], W1["sw2"][:, cs(j)], h[:, j], start=False, stop=False)
                                i.then_inc(*step("eo", g, e))
                                return
                            o = fresh("slow", "eo", g, e)
                            pe.wait_ge(*at("hid", g, e, 2))
                            pe.wait_ge(*at("hid", g, e, 3))
                            for c in range(C):
                                for j in range(HJ):
                                    i = mm(o[:, cs(c)], h[:, j, cs(c)], w_ew2[:, e, j], start=j == 0,
                                           stop=j == HJ - 1)
                            i.then_inc(*step("eo", g, e))

                        first(0)
                        o = fresh("quick", "dt", g)
                        pe.wait_ge(*at("xi", g, 1))
                        for j in range(2):
                            i = mm(o[:], W1["wdt"][:, cs(j)], xi[:, j, gs(g)], start=j == 0, stop=j == 1)
                        i.then_inc(*step("dt", g))
                        o = fresh("quick", "bx", g)
                        for j in range(2):
                            i = mm(o[0:ST], W1["wxp"][:, j * ST:(j + 1) * ST], xi[:, j, gs(g)], start=j == 0,
                                   stop=j == 1)
                        i.then_inc(*step("bx", g))
                        first(1)
                        ff = fresh("slow", "ff", 1, g)
                        coming = (1, 1) if g == 0 else (2, 0)
                        norm(*coming)
                        o = fresh("quick", "md", g)
                        pe.wait_ge(*at("delta", g))
                        mm(o[0:ST], mean[:, 0:ST], dab[:]).then_inc(*step("md", g))
                        second(0)
                        first(2)
                        variance(*coming)
                        second(1)
                        o = fresh("quick", "ss", g)
                        pe.wait_ge(*at("states", g))
                        mm(o[:], ones[:], states[:, gs(g)]).then_inc(*step("ss", g))
                        o = fresh("quick", "cbt", g)
                        pe.wait_ge(*at("cmb1", g))
                        for c in range(C):
                            i = nc.tensor.transpose(o[0:E1, cs(c)], cmb1[:, g * C + c], ident[:])
                        i.then_inc(*step("cbt", g))
                        first(3)
                        pe.wait_ge(*at("cbt_s", g))
                        mm(ff[:], w_eb2[:], cbt1[:, g], stop=False)
                        second(2)
                        o = fresh("quick", "wo1", g)
                        pe.wait_ge(*at("z", g))
                        for j in range(2):
                            i = mm(o[:], W1["wout"][:, cs(j)], xi[:, j, gs(g)], start=j == 0, stop=j == 1)
                        i.then_inc(*step("wo1", g))
                        for e in range(4, E1 + 1):
                            first(e)
                            if g and e == 4:
                                gates(0)
                            second(e - 1)
                        second(E1)
                        pe.wait_ge(*at("acc", g, E1 - 1))
                        for c in range(C):
                            i = mm(ff[:, cs(c)], acc[:, c], ident[:], start=False, stop=c == C - 1)
                        i.then_inc(*step("ff", 1, g))

                    def gates(g):
                        if g == 0:
                            pe.wait_ge(ready["two"], 32)
                        pe.wait_ge(*at("xn", 2, g))
                        mm(fresh("quick", "gt", g)[0:32], W2["wg"], xn[2][:, gs(g)]).then_inc(*step("gt", g))

                    def layer2_rec(g):
                        xg = xn[2][:, gs(g)]
                        def query(j):
                            mm(fresh("quick", "q2", g, j)[:], W2["wq"][:, cs(j)], xg).then_inc(*step("q2", g, j))

                        def decays(e):
                            mm(fresh("quick", "ga", g, e)[:], sel_e[:, e:e + 1].to_broadcast([96, P]), g3[:]).then_inc(
                                *step("ga", g, e))
                        pe.wait_ge(*at("g3", g))
                        accs = {}

                        def spread(n):
                            he = n % NH * NE + n // NH
                            mm(fresh("quick", "gb", g, n)[:], sel_he[:, he:he + 1].to_broadcast([96, P]), g3[:]).then_inc(
                                *step("gb", g, n))

                        def project(n):
                            e, h = n // NH, n % NH
                            if h == 0:
                                accs[e] = fresh("slow", "gkv", g, e)
                            pe.wait_ge(*at("xs", g, n))
                            i = mm(accs[e][:], W2["wkv"][:, h * 128:(h + 1) * 128], xs[:, n % 3], start=h == 0,
                                   stop=h == NH - 1)
                            i.then_inc(*step("gkv", g, n))
                        for n in range(NE * NH + 2):
                            if n == NE * NH // 2:
                                norm(*((2, 1) if g == 0 else (3, 0)))
                            if n == NE * NH // 2 + 3:
                                variance(*((2, 1) if g == 0 else (3, 0)))
                            if n < NE * NH // 2 and n % 2 == 0:
                                (decays if n % 4 == 0 else query)(n // 4)
                            if n < NE * NH:
                                spread(n)
                            if n >= 2:
                                project(n - 2)

                    def layer2_att(g):
                        pe.wait_ge(*at("xk", g))
                        mm(fresh("quick", "r2", g)[:], W2["wr"], xr[:]).then_inc(*step("r2", g))
                        mm(fresh("quick", "k2", g)[:], W2["wk"], xk[:]).then_inc(*step("k2", g))
                        for n, blocks in enumerate(VT_JOBS[g]):
                            o = fresh("quick", "vt", g, n)
                            pe.wait_ge(*at("rec", g, NE - 1))
                            for k, blk in enumerate(blocks):
                                src = rec[64:128, blk, 1:L + 1].rearrange("p c e -> p (c e)")
                                i = nc.tensor.transpose(o[:, k * DK:(k + 1) * DK], src, ident[64:128, 64:128])
                            i.then_inc(*step("vt", g, n))
                        pv_bank = {}

                        def score(l):
                            lb = g * GB + l
                            o = fresh("quick", "s2", g, l)
                            mm(o[:].rearrange("p (a b) -> p a b", a=2), sel_q[:],
                               cage[:].rearrange("p (a b) -> p a b", a=1).to_broadcast([L, 2, NE * 2 * L]), stop=False)
                            if l == 0:
                                pe.wait_ge(*at("qf", g, 3))
                            for hg in range(2):
                                i = mm(o[:, hg * 256:hg * 256 + 256],
                                       qf[:, l, 4 * hg:4 * hg + 4].rearrange("p h q -> p (h q)"),
                                       rec[0:64, lb:lb + 2, 1:L + 1].rearrange("p b c e -> p b (c e)"),
                                       start=False, stop=hg == 1)
                            i.then_inc(*step("s2", g, l))

                        def turned(l):
                            o = fresh("quick", "pt", g, l)
                            pe.wait_ge(*at("prob", g, l))
                            for blk in range(2):
                                for hg in range(2):
                                    k = (blk * 2 + hg) * P
                                    i = nc.tensor.transpose(o[:, k:k + P], prob[:, l % 4, hg, blk * P:(blk + 1) * P],
                                                            ident[:])
                            i.then_inc(*step("pt", g, l))

                        def value(l):
                            if l % 2 == 0:
                                pv_bank[0] = fresh("slow", "pv", g, l // 2)
                                if l == 0:
                                    pe.wait_ge(*at("vt_s", g, len(VT_JOBS[g]) - 1))
                            o = pv_bank[0][0:DK, (l % 2) * 256:(l % 2) * 256 + 256]
                            pe.wait_ge(*at("pt_s", g, l))
                            for blk in range(2):
                                i = mm(o, vt[:, g * GB + l + blk], pt[:, l % 3, blk * 256:(blk + 1) * 256],
                                       start=blk == 0, stop=blk == 1)
                            i.then_inc(*step("pv", g, l))

                        def project(half):
                            if half == 0:
                                pv_bank[1] = fresh("slow", "s", 2, g)
                            t = slice(half * GT // 2, (half + 1) * GT // 2)
                            pe.wait_ge(*at("yt", g, 4 * half + 3))
                            for j in range(4):
                                i = mm(pv_bank[1][:, t], W2["wo"][:, cs(j)], yt[:, j, t], start=j == 0, stop=j == 3)
                            i.then_inc(*(step("s", 2, g) if half else step()))
                        entry = entry3(0)
                        for l in range(GB + 7):
                            if l == 2:
                                o = fresh("slow", "v2", g)
                                pe.wait_ge(*at("kr", g))
                                mm(o[:], W2["wv"], kr[:]).then_inc(*step("v2", g))
                            if l == 6 and g == 0:
                                gates(1)
                            if l >= 6 and g == 1:
                                next(entry, None)
                            if l < GB:
                                score(l)
                            if 3 <= l < GB + 3:
                                turned(l - 3)
                            if 5 <= l < GB + 5:
                                value(l - 5)
                            if l == 15 or l == GB + 6:
                                project(l // 18)

                    def entry3(g):
                        xg = xn[3][:, gs(g)]
                        if g == 0:
                            pe.wait_ge(ready["three"], 32)
                        pe.wait_ge(*at("xn", 3, g))
                        o = fresh("quick", "rt3", g)
                        for c in range(C):
                            i = mm(o[:, c * E3:(c + 1) * E3], xg[:, cs(c)], W3["rw"])
                        i.then_inc(*step("rt3", g))
                        yield
                        mm(fresh("quick", "qk3", g)[:], W3["wqk"], xg).then_inc(*step("qk3", g))
                        yield
                        o = fresh("quick", "v3", g)
                        for c in range(C):
                            i = mm(o[:, c * DK:(c + 1) * DK], xg[:, cs(c)], W3["wv"])
                        i.then_inc(*step("v3", g))

                    def layer3(g):
                        xg = xn[3][:, gs(g)]

                        def score(c):
                            n = g * C + c
                            halves = (n + 4) // 4
                            pe.wait_ge(*at("k3", g))
                            for k in range(halves):
                                keys = min(GT, (n + 1) * CT - k * GT)
                                o = fresh("quick", "s3", n, k)
                                last = k == halves - 1
                                i = mm(o[:, 0:keys], q3[:, n * CT:(n + 1) * CT], k3[:, k * GT:k * GT + keys],
                                       stop=not last)
                                if last:
                                    i = mm(o[:, keys - CT:keys], identb[:], above[:], start=False)
                                i.then_inc(*step("s3", n, k))

                        def turned(c):
                            n = g * C + c
                            for k in range((n + 4) // 4):
                                o = fresh("quick", "pt3", n, k)
                                pe.wait_ge(*at("e3", n, k))
                                for j in range(min(4, n + 1 - 4 * k)):
                                    i = nc.tensor.transpose(o[:, cs(j)], p3b[:, n % 2, k * GT + j * CT:
                                                                             k * GT + (j + 1) * CT], ident[:])
                                i.then_inc(*step("pt3", n, k))

                        def values(c):
                            n = g * C + c
                            for k in range((n + 4) // 4):
                                pe.wait_ge(*at("pt3_s", n, k))
                                for j in range(min(4, n + 1 - 4 * k)):
                                    i = mm(ob[:, c * DK:(c + 1) * DK], pt3[:, k, j], v3[:, 4 * k + j],
                                           start=k == 0 and j == 0, stop=4 * k + j == n)
                                i.then_inc(*step("pv3", n, k))
                            if c == C - 1:
                                reached[("o3", g)] = reached[("pv3", n, k)]
                                growing.discard(("o3", g))

                        def first(k):
                            wg_, wu_ = ((W3["shg"], W3["shu"]) if k == EP3 else
                                        (W3["gate"][:, cs(k)], W3["up"][:, cs(k)]))
                            mm(fresh("quick", "gate3", g, k)[:], wg_, xg).then_inc(*step("gate3", g, k))
                            mm(fresh("quick", "up3", g, k)[:], wu_, xg).then_inc(*step("up3", g, k))

                        def weights(k):
                            o = fresh("slow", "cb3", g, k)
                            pe.wait_ge(*at("ct3_s", g))
                            mm(o[:], sel_p[:, k], ct3[:, g]).then_inc(*step("cbb3", g, k))

                        def second(k):
                            pe.wait_ge(*at("hh3", g, k))
                            w = W3["shd"] if k == EP3 else W3["down"][:, cs(k)]
                            i = mm(ff[:], w, hh3[:, k % 3], start=k == EP3, stop=k == EP3 - 1)
                            i.then_inc(*(step("ff", 3, g) if k == EP3 - 1 else step("dn3", g, k)))

                        units = [EP3] + list(range(EP3))
                        entry = entry3(1)
                        for i in range(len(units) + 2):
                            if i < len(units):
                                first(units[i])
                            if i == 2:
                                ob = fresh("slow", "o3", g)
                                ff = fresh("slow", "ff", 3, g)
                                o = fresh("slow", "ct3", g)
                                ct_out = o[0:48].bitcast(BF16)
                                pe.wait_ge(*at("cb3", g))
                                for c in range(C):
                                    j = nc.tensor.transpose(ct_out[:, cs(c)], cb3[:, g * C + c], identb[:])
                                j.then_inc(*step("ct3", g))
                            if g == 0 and i == 1:
                                norm(3, 1)
                            if g == 0 and i == 3:
                                variance(3, 1)
                            if g == 1 and i in NORM0:
                                norm(0, NORM0[i])
                            if g == 1 and i in VAR0:
                                variance(0, VAR0[i])
                            if i % 2 == 0 and i // 2 < C:
                                score(i // 2)
                            if i % 2 == 1 and i // 2 < C:
                                turned(i // 2)
                            if 2 <= i <= len(units):
                                weights(units[i - 1])
                            if i >= 2 and i % 2 == 0 and i // 2 - 1 < C:
                                values(i // 2 - 1)
                            if i >= 2:
                                second(units[i - 2])
                            if 6 <= i and g == 0:
                                next(entry, None)
                            if i == len(units):
                                o = fresh("quick", "ob3", g)
                                pe.wait_ge(*at("ot3", g))
                                for c in range(C):
                                    j = nc.tensor.transpose(o[0:DK, cs(c)], ot3[:, g % 2, c], ident[:])
                                j.then_inc(*step("ob3", g))
                                o = fresh("slow", "s", 3, g)
                                pe.wait_ge(*at("o3_s", g))
                                mm(o[:], w_out3[:], o3[:, g]).then_inc(*step("s", 3, g))

                    side_by_side(layer0)
                    head(1, 0)
                    now[0] = 1
                    pe.wait_ge(ready["one"], 32)
                    for g in range(G):
                        layer1(g)
                    now[0] = 2
                    for g in range(G):
                        layer2_rec(g)
                        layer2_att(g)
                    now[0] = 3
                    for g in range(G):
                        layer3(g)

                def psum(*job):
                    return bank[known.get(job + ("bank",), 0)]

                @block.scalar
                def _(act):
                    now = [0]

                    def step(*m):
                        return prog["scalar", now[0]].step(*m)

                    def after(*needs):
                        s = prog["scalar", now[0]]
                        if not s.count and now[0]:
                            s = prog["scalar", now[0] - 1]
                        if s.count:
                            act.wait_ge(s.sem, s.count)
                        for m in needs:
                            act.wait_ge(*at(*m))

                    def fn(o, i, f, bias=0.0, scale=1.0, **kw):
                        return nc.scalar.activation(o, i, f, bias=bias, scale=scale, **kw)

                    def square(l, g):
                        after(("xc", l, g), *([("xn", (l - 1) % 4, g)] if l != 1 else []))
                        fn(sq[:, g], psum("xc", l, g)[:], ACT.Square).then_inc(*step("sq", l, g))

                    def logs(l, g):
                        after()
                        fn(called[:], mean[:, 0:1], ACT.Ln).then_inc(*step())
                        after(("var", l, g))
                        fn(rs[:, g], psum("var", l, g)[:], ACT.Ln, bias=EPS).then_inc(*step("var", l, g, "read"))
                        if l == 1:
                            fn(rs2[:], psum("var", l, g)[:], ACT.Ln, bias=EPS * EPS_RMS, scale=1 + EPS_RMS).then_inc(
                                *step())
                            reached[("var", l, g, "read")] = (s_now().sem.name, s_now().count)

                    def powers(l, g):
                        after()
                        fn(rs[:, g], rs[:, g], ACT.Exp, scale=-0.5).then_inc(*step("rs", l, g))
                        if l == 1:
                            fn(rs2[:], rs2[:], ACT.Exp, scale=-0.5).then_inc(*step("rs2", g))

                    def rsqrt(l, g):
                        logs(l, g)
                        powers(l, g)

                    def s_now():
                        return prog["scalar", now[0]]

                    def norm(l, g):
                        square(l, g)
                        rsqrt(l, g)

                    def gate(l, g, src, bias, *needs):
                        after(*needs, *([("x", l + 1, 0) if l < 3 else ("x out", 0)] if g else []))
                        fn(tz[:], src, ACT.Tanh, scale=0.5, bias=bias).then_inc(*step("tz", l, g))

                    def layer0(g):
                        after(("qk0", g))
                        qk = psum("qk0", g)[0:2 * DM]
                        fn(ek[:, g], qk, ACT.Relu, scale=-1.0).then_inc(*step())
                        after()
                        fn(ek[:, g], ek[:, g], ACT.Exp, scale=-1.0).then_inc(*step("ek", g))
                        yield
                        after(("kvg0", g))
                        kv = psum("kvg0", g)[:, 0:C * KVG].rearrange("p (c k) -> p c k", k=KVG)
                        fn(vtok0[:, g * C:(g + 1) * C, 0:DM], kv[:, :, DM:2 * DM], ACT.Copy).then_inc(
                            *step("vtok0", g))
                        fn(et[:, g], kv[:, :, 0:DM], ACT.Relu, scale=-1.0).then_inc(*step())
                        after()
                        fn(et[:, g], et[:, g], ACT.Exp, scale=-1.0).then_inc(*step("et", g))
                        yield
                        after(("gdiff", g))
                        fn(gw[:, g * C:(g + 1) * C, 1], gw[:, g * C:(g + 1) * C, 0], ACT.Exp).then_inc(
                            *step("gexp", g))
                        yield
                        after(("ff", 0, g))
                        fn(tz0[:, g], psum("ff", 0, g)[:], ACT.Tanh, scale=0.5, bias=half0[:]).then_inc(*step("tz", 0, g))
                        yield
                        after(("ct0", g))
                        fn(comb0[:, g], psum("ct0", g)[0:DM], ACT.Copy).then_inc(*step("comb0", g))
                        reached[("ct0", g, "read")] = reached[("comb0", g)]

                    def layer1(g):
                        def relus(e):
                            for j in range(1, HJ, 2):
                                needs = [("h1", g, e, j)]
                                if e >= 2:
                                    needs.append(("eo", g, e - 2))
                                elif g == 1:
                                    needs.append(("eo", 0, E1 - 1 + (1 if e % 2 == 0 else 0)))
                                after(*needs)
                                bias = W1["sb1"][:, j:j + 1] if e == E1 else W1["eb1"][:, e * HJ + j:e * HJ + j + 1]
                                fn(hid[:, e % 2, j], psum("h1", g, e, j)[:], ACT.Relu, bias=bias).then_inc(
                                    *step("hid", g, e, j))
                                reached[("h1", g, e, j, "read")] = reached[("hid", g, e, j)]
                        after(("rt1", g))
                        fn(pr[:, g * C:(g + 1) * C], psum("rt1", g)[:, 0:C * E1].rearrange(
                            "p (c k) -> p c k", k=E1), ACT.Exp, scale=-1.0).then_inc(*step("rt1", g, "read"))
                        for j in range(4):
                            after(("xr", g, j), *([("tx1", g, j - 2)] if j >= 2 else [("tx1", 0, j + 2)] if g else []))
                            fn(tx[:, j % 2], psum("xr", g, j)[:], ACT.Tanh, scale=0.5,
                               bias=half1[:, j:j + 1]).then_inc(*step("tx", g, j))
                        relus(0)
                        after(("dt", g))
                        fn(dab[:], psum("dt", g)[:], ACT.Abs, bias=W1["bdt"]).then_inc(*step("dabs", g))
                        after()
                        fn(dab[:], dab[:], ACT.Exp, scale=-1.0).then_inc(*step())
                        after()
                        fn(dab[:], dab[:], ACT.Ln, bias=1.0).then_inc(*step("dab", g))
                        after(("bx", g))
                        fn(bx[:, gs(g)], psum("bx", g)[0:ST], ACT.Identity, bias=S1["bxp"]).then_inc(
                            *step("bx", g, "read"))
                        fn(xd[:], xn[1][:, gs(g)], ACT.Identity, bias=W1["bout"], scale=W1["dskip"]).then_inc(
                            *step("xd", g))

                        relus(1)
                        coming = (1, 1) if g == 0 else (2, 0)
                        square(*coming)
                        after(("md", g))
                        fn(decay[:, gs(g)], psum("md", g)[0:ST], ACT.Exp, scale=neg_a[:]).then_inc(
                            *step("decay", g))
                        reached[("md", g, "read")] = reached[("decay", g)]
                        relus(2)
                        rsqrt(*coming)
                        after(("ss", g))
                        fn(ssum[:], psum("ss", g)[:], ACT.Copy).then_inc(*step("ssum", g))
                        reached[("ss", g, "read")] = reached[("ssum", g)]
                        after(("cbt", g))
                        fn(cbt1[:, g], psum("cbt", g)[0:E1], ACT.Copy).then_inc(*step("cbt_s", g))
                        reached[("cbt", g, "read")] = reached[("cbt_s", g)]
                        for e in range(3, E1 + 1):
                            relus(e)
                            if g and e == 4:
                                gates(0)
                        gate(1, g, psum("ff", 1, g)[:], half1[:, 4:5], ("ff", 1, g))

                    def gates(g):
                        after(("gt", g), *([("g3", 0)] if g else []))
                        fn(gfm[:, 0], psum("gt", g)[0:32], ACT.Exp, scale=-1.0, bias=neg_bg[:]).then_inc(
                            *step("gt", g, "read"))

                    def layer2_rec(g):
                        if g == 0:
                            after(("x", 2, 1))
                        def query(j):
                            after(("q2", g, j), *([("s2", 0, GB - 1)] if g else []))
                            for half in range(2):
                                fn(qf[:, :, 2 * j + half], psum("q2", g, j)[half * 64:half * 64 + 64].rearrange(
                                    "p (l q) -> p l q", q=L), ACT.Copy, scale=DK ** -0.5).then_inc(*step("qf", g, j))
                            reached[("q2", g, j, "read")] = reached[("qf", g, j)]

                        def decays(e):
                            after(("ga", g, e), *([("rec", 0, NE - 1)] if g else []))
                            fn(abc[:, e, :, 1:L + 1],
                               psum("ga", g, e)[:].rearrange("p (l c) -> p l c", c=L), ACT.Relu, scale=-1.0,
                               bias=1.0).then_inc(*step("abc", g, e))
                            reached[("ga", g, e, "read")] = reached[("abc", g, e)]

                        def summed(e):
                            after(("gkv", g, e * NH + NH - 1))
                            if e == 0 and g == 0:
                                act.wait_ge(*at("chains"))
                            fn(rec[:, 1 + g * GB:1 + (g + 1) * GB, 1:L + 1, e],
                               psum("gkv", g, e)[:].rearrange("p (l c) -> p l c", c=L), ACT.Copy).then_inc(
                                *step("gkv_s", g, e))
                            reached[("gkv", g, e, "read")] = reached[("gkv_s", g, e)]
                        coming = (2, 1) if g == 0 else (3, 0)
                        for i in range(4):
                            decays(i)
                            if i == 3:
                                summed(0)
                            query(i)
                        square(*coming)
                        summed(1)
                        rsqrt(*coming)
                        summed(2)
                        summed(3)

                    def layer2_att(g):
                        after(("r2", g))
                        fn(tr[:], psum("r2", g)[:], ACT.Tanh, scale=0.5).then_inc(*step("r2", g, "read"))
                        after(("k2", g))
                        fn(kr[:], psum("k2", g)[:], ACT.Relu).then_inc(*step("k2", g, "read"))
                        after()
                        fn(kr[:], kr[:], ACT.Square).then_inc(*step("kr", g))
                        for n, blocks in enumerate(VT_JOBS[g]):
                            after(("vt", g, n), *([("pv", 0, GB - 1)] if g else []))
                            k = len(blocks)
                            fn(vt[:, blocks[0]:blocks[0] + k], psum("vt", g, n)[:, 0:k * DK].rearrange(
                                "p (a b) -> p a b", b=DK), ACT.Copy).then_inc(*step("vt_s", g, n))
                            reached[("vt", g, n, "read")] = reached[("vt_s", g, n)]

                        def probs(l):
                            needs = [("mx2", g, l)]
                            if l >= 4:
                                needs.append(("pt", g, l - 4))
                            elif g == 1:
                                needs.append(("pt", 0, GB - 1))
                            after(*needs)
                            for hg in range(2):
                                fn(prob[:, l % 4, hg], psum("s2", g, l)[:, hg * 256:hg * 256 + 256], ACT.Exp,
                                   bias=smx[:, l % 4, hg:hg + 1],
                                   accum_out=smx[:, l % 4, 2 + hg:3 + hg]).then_inc(*step("e2", g, l))
                            reached[("s2", g, l, "read")] = reached[("e2", g, l)]

                        def turned(l):
                            needs = [("pt", g, l)]
                            if l >= 3:
                                needs.append(("pv", g, l - 3))
                            elif g == 1:
                                needs.append(("pv", 0, GB - 1))
                            after(*needs)
                            fn(pt[:, l % 3], psum("pt", g, l)[:], ACT.Copy).then_inc(*step("pt_s", g, l))
                            reached[("pt", g, l, "read")] = reached[("pt_s", g, l)]
                        ahead = entry3(0)
                        for l in range(GB + 3):
                            if l == 6:
                                after(("of", g), *([("x", 3, 0)] if g else []))
                                fn(tz[:], of[:], ACT.Tanh, scale=0.25).then_inc(*step("tz", 2, g))
                            if l == 7 and g == 0:
                                gates(1)
                            if l >= 7 and g == 1:
                                next(ahead, None)
                            if l < GB:
                                probs(l)
                            if l >= 3:
                                turned(l - 3)

                    def entry3(g):
                        after(("qk3", g), *([("gkv", 1, NE * NH - 1)] if g == 0 else []))
                        fn(q3[:, gs(g)], psum("qk3", g)[0:DK], ACT.Copy, scale=DK ** -0.5).then_inc(*step())
                        fn(k3[:, gs(g)], psum("qk3", g)[DK:P], ACT.Copy).then_inc(*step("k3", g))
                        reached[("qk3", g, "read")] = reached[("k3", g)]
                        yield
                        after(("v3", g))
                        fn(v3[:, g * C:(g + 1) * C], psum("v3", g)[:, 0:C * DK].rearrange(
                            "p (c k) -> p c k", k=DK), ACT.Copy).then_inc(*step("v3_s", g))
                        reached[("v3", g, "read")] = reached[("v3_s", g)]
                        after(("gdiff3", g))
                        fn(w3s[:, g * C:(g + 1) * C, 1], w3s[:, g * C:(g + 1) * C, 0], ACT.Exp).then_inc(
                            *step("gexp3", g))

                    def layer3(g):
                        def probs(c):
                            n = g * C + c
                            halves = (n + 4) // 4
                            needs = [("mx3", n)]
                            if n >= 2:
                                needs.append(("pt3", n - 2, (n + 2) // 4 - 1))
                            after(*needs)
                            for k in range(halves):
                                keys = min(GT, (n + 1) * CT - k * GT)
                                fn(p3b[:, n % 2, k * GT:k * GT + keys], psum("s3", n, k)[:, 0:keys], ACT.Exp,
                                   bias=sm3[:, n, 0:1], accum_out=sm3[:, n, 1 + k:2 + k]).then_inc(
                                    *step("e3", n, k))
                                reached[("s3", n, k, "read")] = reached[("e3", n, k)]

                        def turned(c):
                            n = g * C + c
                            halves = (n + 4) // 4
                            for k in range(halves):
                                kc = min(4, n + 1 - 4 * k)
                                after(("pt3", n, k), *([("pv3", n - 1, (n + 3) // 4 - 1)] if n else []))
                                fn(pt3[:, k, 0:kc], psum("pt3", n, k)[:, 0:kc * CT].rearrange(
                                    "p (a b) -> p a b", b=CT), ACT.Copy).then_inc(*step("pt3_s", n, k))
                                reached[("pt3", n, k, "read")] = reached[("pt3_s", n, k)]

                        units = [EP3] + list(range(EP3))
                        if g == 0:
                            after(("pv", 1, GB - 1))
                        ahead = entry3(1)
                        for i in range(len(units) + 2):
                            if i < len(units):
                                k = units[i]
                                needs = [("gate3", g, k)]
                                if i >= 2:
                                    needs.append(("hg3", g, units[i - 2]))
                                elif g:
                                    needs.append(("hg3", 0, EP3 - 1))
                                after(*needs)
                                fn(tg3[:, i % 2], psum("gate3", g, k)[:], ACT.Tanh, scale=0.5).then_inc(
                                    *step("tg3", g, k))
                            if i == 2:
                                after(("ct3", g))
                                fn(ct3[:, g], psum("ct3", g)[0:48].bitcast(BF16)[:, 0:GT], ACT.Copy).then_inc(
                                    *step("ct3_s", g))
                                reached[("ct3", g, "read")] = reached[("ct3_s", g)]
                            if g == 0 and i == 1:
                                square(3, 1)
                            if g == 0 and i == 3:
                                rsqrt(3, 1)
                            if g == 1 and i in NORM0:
                                square(0, NORM0[i])
                            if g == 1 and i == max(VAR0):
                                for stage in (logs, powers):
                                    for k in range(G):
                                        stage(0, k)
                            if i % 2 == 0 and i // 2 < C:
                                probs(i // 2)
                            if i % 2 == 1 and i // 2 < C:
                                turned(i // 2)
                            if i >= 7 and g == 0:
                                next(ahead, None)
                            if i == len(units):
                                after(("ob3", g))
                                fn(o3[:, g], psum("ob3", g)[0:DK], ACT.Copy).then_inc(*step("o3_s", g))
                                reached[("ob3", g, "read")] = reached[("o3_s", g)]
                        gate(3, g, psum("ff", 3, g)[:], 0.0, ("ff", 3, g))

                    side_by_side(layer0)
                    norm(1, 0)
                    now[0] = 1
                    for g in range(G):
                        layer1(g)
                    now[0] = 2
                    for g in range(G):
                        layer2_rec(g)
                        layer2_att(g)
                    now[0] = 3
                    for g in range(G):
                        layer3(g)

                @block.vector
                def _(dve):
                    now = [0]
                    v = nc.vector

                    def step(*m):
                        return prog["vector", now[0]].step(*m)

                    def after(*needs):
                        s = prog["vector", now[0]]
                        if not s.count and now[0]:
                            s = prog["vector", now[0] - 1]
                        if s.count:
                            dve.wait_ge(s.sem, s.count)
                        for m in needs:
                            dve.wait_ge(*at(*m))

                    def norm(l, g):
                        after(("rs", l, g), *([("x", l, g)] if l else []))
                        v.tensor_tensor(xn[l][:, gs(g)], psum("xc", l, g)[:], rs[:, g], ALU.mult).then_inc(
                            *step("xn", l, g))
                        reached[("xc", l, g, "read")] = reached[("xn", l, g)]
                        if l == 1:
                            dve.wait_ge(*at("rs2", g))
                            v.scalar_tensor_tensor(nm[:, gs(g)], psum("xc", l, g)[:], W1["wn"], rs2[:], ALU.mult,
                                                   ALU.mult).then_inc(*step("nm", g))
                            reached[("xc", l, g, "read")] = reached[("nm", g)]

                    def add_up(l, g):
                        after()
                        v.tensor_tensor(x[:, gs(g)], (x if l else x0)[:, gs(g)], hz[:], ALU.add).then_inc(
                            *step(*(("x", l + 1, g) if l < 3 else ("x out", g))))

                    def finish(l, g, gated, scale):
                        after(("s", l, g))
                        v.scalar_tensor_tensor(hz[:], psum("s", l, g)[:], scale, gated, ALU.mult, ALU.mult).then_inc(
                            *step("s", l, g, "read"))
                        add_up(l, g)

                    def merge(l, g, half_s, bias):
                        after(("ff", l, g), ("tz", l, g))
                        v.scalar_tensor_tensor(hz[:], psum("ff", l, g)[:], bias, half_s, ALU.add, ALU.mult).then_inc(
                            *step("ff", l, g, "read"))
                        after()
                        v.scalar_tensor_tensor(hz[:], tz[:], 1.0, hz[:], ALU.add, ALU.mult).then_inc(*step())
                        add_up(l, g)

                    def layer0(g):
                        cc = slice(g * C, (g + 1) * C)
                        qk = psum("qk0", g)
                        kv = psum("kvg0", g)[:, 0:C * KVG].rearrange("p (c k) -> p c k", k=KVG)
                        after(("ek", g))
                        v.scalar_tensor_tensor(sgq[:, gs(g)], qk[0:DM], 0.0, ek[0:DM, g], ALU.max,
                                               ALU.add).then_inc(*step())
                        v.scalar_tensor_tensor(sgk[:, gs(g)], qk[DM:2 * DM], 0.0, ek[DM:2 * DM, g], ALU.max,
                                               ALU.add).then_inc(*step("sgk", g))
                        reached[("qk0", g, "read")] = reached[("sgk", g)]
                        yield
                        after(("kvg0", g), ("et", g))
                        v.tensor_copy(logit[:, cc, 0:NGATE], kv[:, :, 2 * DM:KVG]).then_inc(*step())
                        v.scalar_tensor_tensor(ktok[:, cc], kv[:, :, 0:DM], 0.0, et[:, g], ALU.max,
                                               ALU.add).then_inc(*step("ktok0", g))
                        reached[("kvg0", g, "read")] = reached[("ktok0", g)]
                        after()
                        for c in range(g * C, (g + 1) * C):
                            v.max(top[:, c], logit[:, c]).then_inc(*step())
                        after()
                        v.tensor_tensor(gw[:, cc, 0], top[:, cc, 1], top[:, cc, 0], ALU.subtract).then_inc(
                            *step("gdiff", g))
                        yield
                        after(("gexp", g))
                        v.tensor_scalar(gw[:, cc, 2], gw[:, cc, 1], 1.0, None, ALU.add).then_inc(*step())
                        after()
                        v.reciprocal(gw[:, cc, 3], gw[:, cc, 2]).then_inc(*step())
                        after()
                        v.tensor_tensor(gw[:, cc, 4], gw[:, cc, 1], gw[:, cc, 3], ALU.mult).then_inc(*step())
                        after()
                        v.tensor_tensor(gw[:, cc, 5], gw[:, cc, 4], gw[:, cc, 3], ALU.add).then_inc(*step())
                        after(("y0", g))
                        v.tensor_tensor(ysc[:, g], psum("y0", g)[:].rearrange("p (c k) -> p c k", k=P),
                                        gw[:, cc, 5:6].to_broadcast([P, C, P]), ALU.mult).then_inc(*step("ysc", g))
                        reached[("y0", g, "read")] = reached[("ysc", g)]
                        yield
                        for c in range(C):
                            n = g * C + c
                            after(("kv0", g))
                            v.tensor_tensor(state[:, n + 1, 0], state[:, n, 0], psum("kv0", g)[0:DM, c * 64:c * 64 + DM + 1],
                                            ALU.add).then_inc(*step("state", g))
                        reached[("kv0", g, "read")] = reached[("state", g)]
                        after(("a0", g))
                        v.tensor_tensor(att[:, g], psum("a0", g)[:].rearrange("p (c k) -> p c k", k=P),
                                        causal[:].rearrange("p (a k) -> p a k", a=1).to_broadcast([P, C, P]),
                                        ALU.mult).then_inc(*step("att0", g))
                        reached[("a0", g, "read")] = reached[("att0", g)]
                        yield
                        after(("num0", g))
                        r = psum("num0", g)[:, 0:2 * C * (DM + 1)].rearrange("p (c k d) -> p c k d", c=C, k=2)
                        v.tensor_scalar(den[:, g], r[:, :, :, DM], EPS_MEM, None, ALU.max).then_inc(*step())
                        after()
                        v.reciprocal(den[:, g], den[:, g]).then_inc(*step())
                        after()
                        v.tensor_tensor(den[:, g], den[:, g], flag[:, 0:2].rearrange(
                            "p (a k) -> p a k", a=1).to_broadcast([P, C, 2]), ALU.mult).then_inc(*step())
                        after()
                        v.tensor_tensor(parts[:, g], r[:, :, :, 0:DM], den[:, g].rearrange(
                            "p c (k a) -> p c k a", a=1).to_broadcast([P, C, 2, DM]), ALU.mult).then_inc(
                            *step("num0", g, "read"))
                        after()
                        v.tensor_tensor(ctok[:, g], parts[:, g, :, 0], parts[:, g, :, 1], ALU.add).then_inc(
                            *step("ctok", g))
                        yield
                        after(("tz", 0, g))
                        v.tensor_scalar(gz0[:, g], psum("ff", 0, g)[:], W0["bias"], 0.5, ALU.add, ALU.mult).then_inc(
                            *step("ff", 0, g, "read"))
                        after()
                        v.scalar_tensor_tensor(gz0[:, g], tz0[:, g], 1.0, gz0[:, g], ALU.add, ALU.mult).then_inc(
                            *step())
                        yield
                        finish(0, g, gz0[:, g], 1.0)

                    def top2(g, scores, tops, idx, idf, n):
                        after()
                        for c in range(g * C, (g + 1) * C):
                            v.max(tops[:, c], scores[:, c]).then_inc(*step())
                        after()
                        for c in range(g * C, (g + 1) * C):
                            v.max_index(idx[:, c], tops[:, c], scores[:, c]).then_inc(*step())
                        after()
                        cc = slice(g * C, (g + 1) * C)
                        v.tensor_copy(idf[:, cc], idx[:, cc]).then_inc(*step())

                    def combination(g, idf, w1, w2, oh, cm, n, *name):
                        cc = slice(g * C, (g + 1) * C)
                        io = iota8[:, 0:n].rearrange("p (a k) -> p a k", a=1).to_broadcast([P, C, n])
                        after()
                        for k in range(2):
                            v.tensor_tensor(oh[:, k, cc], io, idf[:, cc, k:k + 1].to_broadcast([P, C, n]),
                                            ALU.is_equal).then_inc(*step())
                        after()
                        for k, w in ((0, w1), (1, w2)):
                            v.tensor_tensor(oh[:, k, cc], oh[:, k, cc], w.to_broadcast([P, C, n]),
                                            ALU.mult).then_inc(*step())
                        after()
                        v.tensor_tensor(cm[:, cc], oh[:, 0, cc], oh[:, 1, cc], ALU.add).then_inc(*step(*name))

                    def route1(g):
                        cc = slice(g * C, (g + 1) * C)
                        after(("rt1", g, "read"))
                        v.tensor_scalar(pr[:, cc], pr[:, cc], 1.0, None, ALU.add).then_inc(*step())
                        yield
                        after()
                        v.reciprocal(pr[:, cc], pr[:, cc]).then_inc(*step())
                        yield
                        top2(g, pr, top1, idx1, idf1, E1)
                        v.scalar_tensor_tensor(wsm1[:, cc, 0], top1[:, cc, 0], 1e-6, top1[:, cc, 1], ALU.add,
                                               ALU.add).then_inc(*step())
                        yield
                        after()
                        v.reciprocal(wsm1[:, cc, 1], wsm1[:, cc, 0]).then_inc(*step())
                        yield
                        after()
                        for k in range(2):
                            v.tensor_tensor(wsm1[:, cc, 2 + k], top1[:, cc, k], wsm1[:, cc, 1], ALU.mult).then_inc(
                                *step())
                        yield
                        combination(g, idf1, wsm1[:, cc, 2:3], wsm1[:, cc, 3:4], oh1, cmb1, E1, "cmb1", g)

                    def layer1(g):
                        def inner(j):
                            after(("tx1", g, j), *([("zp", 0)] if g and j >= 2 else []))
                            dst = xi[:, j, gs(g)] if j < 2 else sr[:, j - 2]
                            v.scalar_tensor_tensor(dst, psum("xr", g, j)[:], W1["bin"][:, j:j + 1], hx[:, j % 2], ALU.add,
                                                   ALU.mult).then_inc(*step("xi", g, j))
                            reached[("xr", g, j, "read")] = reached[("xi", g, j)]

                        def relus(e):
                            for j in range(0, HJ, 2):
                                needs = [("h1", g, e, j)]
                                if e >= 2:
                                    needs.append(("eo", g, e - 2))
                                elif g == 1:
                                    needs.append(("eo", 0, E1 - 1 + (1 if e % 2 == 0 else 0)))
                                after(*needs)
                                bias = W1["sb1"][:, j:j + 1] if e == E1 else W1["eb1"][:, e * HJ + j:e * HJ + j + 1]
                                v.tensor_scalar(hid[:, e % 2, j], psum("h1", g, e, j)[:], bias, 0.0, ALU.add,
                                                ALU.max).then_inc(*step("hid", g, e, j))
                                reached[("h1", g, e, j, "read")] = reached[("hid", g, e, j)]

                        def weigh(e):
                            after(("eo", g, e))
                            for c in range(C):
                                w = cmb1[:, g * C + c, e:e + 1]
                                src = psum("eo", g, e)[:, cs(c)]
                                if e == 0:
                                    i = v.tensor_scalar(acc[:, c], src, w, None, ALU.mult)
                                else:
                                    i = v.scalar_tensor_tensor(acc[:, c], src, w, acc[:, c], ALU.mult, ALU.add)
                                i.then_inc(*step("acc", g, e))
                            reached[("eo", g, e, "read")] = reached[("acc", g, e)]
                        routing = route1(g)
                        for j in range(4):
                            inner(j)
                            if j < 3:
                                next(routing)
                        relus(0)
                        next(routing)
                        after(("dabs", g))
                        v.tensor_scalar(dpos[:], psum("dt", g)[:], W1["bdt"], 0.0, ALU.add, ALU.max).then_inc(
                            *step("dt", g, "read"))
                        relus(1)
                        after(("dab", g))
                        v.tensor_tensor(dab[:], dab[:], dpos[:], ALU.add).then_inc(*step("delta", g))
                        for _ in routing:
                            pass
                        after(("decay", g), ("bx", g, "read"))
                        v.tensor_tensor_scan(states[:, gs(g)], decay[:, gs(g)], bx[:, gs(g)],
                                             states[:, g * GT - 1:g * GT] if g else 0.0, ALU.mult,
                                             ALU.add).then_inc(*step("states", g))
                        weigh(0)
                        relus(2)
                        weigh(1)
                        norm(*((1, 1) if g == 0 else (2, 0)))
                        relus(3)
                        after(("wo1", g), ("ssum", g))
                        v.tensor_tensor(s1out[:], psum("wo1", g)[:], ssum[:], ALU.mult).then_inc(
                            *step("wo1", g, "read"))
                        after(("xd", g))
                        v.tensor_tensor(s1out[:], s1out[:], xd[:], ALU.add).then_inc(*step())
                        after()
                        v.tensor_scalar(s1out[:], s1out[:], 0.5, None, ALU.mult).then_inc(*step("s", 1, g))
                        ahead = gates(0)
                        if g:
                            dve.wait_ge(ready["two"], 32)
                        for e in range(4, E1 + 1):
                            weigh(e - 2)
                            relus(e)
                            if g:
                                next(ahead, None)
                                next(ahead, None)
                                if e == E1:
                                    for _ in ahead:
                                        pass
                        weigh(E1 - 1)
                        merge(1, g, s1out[:], W1["sb2"])

                    def chains():
                        after(("s", 1, 1))
                        init = W2["init"].rearrange("p (l e) -> p l e", e=NE)
                        v.tensor_copy(rec[:, 0, 1:L + 1], init).then_inc(*step())
                        v.tensor_copy(rec[:, 1:NB + 1, 0], init).then_inc(*step())
                        v.memset(rec[:, 0, 0], 0.0).then_inc(*step())
                        v.memset(abc[:, :, :, 0:1], 0.0).then_inc(*step("chains"))

                    def gates(g):
                        after(("gt", g, "read"))
                        gate_, rest = gfm[:, 0], gfm[:, 1]
                        v.tensor_scalar(gate_, gate_, 1.0, None, ALU.add).then_inc(*step())
                        for c in range(C):
                            yield
                            after()
                            v.reciprocal(gfm[:, 0, cs(c)], gfm[:, 0, cs(c)]).then_inc(*step())
                        yield
                        after(*([("gkv", 0, NE * NH - 1)] if g else []))
                        v.tensor_copy(gb[:, 0], gate_).then_inc(*step())
                        v.tensor_copy(g3[0:32], gate_).then_inc(*step())
                        yield
                        after()
                        v.tensor_tensor(rest, gate_, gb[:, 0], ALU.subtract).then_inc(*step())
                        yield
                        after()
                        v.tensor_copy(gb[:, 1], rest).then_inc(*step())
                        v.tensor_copy(g3[32:64], rest).then_inc(*step())
                        yield
                        after()
                        v.tensor_tensor(g3[64:96], rest, gb[:, 1], ALU.subtract).then_inc(*step("g3", g))

                    def shift(g):
                        after(*([("v2", 0)] if g else []))
                        now_, before = xn[2][:, gs(g)], xn_a[:, g * GT:(g + 1) * GT]
                        v.tensor_tensor(dx[:], now_, before, ALU.subtract).then_inc(*step())
                        yield
                        after()
                        v.scalar_tensor_tensor(xr[:], dx[:], W2["mur"], before, ALU.mult, ALU.add).then_inc(
                            *step())
                        yield
                        after()
                        v.scalar_tensor_tensor(xk[:], dx[:], W2["muk"], before, ALU.mult, ALU.add).then_inc(
                            *step("xk", g))

                    def mixed(g):
                        after(("r2", g, "read"), ("v2", g))
                        v.scalar_tensor_tensor(of[:], tr[:], 1.0, psum("v2", g)[:], ALU.add, ALU.mult).then_inc(
                            *step("of", g))
                        reached[("v2", g, "read")] = reached[("of", g)]
                        yield
                        yield
                        after(("tz", 2, g))
                        v.scalar_tensor_tensor(hz[:], tz[:], 1.0, of[:], ALU.add, ALU.mult).then_inc(*step())

                    def layer2_rec(g):
                        side = shift(g)
                        for n in range(NE * NH):
                            if n == 3 and g == 0:
                                chains()
                            if n >= 20:
                                next(side, None)
                            if n == 26:
                                norm(*((2, 1) if g == 0 else (3, 0)))
                            needs = [("gb", g, n)]
                            if n >= 3:
                                needs.append(("gkv", g, n - 3))
                            elif g:
                                needs.append(("gkv", 0, NE * NH - 1))
                            after(*needs)
                            v.tensor_tensor(xs[:, n % 3], psum("gb", g, n)[:], xn[2][:, gs(g)], ALU.mult).then_inc(
                                *step("xs", g, n))
                            reached[("gb", g, n, "read")] = reached[("xs", g, n)]
                            if n % NH == NH - 1 and n // NH >= 1:
                                scan(g, n // NH - 1)
                        scan(g, NE - 1)

                    def scan(g, e):
                        after(("gkv_s", g, e), ("abc", g, e))
                        r = rec[:, 1 + g * GB:1 + (g + 1) * GB].rearrange("p l c e -> p (l c) e")[:, :, e]
                        a = abc[:, e].rearrange("p l c -> p (l c)")
                        v.tensor_tensor_scan(r, a, r, 0.0, ALU.mult, ALU.add).then_inc(*step("rec", g, e))

                    def layer2_att(g):
                        def maxima(l):
                            needs = [("s2", g, l)]
                            after(*needs)
                            v.tensor_reduce(smx[:, l % 4, 0:2], psum("s2", g, l)[:].rearrange(
                                "p (a b) -> p a b", a=2), AX.X, ALU.max, negate=True).then_inc(*step("mx2", g, l))

                        def sums(l):
                            needs = [("e2", g, l)]
                            if l >= 4:
                                needs.append(("prob", g, l - 4))
                            elif g:
                                needs.append(("prob", 0, GB + l - 4))
                            after(*needs)
                            v.reciprocal(smx[:, l % 4, 4:6], smx[:, l % 4, 2:4]).then_inc(*step("rc2", g, l))

                        def out_rows(l2):
                            after(("pv", g, 2 * l2 + 1), *([("s", 2, 0)] if g else []))
                            src = psum("pv", g, l2)[0:DK].rearrange("p (l h a q) -> p h a l q", l=2, h=4, a=2)
                            t = slice(2 * l2 * L, 2 * (l2 + 1) * L)
                            for half in range(2):
                                v.tensor_copy(yt[half * 64:half * 64 + 64, :, t].rearrange("p h (l q) -> p h l q", q=L),
                                              src[:, :, half]).then_inc(*step("yt", g, l2))
                            reached[("pv", g, l2, "read")] = reached[("yt", g, l2)]
                        side, ahead = mixed(g), route3(0) if g else gates(1)
                        if g:
                            dve.wait_ge(ready["three"], 32)
                        for l in range(GB + 7):
                            if l >= 8 if g == 0 else l in (6, 7) or l >= 10:
                                next(ahead, None)
                            if l < GB:
                                maxima(l)
                            if 4 <= l <= 8:
                                next(side, None)
                            if 1 <= l < GB + 1:
                                sums(l - 1)
                            if l >= 7 and l % 2 == 1 and (l - 7) // 2 < GB // 2:
                                out_rows((l - 7) // 2)
                        finish(2, g, hz[:], 0.25)

                    def route3(g):
                        cc = slice(g * C, (g + 1) * C)
                        after(("rt3", g))
                        v.tensor_tensor(lg3[:, cc], psum("rt3", g)[:, 0:C * E3].rearrange("p (c k) -> p c k", k=E3),
                                        W3["rb"].rearrange("p (a k) -> p a k", a=1).to_broadcast([P, C, E3]),
                                        ALU.add).then_inc(*step("rt3", g, "read"))
                        yield
                        top2(g, lg3, top3, idx3, idf3, E3)
                        v.tensor_tensor(w3s[:, cc, 0], top3[:, cc, 1], top3[:, cc, 0], ALU.subtract).then_inc(
                            *step("gdiff3", g))
                        yield
                        after(("gexp3", g))
                        v.tensor_scalar(w3s[:, cc, 0], w3s[:, cc, 1], 1.0, None, ALU.add).then_inc(*step())
                        yield
                        after()
                        v.reciprocal(w3s[:, cc, 2], w3s[:, cc, 0]).then_inc(*step())
                        yield
                        after()
                        v.tensor_tensor(w3s[:, cc, 3], w3s[:, cc, 1], w3s[:, cc, 2], ALU.mult).then_inc(*step())
                        yield
                        combination(g, idf3, w3s[:, cc, 2:3], w3s[:, cc, 3:4], oh3, cm3, E3)
                        yield
                        after()
                        v.tensor_copy(cb3[:, cc, 0:16], cm3[:, cc]).then_inc(*step())
                        yield
                        after()
                        v.tensor_tensor(cr3[:, cc], cm3[:, cc], cb3[:, cc, 0:16], ALU.subtract).then_inc(*step())
                        yield
                        after()
                        v.tensor_copy(cb3[:, cc, 16:32], cr3[:, cc]).then_inc(*step())
                        yield
                        after()
                        v.tensor_tensor(cb3[:, cc, 32:48], cr3[:, cc], cb3[:, cc, 16:32], ALU.subtract).then_inc(
                            *step("cb3", g))

                    routing = route3(1)

                    def centered(l, g):
                        after(("sq", l, g))
                        v.tensor_copy(xn[l][:, gs(g)], psum("xc", l, g)[:]).then_inc(*step("xc", l, g, "read"))

                    def scaled_norm(l, g):
                        after(("rs", l, g))
                        v.tensor_tensor(xn[l][:, gs(g)], xn[l][:, gs(g)], rs[:, g], ALU.mult).then_inc(
                            *step("xn", l, g))

                    def layer3(g):
                        def maxima(c):
                            n = g * C + c
                            halves = (n + 4) // 4
                            for k in range(halves):
                                keys = min(GT, (n + 1) * CT - k * GT)
                                after(("s3", n, k))
                                i = v.tensor_reduce(sm3[:, n, (3 if halves == 2 else 0) + k:][:, 0:1],
                                                    psum("s3", n, k)[:, 0:keys], AX.X, ALU.max, negate=True)
                                i.then_inc(*step(*(("mx3", n) if halves == 1 else ())))
                            if halves == 2:
                                after()
                                v.tensor_tensor(sm3[:, n, 0:1], sm3[:, n, 3:4], sm3[:, n, 4:5], ALU.min).then_inc(
                                    *step("mx3", n))

                        def scaled():
                            cc = slice(g * C, (g + 1) * C)
                            after(("o3", g))
                            if g == 1:
                                v.tensor_tensor(sm3[:, cc, 1], sm3[:, cc, 1], sm3[:, cc, 2], ALU.add).then_inc(*step())
                                after()
                            v.reciprocal(sm3[:, cc, 5], sm3[:, cc, 1]).then_inc(*step())
                            after()
                            v.tensor_tensor(ot3[:, g % 2], psum("o3", g)[:, 0:C * DK].rearrange(
                                "p (c d) -> p c d", d=DK), sm3[:, cc, 5:6].to_broadcast([P, C, DK]),
                                            ALU.mult).then_inc(*step("ot3", g))
                            reached[("o3", g, "read")] = reached[("ot3", g)]

                        def inner(i, k):
                            after(("tg3", g, k))
                            v.scalar_tensor_tensor(h3[:, i % 2], tg3[:, i % 2], 1.0, psum("gate3", g, k)[:], ALU.add,
                                                   ALU.mult).then_inc(*step("hg3", g, k))
                            reached[("gate3", g, k, "read")] = reached[("hg3", g, k)]
                            needs = [("up3", g, k)]
                            if i >= 4:
                                needs.append(("dn3", g, k - 3))
                            elif i == 3:
                                needs.append(("dn3", g, EP3))
                            elif g:
                                needs.append(("ff", 3, 0))
                            after(*needs)
                            v.scalar_tensor_tensor(hh3[:, k % 3], h3[:, i % 2], 0.5, psum("up3", g, k)[:], ALU.mult,
                                                   ALU.mult).then_inc(*step("up3", g, k, "read"))
                            if k == EP3:
                                reached[("hh3", g, k)] = reached[("up3", g, k, "read")]

                        def weigh(k):
                            after(("cbb3", g, k))
                            v.tensor_tensor(hh3[:, k % 3], hh3[:, k % 3], psum("cb3", g, k)[:], ALU.mult).then_inc(
                                *step("hh3", g, k))
                            reached[("cb3", g, k, "read")] = reached[("hh3", g, k)]

                        units = [EP3] + list(range(EP3))
                        for i in range(len(units) + 2):
                            if i < len(units):
                                inner(i, units[i])
                            if i == 1 and g == 0:
                                centered(3, 1)
                            if i == 5 and g == 0:
                                scaled_norm(3, 1)
                            if g == 1 and i in NORM0:
                                centered(0, NORM0[i])
                            if g == 1 and i - 1 in VAR0:
                                scaled_norm(0, VAR0[i - 1])
                            if i % 2 == 0 and i // 2 < C:
                                maxima(i // 2)
                            if i == len(units):
                                scaled()
                            if 2 <= i <= len(units):
                                weigh(units[i - 1])
                            for _ in range(ROUTE3_STEPS[g].get(i, 0)):
                                next(routing, None)
                        after(("s", 3, g))
                        v.tensor_scalar(s3h[:], psum("s", 3, g)[:], W3["bout"], 0.5, ALU.add, ALU.mult).then_inc(
                            *step("s", 3, g, "read"))
                        merge(3, g, s3h[:], 0.0)

                    side_by_side(layer0)
                    norm(1, 0)
                    now[0] = 1
                    for g in range(G):
                        layer1(g)
                    now[0] = 2
                    for g in range(G):
                        layer2_rec(g)
                        layer2_att(g)
                    now[0] = 3
                    for g in range(G):
                        layer3(g)

                @block.gpsimd
                def _(pool):
                    now = [1]

                    def step(*m):
                        return prog["gpsimd", now[0]].step(*m)

                    for g in range(G):
                        for j in range(4):
                            pool.wait_ge(*at("tx", g, j))
                            if j >= 2:
                                pool.wait_ge(*at("xi", g, j - 2))
                            elif g:
                                pool.wait_ge(*at("xi", 0, j + 2))
                            nc.gpsimd.tensor_scalar(hx[:, j % 2], tx[:, j % 2], 1.0, 0.5, ALU.add, ALU.mult).then_inc(
                                *step("tx1", g, j))
                        pool.wait_ge(*at("xi", g, 3))
                        pool.wait_ge(*at("bx", g))
                        nc.gpsimd.tensor_tensor(xi[:, 0, gs(g)], xi[:, 0, gs(g)], sr[:, 0], ALU.mult).then_inc(
                            *step())
                        nc.gpsimd.tensor_tensor(xi[:, 1, gs(g)], xi[:, 1, gs(g)], sr[:, 1], ALU.mult).then_inc(
                            *step("z", g))
                        reached[("zp", g)] = reached[("z", g)]
                    now[0] = 2
                    for g in range(G):
                        for l in range(GB):
                            pool.wait_ge(*at("rc2", g, l))
                            nc.gpsimd.tensor_tensor(prob[:, l % 4], prob[:, l % 4],
                                                    smx[:, l % 4, 4:6].rearrange("p (a b) -> p a b", b=1).to_broadcast(
                                                        [P, 2, 4 * 2 * L]), ALU.mult).then_inc(*step("prob", g, l))

            nc.all_engine_barrier()
            for name, s in sems.items():
                if not name.startswith(("once", "loaded")):
                    nc.sync.sem_clear(s)
            nc.all_engine_barrier()
    return reached


def kernel(**inputs):
    import concourse.bacc as bacc
    from concourse.bass_utils import run_bass_kernel_spmd as run

    a = {k: np.asarray(v) for k, v in inputs.items()}

    def rows(w, p=P):
        return w.reshape(-1, p, w.shape[-1]).transpose(1, 0, 2).reshape(p, -1)

    def col(v, p=P):
        return v.reshape(-1, p).T

    def pack(pieces, spec):
        for piece, (name, n) in zip(pieces, spec):
            assert piece.shape[1] == n, (name, piece.shape, n)
        return np.concatenate(pieces, axis=1)

    mn = a["L0_attn_memory_norm"]
    p0 = pack([np.concatenate([a["L0_attn_w_q"], a["L0_attn_w_k"]]).T,
               np.concatenate([a["L0_attn_w_k"], a["L0_attn_w_v"], a["L0_ffn_W_gate"].T]).T,
               a["L0_ffn_W_shared"].T, a["L0_ffn_W_expert"].T, col(a["L0_ffn_bias"]),
               np.repeat(mn[None], P, 0), np.repeat(a["L0_attn_gate"][None], P, 0)], PACK0)
    s0 = pack([np.concatenate([a["L0_attn_memory"], mn[:, None]], 1), a["L0_attn_w_o"].T], SMALL0)
    p1 = pack([a["L1_attn_W_in"], rows(a["L1_attn_W_dt"]), rows(a["L1_attn_W_xp"]), rows(a["L1_attn_W_out"]),
               a["L1_ffn_router_w"].T, a["L1_ffn_sw1"], rows(a["L1_ffn_sw2"])], PACK1)
    b1 = pack([col(a["L1_attn_b_in"]),
               col(a["L1_attn_b_dt"]), col(a["L1_attn_b_out"]), col(a["L1_attn_D"]), col(a["L1_ffn_norm_weight"]),
               col(a["L1_ffn_sb1"]), col(a["L1_ffn_sb2"]), col(a["L1_ffn_eb1"])], BIAS1)
    s1 = pack([col(a["L1_attn_A_log"], ST), col(a["L1_attn_b_xp"], ST)], SMALL1)
    eb2 = a["L1_ffn_eb2"]
    ew1 = a["L1_ffn_ew1"].transpose(1, 0, 2)
    ew2 = a["L1_ffn_ew2"].reshape(E1, HJ, P, D).transpose(2, 0, 1, 3)
    wkv = np.concatenate([a["L2_attn_w_K"], a["L2_attn_w_V"]], 1).transpose(2, 0, 1).reshape(D, -1)
    init = np.concatenate([a["L2_attn_init_K_rec"], a["L2_attn_init_V_rec"]], 2).transpose(2, 1, 0).reshape(P, -1)
    p2 = pack([a["L2_attn_w_G"].reshape(NH * NE, D).T, wkv, a["L2_attn_w_Q"].reshape(NH * DK, D).T,
               rows(a["L2_attn_w_O"]), init, a["L2_ffn_W_r"].T, a["L2_ffn_W_k"].T, a["L2_ffn_W_v"].T,
               col(a["L2_ffn_mu_r"]), col(a["L2_ffn_mu_k"])], PACK2)
    bg = a["L2_attn_b_G"].reshape(NH * NE, 1)
    qkv = a["L3_attn_w_qkv"]
    p3 = pack([qkv[:2 * DK].T, qkv[2 * DK:].T, col(a["L3_attn_b_out"]), a["L3_ffn_router_w"].T,
               np.repeat(a["L3_ffn_router_bias"][None], P, 0),
               a["L3_ffn_gate_proj"].transpose(1, 0, 2).reshape(D, -1),
               a["L3_ffn_up_proj"].transpose(1, 0, 2).reshape(D, -1),
               rows(a["L3_ffn_down_proj"].reshape(E3 * H3, D)),
               a["L3_ffn_sh_gate"].T, a["L3_ffn_sh_up"].T, a["L3_ffn_sh_down"].T], PACK3)
    wout3 = a["L3_attn_w_out"].T
    x = a["L0_attn_hidden_states"].transpose(0, 2, 1)
    cf, cb = constants()
    given = dict(x=x, cf=cf, cb=cb, p0=p0, s0=s0, p1=p1, b1=b1, s1=s1, eb2=eb2, ew1=ew1, ew2=ew2, p2=p2, bg=bg, p3=p3, wout3=wout3)
    given = {f"in_{k}": np.ascontiguousarray(v) for k, v in given.items()}

    def build(known):
        nc = bacc.Bacc("TRN2", target_bir_lowering=False, num_devices=1)
        args = [nc.dram_tensor(k, v.shape, mybir.dt.from_np(v.dtype), kind="ExternalInput").ap() for k, v in given.items()]
        args.append(nc.dram_tensor("out_x", (B, P, T), F32, kind="ExternalOutput").ap())
        return nc, four_layers(nc, known, *args)

    _, known = build({})
    nc, _ = build(known)
    r = run(nc, [given], core_ids=[0])
    return np.ascontiguousarray(r.results[0]["out_x"].transpose(0, 2, 1))
```
